# Optimizing a Trainium2 kernel written in Bass

```python
import numpy as np
import jax
import jax.numpy as jnp

def _softmax(x, axis=-1):
    return jax.nn.softmax(x, axis=axis)

def _gelu(x):
    return jax.nn.gelu(x, approximate=True)

def _silu(x):
    return jax.nn.silu(x)

def _sigmoid(x):
    return jax.nn.sigmoid(x)

def _layernorm(x, axis=-1, eps=1e-05):
    m = jnp.mean(x, axis=axis, keepdims=True)
    v = jnp.var(x, axis=axis, keepdims=True)
    return (x - m) / jnp.sqrt(v + eps)

def _scatter_add(tgt, idx, src, axis=0):
    return tgt.at[idx].add(src)

def _segment_sum(src, seg, n):
    return jax.ops.segment_sum(src, seg, n)
kernel_name = 'mk_audio_tower_d2_tok_audfeat2048_r4_163c24'

def setup_inputs(seed: int=0):
    np.random.seed(seed)
    _w = jnp.asarray

    def _rec_inputs():
        import jax
        import jax.numpy as jnp
        _rk = jax.random.key(seed)
        x = -0.000392918 + 0.999932 * jax.random.normal(jax.random.fold_in(_rk, 1), (64, 375, 64), jnp.float32)
        return x
    x = _rec_inputs()

    def _L0_tok_setup():
        import jax, jax.numpy as jnp
        import numpy as np
        TIN = 16
        FEAT = 64
        IN_DIM = TIN * FEAT
        HDIM = 512
        EPS = 1e-06

        def layer_norm(x, gamma, beta, eps):
            mu = jnp.mean(x, axis=-1, keepdims=True)
            var = jnp.mean(jnp.square(x - mu), axis=-1, keepdims=True)
            return (x - mu) * jax.lax.rsqrt(var + eps) * gamma + beta
        key = jax.random.key(seed)
        ks = jax.random.split(key, 4)
        x = jax.random.normal(ks[0], (64, 1024, FEAT), dtype=jnp.float32)
        W = jax.random.normal(ks[1], (IN_DIM, HDIM), dtype=jnp.float32) / np.sqrt(IN_DIM)
        b = jnp.zeros((HDIM,), dtype=jnp.float32)
        g1 = jnp.ones((IN_DIM,), dtype=jnp.float32)
        b1 = jnp.zeros((IN_DIM,), dtype=jnp.float32)
        g2 = jnp.ones((HDIM,), dtype=jnp.float32)
        b2 = jnp.zeros((HDIM,), dtype=jnp.float32)
        return {'x': x, 'W': W, 'b': b, 'g1': g1, 'b1': b1, 'g2': g2, 'b2': b2}
    _L0_tok_all = _L0_tok_setup()
    _L0_tok_in = {k: v for k, v in _L0_tok_all.items() if k in ('W', 'b', 'g1', 'b1', 'g2', 'b2')}
    del _L0_tok_all

    def _L0_attn_setup():
        import jax, jax.numpy as jnp
        import numpy as np
        H = 8
        R = 2
        D = 128
        DEG = 2
        GATE_OFFSET = 6.906768

        def _power_attention(q, k, v, log_g):
            B, T, hq, d = q.shape
            scale = 1.0 / d ** 0.5
            k = jnp.repeat(k, R, axis=2)
            v = jnp.repeat(v, R, axis=2)
            logG = jnp.cumsum(log_g, axis=1)
            logG = jnp.repeat(logG, R, axis=2)
            logG = jnp.transpose(logG, (0, 2, 1))
            qk = jnp.einsum('bthd,bshd->bhts', q, k) * scale
            a = qk ** DEG
            gate = logG[:, :, :, None] - logG[:, :, None, :]
            causal = jnp.tril(jnp.ones((T, T), dtype=bool))
            a = jnp.where(causal, a * jnp.exp(gate), 0.0)
            norm = jnp.sum(a, axis=-1) + 1e-06
            y = jnp.einsum('bhts,bshd->bthd', a, v)
            y = y / jnp.transpose(norm, (0, 2, 1))[..., None]
            return y
        key = jax.random.key(seed)
        ks = jax.random.split(key, 7)
        B, T, C = (1, 512, 512)
        q_dim = H * R * D
        kv_dim = H * D
        s = 0.02
        return {'hidden_states': jax.random.normal(ks[0], (B, T, C), dtype=jnp.float32), 'Wq': jax.random.normal(ks[1], (C, q_dim), dtype=jnp.float32) * s, 'Wk': jax.random.normal(ks[2], (C, kv_dim), dtype=jnp.float32) * s, 'Wv': jax.random.normal(ks[3], (C, kv_dim), dtype=jnp.float32) * s, 'Wg': jax.random.normal(ks[4], (C, H), dtype=jnp.float32) * s, 'Wc': jax.random.normal(ks[5], (q_dim, C), dtype=jnp.float32) * s, 'bc': jnp.zeros((C,), dtype=jnp.float32)}
    _L0_attn_all = _L0_attn_setup()
    _L0_attn_in = {k: v for k, v in _L0_attn_all.items() if k in ('Wq', 'Wk', 'Wv', 'Wg', 'Wc', 'bc')}
    del _L0_attn_all

    def _L0_ffn_setup():
        import jax, jax.numpy as jnp
        import numpy as np
        from jax import lax
        TOP_K = 4
        ROUTED_SCALING = 1.0
        RENORMALIZE = True

        def _swiglu_ffn(x, wg, wu, wd):
            return jax.nn.silu(x @ wg.T) * (x @ wu.T) @ wd.T
        key = jax.random.key(seed)
        ks = jax.random.split(key, 9)
        H, I, E = (512, 256, 16)
        s = 0.02
        return {'hidden_states': jax.random.normal(ks[0], (2, 256, H), jnp.float32), 'gate_w': jax.random.normal(ks[1], (E, H), jnp.float32) * s, 'expert_bias': jax.random.normal(ks[2], (E,), jnp.float32) * s, 'w_gate': jax.random.normal(ks[3], (E, I, H), jnp.float32) * s, 'w_up': jax.random.normal(ks[4], (E, I, H), jnp.float32) * s, 'w_down': jax.random.normal(ks[5], (E, H, I), jnp.float32) * s, 'sw_gate': jax.random.normal(ks[6], (I, H), jnp.float32) * s, 'sw_up': jax.random.normal(ks[7], (I, H), jnp.float32) * s, 'sw_down': jax.random.normal(ks[8], (H, I), jnp.float32) * s}
    _L0_ffn_all = _L0_ffn_setup()
    _L0_ffn_in = {k: v for k, v in _L0_ffn_all.items() if k in ('gate_w', 'expert_bias', 'w_gate', 'w_up', 'w_down', 'sw_gate', 'sw_up', 'sw_down')}
    del _L0_ffn_all

    def _L1_attn_setup():
        import jax, jax.numpy as jnp
        import numpy as np
        N_HEAD = 16
        N_KV_HEAD = 4
        N_EMBD = 512

        def rotate_half(x):
            x1, x2 = jnp.split(x, 2, axis=-1)
            return jnp.concatenate([-x2, x1], axis=-1)

        def rope_tables(T, k):
            inv = jnp.power(10000.0, -2.0 * jnp.arange(k // 2, dtype=jnp.float32) / k)
            ang = jnp.arange(T, dtype=jnp.float32)[:, None] * inv[None, :]
            cos = jnp.tile(jnp.cos(ang), (1, 2))
            sin = jnp.tile(jnp.sin(ang), (1, 2))
            return (cos, sin)
        key = jax.random.key(seed)
        ks = jax.random.split(key, 5)
        B, T, D = (4, 256, N_EMBD)
        g, h = (N_KV_HEAD, N_HEAD)
        k = D // h
        s = 0.02
        return {'x': jax.random.normal(ks[0], (B, T, D), dtype=jnp.float32), 'Wq': jax.random.normal(ks[1], (D, D), dtype=jnp.float32) * s, 'Wk': jax.random.normal(ks[2], (D, g * k), dtype=jnp.float32) * s, 'Wv': jax.random.normal(ks[3], (D, g * k), dtype=jnp.float32) * s, 'Wo': jax.random.normal(ks[4], (D, D), dtype=jnp.float32) * s}
    _L1_attn_all = _L1_attn_setup()
    _L1_attn_in = {k: v for k, v in _L1_attn_all.items() if k in ('Wq', 'Wk', 'Wv', 'Wo')}
    del _L1_attn_all

    def _L1_ffn_setup():
        import jax, jax.numpy as jnp
        import numpy as np
        EPS = 1e-05
        RMS_EPS = 1e-06

        def _rmsnorm(x):
            return x * jax.lax.rsqrt(jnp.mean(x * x, axis=-1, keepdims=True) + RMS_EPS)

        def _act_quant(x):
            scale = 127.0 / jnp.clip(jnp.max(jnp.abs(x), axis=-1, keepdims=True), EPS)
            q = jnp.round(jnp.clip(x * scale, -128.0, 127.0)) / scale
            return x + jax.lax.stop_gradient(q - x)

        def _weight_quant(w):
            scale = 1.0 / jnp.clip(jnp.mean(jnp.abs(w)), EPS)
            q = jnp.round(jnp.clip(w * scale, -1.0, 1.0)) / scale
            return w + jax.lax.stop_gradient(q - w)

        def _bitlinear(x, w):
            xq = _act_quant(_rmsnorm(x))
            wq = _weight_quant(w)
            return jnp.einsum('bsi,oi->bso', xq, wq)
        key = jax.random.key(seed)
        k1, k2, k3, k4 = jax.random.split(key, 4)
        B, S, D, F = (2, 512, 512, 2048)
        x = jax.random.normal(k1, (B, S, D), dtype=jnp.float32)
        w_gate = jax.random.normal(k2, (F, D), dtype=jnp.float32) * 0.02
        w_up = jax.random.normal(k3, (F, D), dtype=jnp.float32) * 0.02
        w_down = jax.random.normal(k4, (D, F), dtype=jnp.float32) * 0.02
        return {'x': x, 'w_gate': w_gate, 'w_up': w_up, 'w_down': w_down}
    _L1_ffn_all = _L1_ffn_setup()
    _L1_ffn_in = {k: v for k, v in _L1_ffn_all.items() if k in ('w_gate', 'w_up', 'w_down')}
    del _L1_ffn_all
    return {'x': x, 'L0_tok_W': _L0_tok_in['W'], 'L0_tok_b': _L0_tok_in['b'], 'L0_tok_g1': _L0_tok_in['g1'], 'L0_tok_b1': _L0_tok_in['b1'], 'L0_tok_g2': _L0_tok_in['g2'], 'L0_tok_b2': _L0_tok_in['b2'], 'L0_attn_Wq': _L0_attn_in['Wq'], 'L0_attn_Wk': _L0_attn_in['Wk'], 'L0_attn_Wv': _L0_attn_in['Wv'], 'L0_attn_Wg': _L0_attn_in['Wg'], 'L0_attn_Wc': _L0_attn_in['Wc'], 'L0_attn_bc': _L0_attn_in['bc'], 'L0_ffn_gate_w': _L0_ffn_in['gate_w'], 'L0_ffn_expert_bias': _L0_ffn_in['expert_bias'], 'L0_ffn_w_gate': _L0_ffn_in['w_gate'], 'L0_ffn_w_up': _L0_ffn_in['w_up'], 'L0_ffn_w_down': _L0_ffn_in['w_down'], 'L0_ffn_sw_gate': _L0_ffn_in['sw_gate'], 'L0_ffn_sw_up': _L0_ffn_in['sw_up'], 'L0_ffn_sw_down': _L0_ffn_in['sw_down'], 'L1_attn_Wq': _L1_attn_in['Wq'], 'L1_attn_Wk': _L1_attn_in['Wk'], 'L1_attn_Wv': _L1_attn_in['Wv'], 'L1_attn_Wo': _L1_attn_in['Wo'], 'L1_ffn_w_gate': _L1_ffn_in['w_gate'], 'L1_ffn_w_up': _L1_ffn_in['w_up'], 'L1_ffn_w_down': _L1_ffn_in['w_down']}

def reference(x, L0_tok_W, L0_tok_b, L0_tok_g1, L0_tok_b1, L0_tok_g2, L0_tok_b2, L0_attn_Wq, L0_attn_Wk, L0_attn_Wv, L0_attn_Wg, L0_attn_Wc, L0_attn_bc, L0_ffn_gate_w, L0_ffn_expert_bias, L0_ffn_w_gate, L0_ffn_w_up, L0_ffn_w_down, L0_ffn_sw_gate, L0_ffn_sw_up, L0_ffn_sw_down, L1_attn_Wq, L1_attn_Wk, L1_attn_Wv, L1_attn_Wo, L1_ffn_w_gate, L1_ffn_w_up, L1_ffn_w_down):
    import jax
    import jax.numpy as jnp

    def _L0_tok_ref(x, W, b, g1, b1, g2, b2):
        import jax, jax.numpy as jnp
        import numpy as np
        TIN = 16
        FEAT = 64
        IN_DIM = TIN * FEAT
        HDIM = 512
        EPS = 1e-06

        def layer_norm(x, gamma, beta, eps):
            mu = jnp.mean(x, axis=-1, keepdims=True)
            var = jnp.mean(jnp.square(x - mu), axis=-1, keepdims=True)
            return (x - mu) * jax.lax.rsqrt(var + eps) * gamma + beta
        bsz, T, F = x.shape
        n_patch = T // TIN
        x = x[:, :n_patch * TIN, :].reshape(bsz, n_patch, TIN * F)
        x = layer_norm(x, g1, b1, EPS)
        x = jnp.einsum('bpd,dh->bph', x, W) + b
        return layer_norm(x, g2, b2, EPS)

    def _L0_attn_ref(hidden_states, Wq, Wk, Wv, Wg, Wc, bc):
        import jax, jax.numpy as jnp
        import numpy as np
        H = 8
        R = 2
        D = 128
        DEG = 2
        GATE_OFFSET = 6.906768

        def _power_attention(q, k, v, log_g):
            B, T, hq, d = q.shape
            scale = 1.0 / d ** 0.5
            k = jnp.repeat(k, R, axis=2)
            v = jnp.repeat(v, R, axis=2)
            logG = jnp.cumsum(log_g, axis=1)
            logG = jnp.repeat(logG, R, axis=2)
            logG = jnp.transpose(logG, (0, 2, 1))
            qk = jnp.einsum('bthd,bshd->bhts', q, k) * scale
            a = qk ** DEG
            gate = logG[:, :, :, None] - logG[:, :, None, :]
            causal = jnp.tril(jnp.ones((T, T), dtype=bool))
            a = jnp.where(causal, a * jnp.exp(gate), 0.0)
            norm = jnp.sum(a, axis=-1) + 1e-06
            y = jnp.einsum('bhts,bshd->bthd', a, v)
            y = y / jnp.transpose(norm, (0, 2, 1))[..., None]
            return y
        B, T, C = hidden_states.shape
        q = (hidden_states @ Wq).reshape(B, T, H * R, D)
        k = (hidden_states @ Wk).reshape(B, T, H, D)
        v = (hidden_states @ Wv).reshape(B, T, H, D)
        g = hidden_states @ Wg
        log_g = jax.nn.log_sigmoid(GATE_OFFSET + g.astype(jnp.float32))
        y = _power_attention(q, k, v, log_g)
        y = y.reshape(B, T, H * R * D)
        return y @ Wc + bc

    def _L0_ffn_ref(hidden_states, gate_w, expert_bias, w_gate, w_up, w_down, sw_gate, sw_up, sw_down):
        import jax, jax.numpy as jnp
        import numpy as np
        from jax import lax
        TOP_K = 4
        ROUTED_SCALING = 1.0
        RENORMALIZE = True

        def _swiglu_ffn(x, wg, wu, wd):
            return jax.nn.silu(x @ wg.T) * (x @ wu.T) @ wd.T
        orig_shape = hidden_states.shape
        H = orig_shape[-1]
        x = hidden_states.reshape(-1, H)
        T = x.shape[0]
        logits = x.astype(jnp.float32) @ gate_w.T
        scores = jax.nn.sigmoid(logits)
        _, topk_idx = lax.top_k(scores + expert_bias[None, :], TOP_K)
        topk_w = jnp.take_along_axis(scores, topk_idx, axis=-1)
        if RENORMALIZE:
            topk_w = topk_w / jnp.sum(topk_w, axis=-1, keepdims=True)
        topk_w = topk_w * ROUTED_SCALING
        E = gate_w.shape[0]
        combine = jnp.zeros((T, E), dtype=x.dtype).at[jnp.arange(T)[:, None], topk_idx].set(topk_w.astype(x.dtype))

        def step(acc, ws):
            wg, wu, wd, cw = ws
            return (acc + cw[:, None] * _swiglu_ffn(x, wg, wu, wd), None)
        routed, _ = lax.scan(step, jnp.zeros_like(x), (w_gate, w_up, w_down, combine.T))
        shared = _swiglu_ffn(x, sw_gate, sw_up, sw_down)
        return (routed + shared).reshape(orig_shape)

    def _L1_attn_ref(x, Wq, Wk, Wv, Wo):
        import jax, jax.numpy as jnp
        import numpy as np
        N_HEAD = 16
        N_KV_HEAD = 4
        N_EMBD = 512

        def rotate_half(x):
            x1, x2 = jnp.split(x, 2, axis=-1)
            return jnp.concatenate([-x2, x1], axis=-1)

        def rope_tables(T, k):
            inv = jnp.power(10000.0, -2.0 * jnp.arange(k // 2, dtype=jnp.float32) / k)
            ang = jnp.arange(T, dtype=jnp.float32)[:, None] * inv[None, :]
            cos = jnp.tile(jnp.cos(ang), (1, 2))
            sin = jnp.tile(jnp.sin(ang), (1, 2))
            return (cos, sin)
        B, T, D = x.shape
        h, g = (N_HEAD, N_KV_HEAD)
        k = D // h
        Q = (x @ Wq).reshape(B, T, h, k).transpose(0, 2, 1, 3)
        K = (x @ Wk).reshape(B, T, g, k).transpose(0, 2, 1, 3)
        V = (x @ Wv).reshape(B, T, g, k).transpose(0, 2, 1, 3)
        K = jnp.repeat(K, h // g, axis=1)
        V = jnp.repeat(V, h // g, axis=1)
        cos, sin = rope_tables(T, k)
        cos = cos[None, None]
        sin = sin[None, None]
        Q = Q * cos + rotate_half(Q) * sin
        K = K * cos + rotate_half(K) * sin
        scores = jnp.einsum('bhqk,bhsk->bhqs', Q, K) / jnp.sqrt(jnp.float32(k))
        causal = jnp.tril(jnp.ones((T, T), dtype=bool))
        scores = jnp.where(causal[None, None], scores, -jnp.inf)
        A = jax.nn.softmax(scores, axis=-1)
        Y = jnp.einsum('bhqs,bhsk->bhqk', A, V)
        Y = Y.transpose(0, 2, 1, 3).reshape(B, T, D)
        return Y @ Wo

    def _L1_ffn_ref(x, w_gate, w_up, w_down):
        import jax, jax.numpy as jnp
        import numpy as np
        EPS = 1e-05
        RMS_EPS = 1e-06

        def _rmsnorm(x):
            return x * jax.lax.rsqrt(jnp.mean(x * x, axis=-1, keepdims=True) + RMS_EPS)

        def _act_quant(x):
            scale = 127.0 / jnp.clip(jnp.max(jnp.abs(x), axis=-1, keepdims=True), EPS)
            q = jnp.round(jnp.clip(x * scale, -128.0, 127.0)) / scale
            return x + jax.lax.stop_gradient(q - x)

        def _weight_quant(w):
            scale = 1.0 / jnp.clip(jnp.mean(jnp.abs(w)), EPS)
            q = jnp.round(jnp.clip(w * scale, -1.0, 1.0)) / scale
            return w + jax.lax.stop_gradient(q - w)

        def _bitlinear(x, w):
            xq = _act_quant(_rmsnorm(x))
            wq = _weight_quant(w)
            return jnp.einsum('bsi,oi->bso', xq, wq)
        gate = jax.nn.silu(_bitlinear(x, w_gate))
        up = _bitlinear(x, w_up)
        return _bitlinear(gate * up, w_down)
    h = _L0_tok_ref(x, L0_tok_W, L0_tok_b, L0_tok_g1, L0_tok_b1, L0_tok_g2, L0_tok_b2)
    h = h + _L0_attn_ref(_layernorm(h, axis=-1), L0_attn_Wq, L0_attn_Wk, L0_attn_Wv, L0_attn_Wg, L0_attn_Wc, L0_attn_bc)
    h = h + _L0_ffn_ref(_layernorm(h, axis=-1), L0_ffn_gate_w, L0_ffn_expert_bias, L0_ffn_w_gate, L0_ffn_w_up, L0_ffn_w_down, L0_ffn_sw_gate, L0_ffn_sw_up, L0_ffn_sw_down)
    h = h + _L1_attn_ref(_layernorm(h, axis=-1), L1_attn_Wq, L1_attn_Wk, L1_attn_Wv, L1_attn_Wo)
    h = h + _L1_ffn_ref(_layernorm(h, axis=-1), L1_ffn_w_gate, L1_ffn_w_up, L1_ffn_w_down)
    return h

_drawn_inputs = setup_inputs


def setup_inputs(seed=0):
    import zlib

    import numpy as np

    out = dict(_drawn_inputs(seed))
    spreads = {'L0_tok_b': (0.0, 0.1),
     'L0_tok_g1': (1.0, 0.2),
     'L0_tok_b1': (0.0, 0.1),
     'L0_tok_g2': (1.0, 0.2),
     'L0_tok_b2': (0.0, 0.1),
     'L0_attn_bc': (0.0, 0.1)}
    factors = {'L0_attn_Wg': 8.0,
     'L0_ffn_gate_w': 3.036,
     'L0_ffn_expert_bias': 5.876,
     'L0_ffn_w_gate': 2.759,
     'L0_ffn_w_up': 2.712,
     'L0_ffn_w_down': 2.715,
     'L1_attn_Wq': 3.525,
     'L1_attn_Wk': 3.538}
    for name, (base, spread) in spreads.items():
        noise = np.random.default_rng([zlib.crc32(name.encode()), seed]).standard_normal(out[name].shape)
        drawn = base * np.exp(spread * noise) if base else spread * noise
        out[name] = jnp.asarray(drawn.astype(out[name].dtype))
    for name, factor in factors.items():
        out[name] = (out[name] * factor).astype(out[name].dtype)
    return out
```

```python
from contextlib import ExitStack

import numpy as np

import concourse.bass as bass
from concourse import mybir

P = 128
SEQS, SL = 64, 23
T = SEQS * SL
NT = (T + P - 1) // P
TP = NT * P
AT = 4 * SL
CW = 4 * AT
CH = T // CW
DIN, D = 1024, 512
KI, KD = DIN // P, D // P
HEADS, REP, DH = 8, 2, 128
EXP = 16
FI = 256
TOPK = 4
G4, J4, HD = 4, 4, 32
FF = 2048
NF = FF // 512
UNITS = HEADS + EXP + 1 + 1
WS = 256.0
AS = 16.0
MAGIC = 12582912.0
NEG = -1.0e30

F32 = mybir.dt.float32
F16 = mybir.dt.float16
BF16 = mybir.dt.bfloat16
ALU = mybir.AluOpType
ACT = mybir.ActivationFunctionType
AX = mybir.AxisListType
ds = bass.ds


def free(n):
    return n + 1


def ready(n):
    return n + 3


class Order:

    def __init__(self, eng, sem):
        self.eng, self.sem, self.at, self.n = eng, sem, 0, 0

    def __call__(self, ins):
        self.n += 1
        ins.then_inc(self.sem, 1)
        self.eng.wait_ge(self.sem, self.at + self.n)

    def enter(self, i, per):
        self.base, self.per = self.at + self.n, per
        self.at, self.n = self.base + i * per, 0

    def leave(self, count):
        assert self.n == self.per, ("ordered instructions of the loop body", self.n, self.per)
        self.at, self.n = self.base + count * self.per, 0


class Answers:

    def __init__(self, eng, sem):
        self.eng, self.sem, self.at, self.n = eng, sem, 0, 0

    def next(self):
        self.n += 1
        self.eng.wait_ge(self.sem, self.at + self.n)

    def enter(self, i, per):
        self.base, self.per = self.at + self.n, per
        self.at, self.n = self.base + i * per, 0

    def leave(self, count):
        assert self.n == self.per, ("answers of the loop body", self.n, self.per)
        self.at, self.n = self.base + count * self.per, 0


def build(nc, t, out):
    ctx = ExitStack()
    with ctx:
        def sb(name, shape, dt=F32):
            return ctx.enter_context(nc.sbuf_tensor(name, shape, dt))

        def sem(name):
            return ctx.enter_context(nc.semaphore(name))

        h = sb("h", [P, NT, D])
        nT = [sb(f"nT_{x}", [P, KD, TP], F16) for x in ("hi", "lo")]
        st_a = sb("st_a", [P, 2048])
        st_b = sb("st_b", [P, 1024])
        wa = [sb(f"wa_{x}", [P, 4, 512], F16) for x in ("hi", "lo")]
        wb = [sb(f"wb_{x}", [P, 2, 512], F16) for x in ("hi", "lo")]
        wo = [sb(f"wo_{x}", [P, KD, D], F16) for x in ("hi", "lo")]
        ident = sb("ident", [P, P])
        identb = sb("identb", [P, P], BF16)
        ones = sb("ones", [P, P])
        tri = sb("tri", [P, AT])
        mask = sb("mask", [P, AT])
        maskT = sb("maskT", [P, AT])
        cosT = sb("cosT", [P, CW])
        sinT = sb("sinT", [P, CW])
        bcol = sb("bcol", [P, KD])
        ebias = sb("ebias", [P, EXP])
        gst = sb("gst", [P, KD, HEADS + EXP])
        gw = [sb(f"gw_{x}", [P, KD, HEADS + EXP], F16) for x in ("hi", "lo")]
        bst = sb("bst", [P, 2, 2, 6])
        mv = sb("mv", [P, 2, 2])
        rstd = sb("rstd", [P, 2])
        rt_in = sb("rt_in", [P, 1])
        rt_out = sb("rt_out", [P, 1])
        neg_half = sb("neg_half", [P, 1])
        nbias = sb("nbias", [P, 2])
        nrm = sb("nrm", [P, 2, D])
        cw = sb("cw", [P, EXP + 1, NT])
        cwe = sb("cwe", [P, NT])
        asum = sb("asum", [P, 3])
        apart = sb("apart", [P, 3])
        wsc = sb("wsc", [P, 3])
        wdq = sb("wdq", [P, 3])
        wq_st = sb("wq_st", [P, 3, 1024])
        big = sb("big", [P, KD, TP])
        hact = [big[:, x, :].bitcast(F16).rearrange("p (i t) -> p i t", i=2) for x in range(2)]
        Sc, Pr, PT = [big[:].rearrange("p a b -> p (a b)")[:, x * 16 * AT:(x + 1) * 16 * AT]
                      .rearrange("p (h s) -> p h s", h=16) for x in range(3)]
        flat = big[:].rearrange("p a b -> p (a b)")
        ff = flat[:, 0:2 * FF].rearrange("p (a b) -> p a b", a=2)
        fi = flat[:, 2 * FF:2 * FF + FF // 2].bitcast(BF16)
        fT = flat[:, 2 * FF + FF // 2:3 * FF].bitcast(BF16).rearrange("p (a b) -> p a b", b=P)
        og, sgl = [st_a[:, x * 1024:(x + 1) * 1024].rearrange("p (a b) -> p a b", a=2) for x in range(2)]
        ps = ctx.enter_context(nc.psum_tensor("ps", [P, 8, 512], F32))

        def phase(specs):
            with ExitStack() as c:
                return {n: c.enter_context(nc.sbuf_tensor(n, s, d)) for n, s, d in specs}

        A = phase([("xt", [P, 2, DIN], F32), ("g1", [P, DIN], F32), ("b1", [P, DIN], F32),
                   ("tb", [P, D], F32), ("g2", [P, D], F32), ("b2", [P, D], F32),
                   ("wt_hi", [P, KI, D], F16), ("wt_lo", [P, KI, D], F16), ("z", [P, 2, D], F32),
                   ("xT_hi", [P, 2, KI, P], F16), ("xT_lo", [P, 2, KI, P], F16)])
        B = phase([("lg", [P, HEADS, 16], F32), ("LG", [P, HEADS, 16], F32), ("lt", [P, 3, 128], F32),
                   ("lgh", [P, 16], F32), ("LGh", [P, 16], F32),
                   ("qk", [P, 3, CW], F32), ("v1", [P, 4, DH + 1], F32), ("Dg", [P, 4, AT], F32),
                   ("gt", [P, 4, AT], F32), ("E", [P, 4, AT], F32), ("sq", [P, 2, 2, REP, AT], F32),
                   ("a", [P, 2, 2, REP, AT], F32), ("rn", [P, 2, 2, REP], F32),
                   ("yn", [P, 2, 2, REP, DH], F32), ("yT_hi", [P, REP, CW], F16),
                   ("yT_lo", [P, REP, CW], F16),
                   ("cs", [P, 2, KD, P], F32), ("rt", [P, 8, NT, EXP], F32), ("m8", [P, NT, 8], F32),
                   ("need", [P, NT], F32)])
        with ExitStack() as c:
            DG = {n: c.enter_context(nc.sbuf_tensor(n, s, d)) for n, s, d in [
                ("qw", [P, 3, 8192], BF16)]}
            Dm = phase([("sg", [P, 2, CW], F32), ("ht", [P, 2, CW], F32)])
            Fm = phase([("nTc_hi", [P, KD, CW], F16), ("nTc_lo", [P, KD, CW], F16),
                        ("qraw", [P, 5, CW], F32), ("qsh", [P, CW], F32), ("qcs", [P, CW], F32),
                        ("qr", [P, 5, CW], F32), ("V1", [P, 4, G4, HD + 1], F32),
                        ("mx", [P, 16], F32), ("rd", [P, 16], F32), ("yo", [P, 16, HD], F32)])
            Gm = phase([("ys_hi", [P, 2, KD, P], F16), ("ys_lo", [P, 2, KD, P], F16),
                        ("jk", [P, D], F32), ("ssq", [P, 2], F32), ("am", [P, 2], F32),
                        ("sm", [P, 2, 3], F32), ("qi", [P, 2, D], BF16),
                        ("qT", [P, KD, TP], BF16), ("dq", [P, NT], F32), ("qs", [P, 2, KD, P], BF16),
                        ("dqe", [P, 2, 2], F32), ("dqc", [P, 1], F32), ("dqd", [P, 2], F32),
                        ("ssf", [P, 2, NF], F32)])
            qw = DG["qw"]

        consts_in = sem("consts_in")
        rows_in = sem("rows_in")
        ones_set = sem("ones_set")
        x_in = [sem("x_in0"), sem("x_in1")]
        wa_in, wb_in = sem("wa_in"), sem("wb_in")
        wa_hi, wb_hi = sem("wa_hi"), sem("wb_hi")
        wa_lo, wb_lo = sem("wa_lo"), sem("wb_lo")
        wt_in, wt_hi, wt_lo = sem("wt_in"), sem("wt_hi"), sem("wt_lo")
        passed = sem("passed")
        rt_ask, rt_done = sem("rt_ask"), sem("rt_done")
        dve_o, act_o, pool_o = sem("dve_o"), sem("act_o"), sem("pool_o")
        gw_hi, gw_lo = sem("gw_hi"), sem("gw_lo")
        a_norm, a_tr, a_hi, a_lo = sem("a_norm"), sem("a_tr"), sem("a_hi"), sem("a_lo")
        a_mm, a_h = sem("a_mm"), sem("a_h")
        ln_st, ln_nr, ln_tr = sem("ln_st"), sem("ln_nr"), sem("ln_tr")
        ln_hi, ln_lo = sem("ln_hi"), sem("ln_lo")
        g_mm, g_e1, g_ln, g_lg, g_cum, g_done = [sem(f"gate_{x}") for x in
                                                ("mm", "exp", "ln", "log", "cum", "done")]
        b_pj, b_ev = sem("b_pj"), sem("b_ev")
        b_D, b_g, b_E = sem("b_D"), sem("b_g"), sem("b_E")
        b_sc, b_sq, b_a = sem("b_sc"), sem("b_sq"), sem("b_a")
        b_av, b_yn, b_yt, b_hi, b_lo = [sem(f"b_{x}") for x in ("av", "yn", "yt", "hi", "lo")]
        b_wc, b_acc = sem("b_wc"), sem("b_acc")
        acc_set = sem("acc_set")
        q_in, q_abs, q_sum, q_tot, q_scl = [sem(f"q_{x}") for x in ("in", "abs", "sum", "tot", "scl")]
        c_cp, c_tr, c_h = sem("c_cp"), sem("c_tr"), sem("c_h")
        r_mm, r_exp, r_done = sem("r_mm"), sem("r_exp"), sem("r_done")
        m_gu, m_sg, m_t, m_hi, m_lo = [sem(f"m_{x}") for x in ("gu", "sg", "t", "hi", "lo")]
        m_dn, m_acc, m_pad = sem("m_dn"), sem("m_acc"), sem("m_pad")
        t_in, t_done = [sem("t_in0"), sem("t_in1")], sem("t_done")
        f_x, f_pj, f_ev, f_cos, f_rope, f_sc, f_s = [sem(f"f_{x}") for x in
                                                    ("x", "pj", "ev", "cos", "rope", "sc", "s")]
        f_ex, f_av, f_yn, f_yt, f_hi, f_lo = [sem(f"f_{x}") for x in ("ex", "av", "yn", "yt", "hi", "lo")]
        w_cp, w_mm, w_h, w_sq, w_q, w_tr, w_ev = [sem(f"w_{x}") for x in ("cp", "mm", "h", "sq", "q", "tr", "ev")]
        x_cp, x_gu, x_dq, x_sg, x_t, x_sq, x_q = [sem(f"x_{x}") for x in ("cp", "gu", "dq", "sg", "t", "sq", "q")]
        x_tr, x_ev, x_dn, x_og = [sem(f"x_{x}") for x in ("tr", "ev", "dn", "og")]
        out_st = [sem("out_st0"), sem("out_st1")]

        block = ctx.enter_context(nc.Block())

        @block.sync
        def _(sp):
            def unit_a(n):
                sp.dma_start(st_a[:], t["wa"][n]).then_inc(wa_in, 16)

            def unit_b(n):
                sp.dma_start(st_b[:], t["wb"][n]).then_inc(wb_in, 16)

            for p in range(2):
                sp.sem_inc(out_st[p], 16)
            for k in range(2):
                sp.dma_start(A["xt"][:, k, :], t["x"][k]).then_inc(x_in[k], 16)
            for dst, src in ((A["g1"], "g1"), (A["b1"], "b1"), (A["tb"], "tb"), (A["g2"], "g2"), (A["b2"], "b2")):
                n = t[src].shape[0]
                sp.dma_start(dst[:], t[src].rearrange("(a n) -> a n", a=1).broadcast_to([P, n])).then_inc(rows_in, 16)
            sp.dma_start(st_a[:], t["wt"][0]).then_inc(wt_in, 16)
            for dst, src in ((ident, "ident"), (cosT, "cos"), (sinT, "sin"), (gst, "gst"), (bcol, "bcol")):
                sp.dma_start(dst[:], t[src]).then_inc(consts_in, 16)
            sp.dma_start(tri[0:AT, :], t["tri"]).then_inc(consts_in, 16)
            sp.dma_start(mask[0:AT, :], t["mask"]).then_inc(consts_in, 16)
            sp.dma_start(maskT[0:AT, :], t["maskT"]).then_inc(consts_in, 16)
            sp.dma_start(ebias[:], t["ebias"].rearrange("(a n) -> a n", a=1).broadcast_to([P, EXP])).then_inc(consts_in, 16)
            sp.wait_ge(wt_lo, 1)
            sp.dma_start(st_a[:], t["wt"][1]).then_inc(wt_in, 16)
            unit_b(0)
            with sp.Fori(0, NT // 2 - 1) as i:
                for p in range(2):
                    sp.wait_ge(a_tr, 4 * i + 2 * p + 2)
                    sp.dma_start(A["xt"][:, p, :], t["x"][2 * i + p + 2]).then_inc(x_in[p], 16)
            sp.wait_ge(wt_lo, 2)
            unit_a(0)
            with sp.Fori(0, HEADS) as i:
                sp.wait_ge(q_abs, 3 * i + 1)
                for m in range(3):
                    sp.dma_start(wq_st[:, m, :], t["ffq"][m, i]).then_inc(q_in, 16)
                sp.wait_ge(wa_lo, i + 1)
                unit_a(i + 1)
                sp.wait_ge(wb_lo, i + 1)
                unit_b(i + 1)
            with sp.Fori(HEADS, UNITS - 1) as i:
                sp.wait_ge(wa_lo, i + 1)
                unit_a(i + 1)
                sp.wait_ge(wb_lo, i + 1)
                unit_b(i + 1)
            sp.wait_ge(wa_lo, UNITS)
            sp.dma_start(st_a[:], t["wo"]).then_inc(wa_in, 16)
            with sp.Fori(0, NT // 2 - 1) as i:
                for p in range(2):
                    k = 2 * i + p
                    sp.wait_ge(x_og, ready(k))
                    sp.dma_start(out[ds(k * P, P), :], og[:, p, :]).then_inc(out_st[p], 16)
            for k in (NT - 2, NT - 1):
                rows = T - k * P if k == NT - 1 else P
                sp.wait_ge(x_og, ready(k))
                sp.dma_start(out[k * P:k * P + rows, :], og[0:rows, k % 2, :]).then_inc(out_st[k % 2], 16)
            for p in range(2):
                sp.wait_ge(out_st[p], 16 * (NT // 2) + 16)
        @block.gpsimd
        def _(pool):
            nc.gpsimd.memset(ones[:], 1.0).then_inc(ones_set, 1)
            nc.gpsimd.memset(neg_half[:], -0.5).then_inc(ones_set, 1)
            pool.wait_ge(ones_set, 2)

            def root(n):
                pool.wait_ge(rt_ask, n + 1)
                nc.gpsimd.tensor_tensor(rt_out[:], rt_in[:], neg_half[:], ALU.pow).then_inc(rt_done, 1)

            with pool.Fori(0, 3 * NT) as i:
                root(i)
            pool.wait_ge(b_acc, 4 * CH * HEADS + 2)
            with pool.Fori(0, NT // 2) as i:
                for p in range(2):
                    k = 2 * i + p
                    pool.wait_ge(c_tr, free(k))
                    nc.gpsimd.tensor_copy(B["cs"][:, p], big[:, :, ds(k * P, P)]).then_inc(c_cp, 1)
                    root(3 * NT + k)
            pool.wait_ge(q_scl, 1)
            pool.wait_ge(r_done, 1)
            porder = Order(pool, pool_o)
            for m in range(3):
                with pool.Fori(0, 4) as i:
                    porder.enter(i, 6)
                    for p in range(2):
                        pool.dma_start(wq_st[:, p, :], t["ffq"][m, 2 * i + p]).then_inc(t_in[p], 16)
                    for p in range(2):
                        pool.wait_ge(t_in[p], 16 * (4 * m + i + 1))
                        pool.sem_inc(passed, 1)
                        porder(nc.gpsimd.tensor_scalar(wq_st[:, 2, :], wq_st[:, p, :], wsc[:, m:m + 1], 0.5,
                                                       ALU.mult, ALU.is_gt))
                        pool.sem_inc(passed, 1)
                        porder(nc.gpsimd.tensor_scalar(wq_st[:, p, :], wq_st[:, p, :], wsc[:, m:m + 1], -0.5,
                                                       ALU.mult, ALU.is_lt))
                        pool.sem_inc(passed, 1)
                        porder(nc.gpsimd.tensor_tensor(qw[:, m, ds((2 * i + p) * 1024, 1024)], wq_st[:, 2, :],
                                                       wq_st[:, p, :], ALU.subtract))
                    porder.leave(4)
            pool.sem_inc(t_done, 1)
            with pool.Fori(0, NT) as k:
                root(4 * NT + k)
            with pool.Fori(0, CH) as i:
                pool.wait_ge(f_sc, 4 * i + 1)
                for j in range(5):
                    pool.wait_ge(f_ev, ready(22 * i + j))
                    nc.gpsimd.tensor_tensor(Fm["qr"][:, j, :], Fm["qraw"][:, j, :], cosT[:], ALU.mult).then_inc(f_cos, 1)
            pool.wait_ge(f_lo, 4 * CH + 1)
            with pool.Fori(0, NT // 2) as i:
                for p in range(2):
                    k = 2 * i + p
                    pool.wait_ge(w_mm, free(k))
                    pool.sem_inc(passed, 1)
                    for x in range(2):
                        nc.gpsimd.tensor_copy(Gm[("ys_hi", "ys_lo")[x]][:, p], nT[x][:, :, ds(k * P, P)]).then_inc(w_cp, 1)
                    root(5 * NT + 2 * k)
                    root(5 * NT + 2 * k + 1)
            pool.wait_ge(w_ev, NT + 2)
            with pool.Fori(0, NT // 2) as i:
                for p in range(2):
                    k = 2 * i + p
                    pool.wait_ge(x_gu, 4 * k + 4)
                    pool.sem_inc(passed, 1)
                    nc.gpsimd.tensor_copy(Gm["qs"][:, p], Gm["qT"][:, :, ds(k * P, P)]).then_inc(x_cp, 1)
                    root(7 * NT + k)

        @block.scalar
        def _(act):
            act.sem_inc(ln_nr, 2)
            act.sem_inc(b_ev, 2)
            act.sem_inc(q_abs, 1)
            act.sem_inc(f_ev, 2)
            act.sem_inc(w_ev, 2)
            act.sem_inc(x_ev, 2)
            act.wait_ge(ones_set, 1)

            def split_hi(dst, src, scale, into, sem_out):
                nc.scalar.activation(dst, src, ACT.Copy, scale=scale).then_inc(sem_out, 1)

            def unit_a_hi(n, used=None, count=0):
                act.wait_ge(wa_in, 16 * (n + 1))
                if used is not None:
                    act.wait_ge(used, count)
                nc.scalar.activation(wa[0][:].rearrange("p a b -> p (a b)"), st_a[:], ACT.Copy, scale=WS).then_inc(wa_hi, 1)

            def unit_b_hi(n, used=None, count=0):
                act.wait_ge(wb_in, 16 * (n + 1))
                if used is not None:
                    act.wait_ge(used, count)
                nc.scalar.activation(wb[0][:].rearrange("p a b -> p (a b)"), st_b[:], ACT.Copy, scale=WS).then_inc(wb_hi, 1)

            def ln_norm(n, k, p):
                act.wait_ge(ln_st, n + 1)
                act.wait_ge(ln_tr, free(n))
                nc.scalar.activation(nrm[:, p, :], h[:, ds(k, 1), :].rearrange("p a b -> p (a b)"), ACT.Identity,
                                     bias=nbias[:, p:p + 1], scale=rstd[:, p:p + 1]).then_inc(ln_nr, 1)

            def ln_high(n, k, bank):
                act.wait_ge(ln_tr, ready(n))
                nc.scalar.activation(nT[0][:, :, ds(k * P, P)],
                                     ps[:, bank, :].rearrange("p (a b) -> p a b", a=KD), ACT.Copy).then_inc(ln_hi, 1)

            for j in range(2):
                act.wait_ge(wt_in, 16 * (j + 1))
                nc.scalar.activation(A["wt_hi"][:, 4 * j:4 * j + 4, :].rearrange("p a b -> p (a b)"), st_a[:],
                                     ACT.Copy, scale=WS).then_inc(wt_hi, 1)
            act.wait_ge(consts_in, 144)
            nc.scalar.activation(gw[0][:], gst[:], ACT.Copy, scale=WS).then_inc(gw_hi, 1)

            def tok_high(k, p):
                for j in range(2):
                    act.wait_ge(a_tr, 2 * k + j + 1)
                    nc.scalar.activation(A["xT_hi"][:, p, 4 * j:4 * j + 4, :],
                                         ps[:, j, :].rearrange("p (a b) -> p a b", a=4), ACT.Copy).then_inc(a_hi, 1)

            with act.Fori(0, NT // 2) as i:
                for p in range(2):
                    k = 2 * i + p
                    tok_high(k, p)
                    ln_norm(k, k, p)
                    ln_high(k, k, 4 + p)
            unit_a_hi(0)
            unit_b_hi(0)
            act.wait_ge(g_mm, 2)
            nc.scalar.activation(B["lt"][0:AT, 1, :], B["lt"][0:AT, 1, :], ACT.Exp, scale=-1.0).then_inc(g_e1, 1)
            act.wait_ge(g_e1, 1)
            nc.scalar.activation(B["lt"][0:AT, 1, :], B["lt"][0:AT, 1, :], ACT.Ln, bias=1.0).then_inc(g_ln, 1)
            oh = B["yT_hi"]
            with act.Fori(0, HEADS) as i:
                for c in range(CH):
                    g = CH * i + c
                    for j in range(3):
                        act.wait_ge(b_pj, 5 * g + j + 1)
                        nc.scalar.activation(B["qk"][:, j, :], ps[:, (5 * c + j) % 2, 0:CW], ACT.Copy,
                                             scale=1.0 / WS).then_inc(b_ev, 1)
                    act.wait_ge(b_pj, 5 * g + 4)
                    nc.scalar.activation(B["gt"][0:AT].rearrange("p a b -> p (a b)"),
                                         ps[0:AT, (5 * c + 3) % 2, 0:CW], ACT.Copy).then_inc(b_ev, 1)
                    act.wait_ge(b_pj, 5 * g + 5)
                    nc.scalar.activation(B["v1"][0:AT, :, 0:DH],
                                         ps[0:AT, (5 * c + 4) % 2, :].rearrange("p (a b) -> p a b", a=4), ACT.Copy,
                                         scale=AS / WS).then_inc(b_ev, 1)
                    act.wait_ge(b_g, g + 1)
                    nc.scalar.activation(B["E"][0:AT], B["gt"][0:AT], ACT.Exp).then_inc(b_E, 1)
                    for j in range(2):
                        act.wait_ge(b_sc, 2 * g + j + 1)
                        nc.scalar.activation(B["sq"][0:AT, j].rearrange("p a r t -> p (a r t)"), ps[0:AT, 2 + j, 0:2 * REP * AT],
                                             ACT.Square, scale=float(DH) ** -0.5).then_inc(b_sq, 1)
                    for j in range(2):
                        act.wait_ge(b_yt, 2 * g + j + 1)
                        nc.scalar.activation(oh[:, :, j * 2 * AT:(j + 1) * 2 * AT],
                                             ps[:, 2 + j, 0:CW].rearrange("p (r t) -> p r t", r=REP), ACT.Copy).then_inc(b_hi, 1)
                    if c == 0:
                        for m in range(3):
                            if m == 0:
                                act.wait_ge(q_in, 48 * (i + 1))
                                act.wait_ge(q_sum, i + 1)
                            nc.scalar.activation(wq_st[:, m, :], wq_st[:, m, :], ACT.Abs,
                                                 accum_out=apart[:, m:m + 1]).then_inc(q_abs, 1)
                unit_a_hi(i + 1, b_pj, 5 * CH * (i + 1))
                unit_b_hi(i + 1, b_wc, 4 * CH * (i + 1))
            with act.Fori(0, NT // 2) as i:
                for p in range(2):
                    k = 2 * i + p
                    ln_norm(NT + k, k, p)
                    ln_high(NT + k, k, 4 + p)
            act.wait_ge(r_mm, 1)
            nc.scalar.activation(B["rt"][:, 0], ps[:, 6, 0:NT * EXP].rearrange("p (a b) -> p a b", a=NT), ACT.Exp,
                                 scale=-1.0 / WS).then_inc(r_exp, 1)
            with act.Fori(0, EXP + 1) as e:
                for r0 in range(8):
                    r = 8 * e + r0
                    c, ib = r0 // 2, r0 % 2
                    act.wait_ge(m_gu, r + 1)
                    act.wait_ge(m_t, free(r))
                    nc.scalar.activation(Dm["sg"][:, r0 % 2, :], ps[:, 2 * (r0 % 2), 0:CW], ACT.Silu,
                                         scale=1.0 / WS).then_inc(m_sg, 1)
                    if r0 == 0:
                        act.wait_ge(m_acc, NT * e + 4)
                    act.wait_ge(m_t, ready(r))
                    nc.scalar.activation(hact[0][:, ib, c * CW:(c + 1) * CW], Dm["ht"][:, r0 % 2, :],
                                         ACT.Copy).then_inc(m_hi, 1)
                unit_a_hi(HEADS + e + 1, m_gu, 8 * (e + 1))
                unit_b_hi(HEADS + e + 1, m_dn, NT * (e + 1))
            act.wait_ge(wa_in, 16 * (UNITS + 1))
            nc.scalar.activation(wo[0][:].rearrange("p a b -> p (a b)"), st_a[:], ACT.Copy, scale=WS).then_inc(wa_hi, 1)
            with act.Fori(0, NT // 2) as i:
                for p in range(2):
                    k = 2 * i + p
                    ln_norm(2 * NT + k, k, p)
                    ln_high(2 * NT + k, k, 4 + p)
            with act.Fori(0, CH) as i:
                for j in range(5):
                    act.wait_ge(f_pj, 22 * i + j + 1)
                    nc.scalar.activation(Fm["qraw"][:, j, :], ps[:, j % 2, 0:CW], ACT.Copy, scale=1.0 / WS).then_inc(f_ev, 1)
                act.wait_ge(f_pj, 22 * i + 6)
                nc.scalar.activation(Fm["V1"][0:AT, :, :, 0:HD],
                                     ps[0:AT, 1, :].rearrange("p (a g d) -> p a g d", a=4, g=G4), ACT.Copy,
                                     scale=AS / WS).then_inc(f_ev, 1)
                for a in range(4):
                    n = 4 * i + a
                    act.wait_ge(f_s, ready(n) - 1)
                    nc.scalar.activation(Pr[0:AT], Sc[0:AT], ACT.Exp, scale=float(HD) ** -0.5).then_inc(f_ex, 1)
                    for g in range(G4):
                        m = 22 * i + 6 + 4 * a + g
                        act.wait_ge(f_pj, m + 1)
                        nc.scalar.activation(PT[0:AT, 4 * g:4 * g + 4, :].rearrange("p a b -> p (a b)"),
                                             ps[0:AT, g % 2, 0:CW], ACT.Copy).then_inc(f_ev, 1)
                    act.wait_ge(f_yt, n + 1)
                    nc.scalar.activation(nT[0][:, :, ds(i * CW + a * AT, AT)],
                                         ps[:, 6, 0:CW].rearrange("p (b t) -> p b t", b=KD), ACT.Copy).then_inc(f_hi, 1)
            with act.Fori(0, NT // 2) as i:
                for p in range(2):
                    k = 2 * i + p
                    act.wait_ge(ln_st, 3 * NT + k + 1)
                    act.wait_ge(w_q, free(k))
                    nc.scalar.activation(nrm[:, p, :], h[:, ds(k, 1), :].rearrange("p a b -> p (a b)"), ACT.Identity,
                                         bias=nbias[:, p:p + 1], scale=rstd[:, p:p + 1]).then_inc(ln_nr, 1)
                    act.wait_ge(ln_nr, ready(3 * NT + k))
                    nc.scalar.activation(Gm["jk"][:], nrm[:, p, :], ACT.Square, accum_out=Gm["ssq"][:, p:p + 1]).then_inc(w_sq, 1)
                    act.wait_ge(w_tr, k + 1)
                    nc.scalar.activation(Gm["qT"][:, :, ds(k * P, P)],
                                         ps[:, 2 + p, 0:256].bitcast(BF16).rearrange("p (a b) -> p a b", a=KD),
                                         ACT.Copy).then_inc(w_ev, 1)

            def gated(k, p, first=False):
                def silu(f):
                    act.wait_ge(x_gu, 4 * k + f + 9)
                    act.wait_ge(x_t, free(4 * k + f))
                    if f == 0:
                        act.wait_ge(x_dq, k + 1)
                    nc.scalar.activation(sgl[:, f % 2, :], ps[:, 2 * (f % 2), :], ACT.Silu,
                                         scale=Gm["dqe"][:, p, 0:1]).then_inc(x_sg, 1)

                def square(f):
                    act.wait_ge(x_t, ready(4 * k + f))
                    if f or not first:
                        act.wait_ge(x_sq, 4 * k + f)
                    nc.scalar.activation(Gm["jk"][:], ff[:, p, f * 512:(f + 1) * 512], ACT.Square,
                                         accum_out=Gm["ssf"][:, p, f:f + 1]).then_inc(x_sq, 1)

                silu(0)
                for f in range(1, NF):
                    silu(f)
                    square(f - 1)
                square(NF - 1)

            def f_turned(k):
                for j in range(2):
                    act.wait_ge(x_tr, 2 * k + j + 3)
                    act.wait_ge(x_dn, k + 1)
                    nc.scalar.activation(fT[:, 8 * j:8 * j + 8, :].rearrange("p a b -> p (a b)"),
                                         ps[:, 4 + j, :].bitcast(BF16), ACT.Copy).then_inc(x_ev, 1)

            gated(0, 0, True)
            with act.Fori(0, NT // 2 - 1) as i:
                for p in range(2):
                    k = 2 * i + p
                    gated(k + 1, 1 - p)
                    f_turned(k)
            gated(NT - 1, 1)
            f_turned(NT - 2)
            f_turned(NT - 1)

        @block.tensor
        def _(pe):
            pe.sem_inc(ln_tr, 2)
            pe.sem_inc(c_tr, 2)
            pe.sem_inc(f_sc, 1)
            pe.sem_inc(w_mm, 2)
            pe.sem_inc(x_gu, 8)
            pe.sem_inc(x_tr, 2)
            pe.sem_inc(x_dn, 1)
            pe.wait_ge(consts_in, 144)
            pe.wait_ge(ones_set, 1)

            def ln_turn(n, p, bank):
                pe.wait_ge(ln_nr, ready(n))
                pe.wait_ge(ln_lo, free(n))
                for b in range(KD):
                    ins = nc.tensor.transpose(ps[:, bank, b * P:(b + 1) * P], nrm[:, p, b * P:(b + 1) * P], ident[:])
                ins.then_inc(ln_tr, 1)

            def split3(dst, lhs, rhs, start, stop):
                nc.tensor.matmul(dst, lhs[0], rhs[0], start=start, stop=False)
                nc.tensor.matmul(dst, lhs[0], rhs[1], start=False, stop=False)
                return nc.tensor.matmul(dst, lhs[1], rhs[0], start=False, stop=stop)

            def tok_turn(k, p):
                pe.wait_ge(a_norm, k + 1)
                for j in range(2):
                    pe.wait_ge(a_lo, 2 * k + j + 1)
                    for b in range(4):
                        ins = nc.tensor.transpose(ps[:, j, b * P:(b + 1) * P],
                                                  A["xt"][:, p, (4 * j + b) * P:(4 * j + b + 1) * P], ident[:])
                    ins.then_inc(a_tr, 1)

            def tok_mm(k, p):
                pe.wait_ge(a_lo, 2 * k + 4)
                pe.wait_ge(a_h, k + 1)
                for b in range(KI):
                    ins = split3(ps[:, 2 + p, :], [A["xT_hi"][:, p, b, :], A["xT_lo"][:, p, b, :]],
                                 [A["wt_hi"][:, b, :], A["wt_lo"][:, b, :]], b == 0, b == KI - 1)
                ins.then_inc(a_mm, 1)

            pe.wait_ge(wt_lo, 2)
            with pe.Fori(0, NT // 2) as i:
                for p in range(2):
                    k = 2 * i + p
                    tok_turn(k, p)
                    tok_mm(k, p)
                    ln_turn(k, p, 4 + p)
            pe.wait_ge(ln_lo, ready(NT - 1))
            pe.wait_ge(gw_lo, 1)
            for a in range(T // AT):
                for b in range(KD):
                    x = [nT[0][:, b, a * AT:(a + 1) * AT], nT[1][:, b, a * AT:(a + 1) * AT]]
                    ins = split3(ps[0:AT, 0, a * HEADS:(a + 1) * HEADS], x,
                                 [gw[0][:, b, 0:HEADS], gw[1][:, b, 0:HEADS]], b == 0, b == KD - 1)
            ins.then_inc(g_mm, 1)
            pe.wait_ge(g_lg, 1)
            nc.tensor.matmul(ps[0:AT, 1, 0:16 * HEADS], tri[0:AT, :], B["lg"][0:AT].rearrange("p a b -> p (a b)"),
                             start=True, stop=True).then_inc(g_cum, 1)

            def out_proj(g, c):
                pe.wait_ge(b_lo, 2 * g + 4)
                for blk in range(4):
                    pe.wait_ge(b_acc, free(4 * g + blk))
                    for r in range(REP):
                        ins = split3(ps[:, 6 + blk % 2, 0:CW],
                                     [wb[x][:, r, blk * P:(blk + 1) * P] for x in range(2)],
                                     [B["yT_hi"][:, r, :], B["yT_lo"][:, r, :]], r == 0, r == REP - 1)
                    ins.then_inc(b_wc, 1)

            pe.wait_ge(g_done, 1)
            with pe.Fori(0, HEADS) as i:
                pe.wait_ge(wa_lo, i + 1)
                for c in range(CH):
                    g = CH * i + c
                    cols = slice(c * CW, (c + 1) * CW)
                    for j in range(3):
                        pe.wait_ge(b_ev, free(5 * g + j))
                        for b in range(KD):
                            ins = split3(ps[:, (5 * c + j) % 2, 0:CW], [wa[x][:, b, j * P:(j + 1) * P] for x in range(2)],
                                         [nT[x][:, b, cols] for x in range(2)], b == 0, b == KD - 1)
                        ins.then_inc(b_pj, 1)
                    pe.wait_ge(b_ev, free(5 * g + 3))
                    pe.wait_ge(b_D, g + 1)
                    nc.tensor.matmul(ps[0:AT, (5 * c + 3) % 2, 0:CW], ones[0:AT, 0:AT], B["Dg"][0:AT].rearrange("p a b -> p (a b)"),
                                     start=True, stop=True).then_inc(b_pj, 1)
                    pe.wait_ge(b_ev, free(5 * g + 4))
                    for a in range(4):
                        tok = slice(c * CW + a * AT, c * CW + (a + 1) * AT)
                        for b in range(KD):
                            ins = split3(ps[0:AT, (5 * c + 4) % 2, a * P:(a + 1) * P], [nT[x][:, b, tok] for x in range(2)],
                                         [wa[x][:, b, 3 * P:4 * P] for x in range(2)], b == 0, b == KD - 1)
                    ins.then_inc(b_pj, 1)
                    pe.wait_ge(b_ev, ready(5 * g + 2))
                    for j in range(2):
                        pe.wait_ge(b_lo, free(2 * g + j))
                        for a in range(2):
                            tok = slice((2 * j + a) * AT, (2 * j + a + 1) * AT)
                            ins = nc.tensor.matmul(ps[0:AT, 2 + j, a * REP * AT:(a + 1) * REP * AT],
                                                   B["qk"][:, 2, tok], B["qk"][:, 0:2, tok], start=True, stop=True)
                        ins.then_inc(b_sc, 1)
                    if c:
                        if c == 1:
                            pe.wait_ge(wb_lo, i + 1)
                        out_proj(g - 1, c - 1)
                    pe.wait_ge(b_ev, ready(5 * g + 4))
                    for j in range(2):
                        pe.wait_ge(b_a, 2 * g + j + 1)
                        if j == 1:
                            pe.wait_ge(b_acc, 4 * g + 2)
                        for a in range(2):
                            for r in range(REP):
                                ins = nc.tensor.matmul(ps[0:AT, 4 + 2 * j + a, r * (DH + 1):(r + 1) * (DH + 1)],
                                                       B["a"][0:AT, j, a, r, :], B["v1"][0:AT, 2 * j + a, :],
                                                       start=True, stop=True)
                        ins.then_inc(b_av, 1)
                    for j in range(2):
                        pe.wait_ge(b_yn, 2 * g + j + 1)
                        for r in range(REP):
                            for a in range(2):
                                ins = nc.tensor.transpose(ps[:, 2 + j, (2 * r + a) * AT:(2 * r + a + 1) * AT],
                                                          B["yn"][0:AT, j, a, r, :], ident[0:AT, 0:AT])
                        ins.then_inc(b_yt, 1)
                out_proj(g, c)
            pe.wait_ge(q_sum, HEADS + 1)
            nc.tensor.matmul(ps[:, 0, 0:3], ones[:], asum[:], start=True, stop=True).then_inc(q_tot, 1)

            def route(k):
                pe.wait_ge(ln_lo, ready(NT + k))
                for b in range(KD):
                    ins = split3(ps[:, 6, ds(k * EXP, EXP)], [nT[x][:, b, ds(k * P, P)] for x in range(2)],
                                 [gw[x][:, b, HEADS:] for x in range(2)], b == 0, b == KD - 1)
                return ins

            with pe.Fori(0, NT // 2) as i:
                for p in range(2):
                    k = 2 * i + p
                    pe.wait_ge(c_cp, k + 1)
                    for b in range(KD):
                        ins = nc.tensor.transpose(ps[:, 2 + p, b * P:(b + 1) * P], B["cs"][:, p, b, :], ident[:])
                    ins.then_inc(c_tr, 1)
                    ln_turn(NT + k, p, 4 + p)
            for k in range(NT):
                ins = route(k)
            ins.then_inc(r_mm, 1)
            with pe.Fori(0, EXP + 1) as e:
                pe.wait_ge(wa_lo, HEADS + e + 1)
                for r0 in range(8):
                    r, c, ib = 8 * e + r0, r0 // 2, r0 % 2
                    pe.wait_ge(m_t, free(r))
                    for q in range(2):
                        for b in range(KD):
                            ins = split3(ps[:, 2 * (r0 % 2) + q, 0:CW],
                                         [wa[x][:, b, q * FI + ib * P:q * FI + (ib + 1) * P] for x in range(2)],
                                         [nT[x][:, b, c * CW:(c + 1) * CW] for x in range(2)], b == 0, b == KD - 1)
                    ins.then_inc(m_gu, 1)
                pe.wait_ge(wb_lo, HEADS + e + 1)
                pe.wait_ge(m_pad, 2)
                for k in range(NT):
                    last = min((k * P + P - 1) // CW, CH - 1)
                    pe.wait_ge(m_lo, 8 * e + 2 * last + 2)
                    pe.wait_ge(m_acc, NT * e + k + 1)
                    for ib in range(2):
                        ins = split3(ps[:, 4 + k % 4, :], [hact[x][:, ib, k * P:(k + 1) * P] for x in range(2)],
                                     [wb[x][:, ib, :] for x in range(2)], ib == 0, ib == 1)
                    ins.then_inc(m_dn, 1)
            with pe.Fori(0, NT // 2) as i:
                for p in range(2):
                    ln_turn(2 * NT + 2 * i + p, p, 4 + p)
            wkv = [wb[x][:].rearrange("p a b -> p (a b)").rearrange("p (a b) -> p a b", a=KD) for x in range(2)]
            nc_ = [Fm["nTc_hi"], Fm["nTc_lo"]]
            pe.wait_ge(wa_lo, UNITS)
            pe.wait_ge(wb_lo, UNITS)
            with pe.Fori(0, CH) as i:
                pe.wait_ge(f_x, i + 1)
                for j in range(5):
                    pe.wait_ge(f_ev, free(22 * i + j))
                    for b in range(KD):
                        w = [wa[x][:, b, j * P:(j + 1) * P] if j < 4 else wkv[x][:, b, 0:P] for x in range(2)]
                        ins = split3(ps[:, j % 2, 0:CW], w, [nc_[x][:, b, :] for x in range(2)], b == 0, b == KD - 1)
                    ins.then_inc(f_pj, 1)
                pe.wait_ge(f_ev, free(22 * i + 5))
                for a in range(4):
                    for b in range(KD):
                        ins = split3(ps[0:AT, 1, a * P:(a + 1) * P], [nc_[x][:, b, a * AT:(a + 1) * AT] for x in range(2)],
                                     [wkv[x][:, b, P:2 * P] for x in range(2)], b == 0, b == KD - 1)
                ins.then_inc(f_pj, 1)
                pe.wait_ge(f_rope, i + 1)

                def scores(a):
                    pe.wait_ge(f_s, 4 * i + a + 1)
                    tok = slice(a * AT, (a + 1) * AT)
                    for j in range(J4):
                        for g in range(G4):
                            r = slice(HD * g, HD * (g + 1))
                            ins = nc.tensor.matmul(ps[0:AT, 2 + g, j * AT:(j + 1) * AT], Fm["qr"][r, j, tok],
                                                   Fm["qr"][r, 4, tok], start=True, stop=True)
                    ins.then_inc(f_sc, 1)

                scores(0)
                for a in range(4):
                    n = 4 * i + a
                    if a < 3:
                        scores(a + 1)
                    pe.wait_ge(f_ex, n + 1)
                    for g in range(G4):
                        m = 22 * i + 6 + 4 * a + g
                        pe.wait_ge(f_ev, free(m))
                        for j in range(J4):
                            ins = nc.tensor.transpose(ps[0:AT, g % 2, j * AT:(j + 1) * AT], Pr[0:AT, 4 * g + j, :],
                                                      ident[0:AT, 0:AT])
                        ins.then_inc(f_pj, 1)
                    pe.wait_ge(f_lo, n + 1)
                    for g in range(G4):
                        pe.wait_ge(f_ev, ready(22 * i + 6 + 4 * a + g))
                        for j in range(J4):
                            c0 = ((g % 2) * J4 + j) * (HD + 1)
                            ins = nc.tensor.matmul(ps[0:AT, 6 + g // 2, c0:c0 + HD + 1], PT[0:AT, 4 * g + j, :],
                                                   Fm["V1"][0:AT, a, g, :], start=True, stop=True)
                    ins.then_inc(f_av, 1)
                    pe.wait_ge(f_yn, n + 1)
                    for b in range(KD):
                        ins = nc.tensor.transpose(ps[:, 6, b * AT:(b + 1) * AT],
                                                  Fm["yo"][0:AT].rearrange("p h d -> p (h d)")[:, b * P:(b + 1) * P],
                                                  ident[0:AT, 0:AT])
                    ins.then_inc(f_yt, 1)
            pe.wait_ge(wa_lo, UNITS + 1)
            with pe.Fori(0, NT // 2) as i:
                for p in range(2):
                    k = 2 * i + p
                    pe.wait_ge(w_cp, 2 * k + 2)
                    pe.wait_ge(w_h, free(k))
                    for b in range(KD):
                        ins = split3(ps[:, p, :], [Gm["ys_hi"][:, p, b, :], Gm["ys_lo"][:, p, b, :]],
                                     [wo[x][:, b, :] for x in range(2)], b == 0, b == KD - 1)
                    ins.then_inc(w_mm, 1)
                    pe.wait_ge(w_q, ready(k))
                    pe.wait_ge(w_ev, free(k))
                    for b in range(KD):
                        ins = nc.tensor.transpose(ps[:, 2 + p, 64 * b:64 * b + 64].bitcast(BF16), Gm["qi"][:, p, b * P:(b + 1) * P],
                                                  identb[:])
                    ins.then_inc(w_tr, 1)

            def gate_up(k, p):
                pe.wait_ge(x_cp, k + 1)
                for f in range(NF):
                    pe.wait_ge(x_t, free(4 * k + f))
                    for q in range(2):
                        for b in range(KD):
                            ins = nc.tensor.matmul(ps[:, 2 * (f % 2) + q, :], Gm["qs"][:, p, b, :],
                                                   qw[:, q, b * FF + f * 512:b * FF + (f + 1) * 512],
                                                   start=b == 0, stop=b == KD - 1)
                    ins.then_inc(x_gu, 1)

            def down(k, p):
                pe.wait_ge(x_q, k + 1)
                for j in range(2):
                    pe.wait_ge(x_ev, 2 * k + j + 1)
                    for b in range(8):
                        ins = nc.tensor.transpose(ps[:, 4 + j, 64 * b:64 * b + 64].bitcast(BF16),
                                                  fi[:, (8 * j + b) * P:(8 * j + b + 1) * P], identb[:])
                    ins.then_inc(x_tr, 1)
                pe.wait_ge(x_og, free(k))
                pe.wait_ge(x_ev, 2 * k + 4)
                for b in range(FF // P):
                    ins = nc.tensor.matmul(ps[:, 6 + p, :], fT[:, b, :], qw[:, 2, b * D:(b + 1) * D],
                                           start=b == 0, stop=b == FF // P - 1)
                ins.then_inc(x_dn, 1)

            pe.wait_ge(t_done, 1)
            gate_up(0, 0)
            with pe.Fori(0, NT // 2 - 1) as i:
                for p in range(2):
                    k = 2 * i + p
                    gate_up(k + 1, 1 - p)
                    down(k, p)
            gate_up(NT - 1, 1)
            down(NT - 2, 0)
            down(NT - 1, 1)

        @block.vector
        def _(dve):
            V = nc.vector
            dve.sem_inc(ln_lo, 2)
            dve.sem_inc(a_lo, 2)
            dve.sem_inc(a_h, 2)
            dve.sem_inc(b_lo, 2)
            dve.sem_inc(q_sum, 1)
            dve.sem_inc(f_s, 1)
            dve.sem_inc(f_lo, 1)
            dve.sem_inc(w_h, 2)
            dve.sem_inc(w_q, 2)
            dve.sem_inc(x_t, 2)
            dve.sem_inc(x_og, 2)
            dve.sem_inc(b_acc, 2)
            dve.sem_inc(m_acc, 4)
            dve.wait_ge(ones_set, 2)
            order = Order(dve, dve_o)
            roots = Answers(dve, rt_done)

            def split_lo(dst, src, hi, sem_out):
                V.scalar_tensor_tensor(dst, src, WS, hi, ALU.mult, ALU.subtract).then_inc(sem_out, 1)

            def unit_a_lo(n):
                dve.wait_ge(wa_hi, n + 1)
                split_lo(wa[1][:].rearrange("p a b -> p (a b)"), st_a[:], wa[0][:].rearrange("p a b -> p (a b)"), wa_lo)

            def unit_b_lo(n):
                dve.wait_ge(wb_hi, n + 1)
                split_lo(wb[1][:].rearrange("p a b -> p (a b)"), st_b[:], wb[0][:].rearrange("p a b -> p (a b)"), wb_lo)

            def root(src, scale, eps):
                V.tensor_scalar(rt_in[:], src, scale, eps, ALU.mult, ALU.add).then_inc(rt_ask, 1)
                roots.next()

            def stats(rows, p, eps, n=1):
                dve.sem_inc(passed, 1)
                for j in range(n):
                    ins = V.bn_stats(bst[:, p, j, :], rows[:, j * 512:(j + 1) * 512] if n > 1 else rows)
                order(ins)
                dve.sem_inc(passed, 1)
                order(V.bn_aggr(mv[:, p, :], bst[:, p, 0:n, :].rearrange("p a b -> p (a b)")))
                root(mv[:, p, 1:2], 1.0, eps)
                return order(V.tensor_copy(rstd[:, p:p + 1], rt_out[:]))

            def row(k):
                return h[:, ds(k, 1), :].rearrange("p a b -> p (a b)")

            def ln_stats(n, k, p, eps=1e-5):
                dve.wait_ge(ln_nr, free(n))
                stats(row(k), p, eps)
                V.scalar_tensor_tensor(nbias[:, p:p + 1], mv[:, p, 0:1], -1.0, rstd[:, p:p + 1], ALU.mult,
                                       ALU.mult).then_inc(ln_st, 1)

            def ln_low(n, k, bank):
                dve.wait_ge(ln_hi, n + 1)
                V.tensor_tensor(nT[1][:, :, ds(k * P, P)], ps[:, bank, :].rearrange("p (a b) -> p a b", a=KD),
                                nT[0][:, :, ds(k * P, P)], ALU.subtract).then_inc(ln_lo, 1)

            for j in range(2):
                dve.wait_ge(wt_hi, j + 1)
                split_lo(A["wt_lo"][:, 4 * j:4 * j + 4, :].rearrange("p a b -> p (a b)"), st_a[:],
                         A["wt_hi"][:, 4 * j:4 * j + 4, :].rearrange("p a b -> p (a b)"), wt_lo)
            dve.wait_ge(gw_hi, 1)
            split_lo(gw[1][:], gst[:], gw[0][:], gw_lo)
            dve.wait_ge(rows_in, 80)

            def tok_norm(i, k, p):
                dve.wait_ge(x_in[p], 16 * (i + 1))
                x = A["xt"][:, p, :]
                stats(x, p, 1e-6, 2)
                order(V.scalar_tensor_tensor(x, x, mv[:, p, 0:1], A["g1"][:], ALU.subtract, ALU.mult))
                V.scalar_tensor_tensor(x, x, rstd[:, p:p + 1], A["b1"][:], ALU.mult, ALU.add).then_inc(a_norm, 1)

            def tok_low(k, p):
                for j in range(2):
                    dve.wait_ge(a_hi, 2 * k + j + 1)
                    V.tensor_tensor(A["xT_lo"][:, p, 4 * j:4 * j + 4, :], ps[:, j, :].rearrange("p (a b) -> p a b", a=4),
                                    A["xT_hi"][:, p, 4 * j:4 * j + 4, :], ALU.subtract).then_inc(a_lo, 1)

            def tok_out(k, p):
                dve.wait_ge(a_mm, k + 1)
                z = A["z"][:, p, :]
                order(V.scalar_tensor_tensor(z, ps[:, 2 + p, :], 1.0 / WS, A["tb"][:], ALU.mult, ALU.add))
                dve.sem_inc(a_h, 1)
                stats(z, p, 1e-6)
                order(V.scalar_tensor_tensor(z, z, mv[:, p, 0:1], A["g2"][:], ALU.subtract, ALU.mult))
                order(V.scalar_tensor_tensor(row(k), z, rstd[:, p:p + 1], A["b2"][:], ALU.mult, ALU.add))

            tok_norm(0, 0, 0)
            with dve.Fori(0, NT // 2 - 1) as i:
                order.enter(i, 2 * 13)
                roots.enter(i, 6)
                for p in range(2):
                    k = 2 * i + p
                    tok_low(k, p)
                    tok_norm(i + p, k + 1, 1 - p)
                    tok_out(k, p)
                    ln_stats(k, k, p)
                    ln_low(k, k, 4 + p)
                order.leave(NT // 2 - 1)
                roots.leave(NT // 2 - 1)
            for p in range(2):
                k = NT - 2 + p
                tok_low(k, p)
                if p == 0:
                    tok_norm(NT // 2 - 1, k + 1, 1)
                tok_out(k, p)
                ln_stats(k, k, p)
                ln_low(k, k, 4 + p)
            unit_a_lo(0)
            unit_b_lo(0)
            dve.wait_ge(consts_in, 144)
            order(V.tensor_copy(identb[:], ident[:]))
            dve.wait_ge(g_mm, 1)
            lt = B["lt"]
            order(V.tensor_scalar(lt[0:AT, 0, :], ps[0:AT, 0, 0:128], 1.0 / WS, 6.906768, ALU.mult, ALU.add))
            V.scalar_tensor_tensor(lt[0:AT, 1, :], lt[0:AT, 0, :], -1.0, lt[0:AT, 0, :], ALU.mult, ALU.max).then_inc(g_mm, 1)
            dve.wait_ge(g_ln, 1)
            V.scalar_tensor_tensor(B["lg"][0:AT], lt[0:AT, 0, :].rearrange("p (a h) -> p h a", h=HEADS), 0.0,
                                   lt[0:AT, 1, :].rearrange("p (a h) -> p h a", h=HEADS), ALU.min,
                                   ALU.subtract).then_inc(g_lg, 1)
            dve.wait_ge(g_cum, 1)
            order(V.tensor_copy(B["LG"][0:AT].rearrange("p a b -> p (a b)"), ps[0:AT, 1, 0:128]))
            order(V.memset(B["v1"][:, :, DH:DH + 1], 1.0))
            order(V.memset(asum[:], 0.0))
            order(V.memset(big[:], 0.0))
            for blk in range(KD):
                ins = V.tensor_scalar(big[:, blk, :], big[:, blk, :], bcol[:, blk:blk + 1], None, ALU.add)
            order(ins)
            dve.sem_inc(g_done, 1)

            def accumulate(g, c):
                for blk in range(4):
                    dve.wait_ge(b_wc, 4 * g + blk + 1)
                    acc = big[:, blk, c * CW:(c + 1) * CW]
                    V.scalar_tensor_tensor(acc, ps[:, 6 + blk % 2, 0:CW], 1.0 / (WS * AS), acc, ALU.mult,
                                           ALU.add).then_inc(b_acc, 1)

            with dve.Fori(0, HEADS) as i:
                order.enter(i, 2 + CH * 5 + 1)
                order(V.tensor_copy(B["lgh"][0:AT], B["lg"][0:AT, ds(i, 1), :].rearrange("p a b -> p (a b)")))
                order(V.tensor_copy(B["LGh"][0:AT], B["LG"][0:AT, ds(i, 1), :].rearrange("p a b -> p (a b)")))
                for c in range(CH):
                    g = CH * i + c
                    V.tensor_tensor(B["Dg"][0:AT], B["lgh"][0:AT, 4 * c:4 * c + 4].unsqueeze(2).broadcast_to([AT, 4, AT]),
                                    tri[0:AT].unsqueeze(1).broadcast_to([AT, 4, AT]), ALU.mult).then_inc(b_D, 1)
                    dve.wait_ge(b_ev, ready(5 * g + 3))
                    order(V.tensor_tensor(B["gt"][0:AT], B["gt"][0:AT],
                                          B["LGh"][0:AT, 4 * c:4 * c + 4].unsqueeze(2).broadcast_to([AT, 4, AT]), ALU.subtract))
                    V.tensor_tensor(B["gt"][0:AT], B["gt"][0:AT], mask[0:AT].unsqueeze(1).broadcast_to([AT, 4, AT]),
                                    ALU.add).then_inc(b_g, 1)
                    if c:
                        accumulate(g - 1, c - 1)
                    dve.wait_ge(b_E, g + 1)
                    for j in range(2):
                        dve.wait_ge(b_sq, 2 * g + j + 1)
                        V.tensor_tensor(B["a"][0:AT, j], B["sq"][0:AT, j],
                                        B["E"][0:AT, 2 * j:2 * j + 2].unsqueeze(2).broadcast_to([AT, 2, REP, AT]),
                                        ALU.mult).then_inc(b_a, 1)
                    for j in range(2):
                        dve.wait_ge(b_av, 2 * g + j + 1)
                        y = ps[0:AT, 4 + 2 * j:6 + 2 * j, 0:REP * (DH + 1)].rearrange("p a (r d) -> p a r d", r=REP)
                        order(V.tensor_scalar(B["rn"][0:AT, j], y[:, :, :, DH], 1e-6, None, ALU.add))
                        order(V.reciprocal(B["rn"][0:AT, j], B["rn"][0:AT, j]))
                        V.tensor_tensor(B["yn"][0:AT, j], y[:, :, :, 0:DH],
                                        B["rn"][0:AT, j].unsqueeze(3).broadcast_to([AT, 2, REP, DH]), ALU.mult).then_inc(b_yn, 1)
                    for j in range(2):
                        dve.wait_ge(b_hi, 2 * g + j + 1)
                        V.tensor_tensor(B["yT_lo"][:, :, j * 2 * AT:(j + 1) * 2 * AT],
                                        ps[:, 2 + j, 0:CW].rearrange("p (r t) -> p r t", r=REP),
                                        B["yT_hi"][:, :, j * 2 * AT:(j + 1) * 2 * AT], ALU.subtract).then_inc(b_lo, 1)
                dve.wait_ge(q_abs, 3 * i + 4)
                order(V.tensor_tensor(asum[:], asum[:], apart[:], ALU.add))
                dve.sem_inc(q_sum, 1)
                unit_a_lo(i + 1)
                accumulate(g, c)
                unit_b_lo(i + 1)
                order.leave(HEADS)
            dve.wait_ge(q_tot, 1)
            order(V.tensor_scalar(wdq[:], ps[:, 0, 0:3], 1.0 / (D * FF), 1e-5, ALU.mult, ALU.max))
            V.reciprocal(wsc[:], wdq[:]).then_inc(q_scl, 1)
            with dve.Fori(0, NT // 2) as i:
                order.enter(i, 2 * 4)
                roots.enter(i, 2)
                for p in range(2):
                    k = 2 * i + p
                    dve.wait_ge(c_tr, ready(k))
                    order(V.tensor_tensor(row(k), ps[:, 2 + p, :], row(k), ALU.add))
                    dve.sem_inc(c_h, 1)
                    ln_stats(NT + k, k, p)
                    ln_low(NT + k, k, 4 + p)
                order.leave(NT // 2)
                roots.leave(NT // 2)

            rt = B["rt"]
            E1, sc, sbz, gt_, eq, ca, cb, sel = [rt[:, x] for x in range(8)]
            dve.wait_ge(r_exp, 1)
            order(V.tensor_scalar(sc, E1, 1.0, None, ALU.add))
            order(V.reciprocal(sc, sc))
            order(V.tensor_tensor(sbz, sc, ebias[:].unsqueeze(1).broadcast_to([P, NT, EXP]), ALU.add))
            for k in range(NT):
                ins = V.max(B["m8"][:, k, :], sbz[:, k, :])
            order(ins)
            thr = B["m8"][:, :, TOPK - 1:TOPK].broadcast_to([P, NT, EXP])
            V.tensor_tensor(gt_, sbz, thr, ALU.is_gt)
            order(V.tensor_tensor(eq, sbz, thr, ALU.is_equal))
            V.tensor_reduce(B["need"][:], gt_, AX.X, ALU.add)
            src, dst = eq, ca
            for s in (1, 2, 4, 8):
                V.tensor_copy(dst[:, :, 0:s], src[:, :, 0:s])
                order(V.tensor_tensor(dst[:, :, s:], src[:, :, s:], src[:, :, 0:EXP - s], ALU.add))
                src, dst = dst, (cb if dst is ca else ca)
            order(V.tensor_tensor(src, src, B["need"][:].unsqueeze(2).broadcast_to([P, NT, EXP]), ALU.add))
            order(V.scalar_tensor_tensor(src, src, TOPK + 0.5, eq, ALU.is_lt, ALU.mult))
            order(V.tensor_tensor(sel, src, gt_, ALU.add))
            order(V.tensor_tensor(sel, sel, sc, ALU.mult))
            order(V.tensor_reduce(B["need"][:], sel, AX.X, ALU.add))
            order(V.reciprocal(B["need"][:], B["need"][:]))
            V.memset(cw[:, EXP, :], 1.0)
            order(V.tensor_tensor(cw[:, 0:EXP, :].rearrange("p e k -> p k e"), sel,
                                  B["need"][:].unsqueeze(2).broadcast_to([P, NT, EXP]), ALU.mult))
            dve.sem_inc(r_done, 1)
            for x in range(2):
                V.memset(hact[x][:, :, T:TP], 0.0).then_inc(m_pad, 1)
            dve.sem_inc(m_t, 2)
            with dve.Fori(0, EXP + 1) as e:
                order.enter(e, 1)
                dve.wait_ge(m_acc, 4 + NT * e)
                order(V.tensor_scalar(cwe[:], cw[:, ds(e, 1), :].rearrange("p a b -> p (a b)"), 1.0 / (WS * AS), None, ALU.mult))
                for r0 in range(8):
                    r, c, ib = 8 * e + r0, r0 // 2, r0 % 2
                    dve.wait_ge(m_sg, r + 1)
                    V.scalar_tensor_tensor(Dm["ht"][:, r0 % 2, :], ps[:, 2 * (r0 % 2) + 1, 0:CW], AS / WS,
                                           Dm["sg"][:, r0 % 2, :], ALU.mult, ALU.mult).then_inc(m_t, 1)
                    dve.wait_ge(m_hi, r + 1)
                    V.tensor_tensor(hact[1][:, ib, c * CW:(c + 1) * CW], Dm["ht"][:, r0 % 2, :],
                                    hact[0][:, ib, c * CW:(c + 1) * CW], ALU.subtract).then_inc(m_lo, 1)
                unit_a_lo(HEADS + e + 1)
                for k in range(NT):
                    dve.wait_ge(m_dn, NT * e + k + 1)
                    V.scalar_tensor_tensor(h[:, k, :], ps[:, 4 + k % 4, :], cwe[:, k:k + 1], h[:, k, :], ALU.mult,
                                           ALU.add).then_inc(m_acc, 1)
                unit_b_lo(HEADS + e + 1)
                order.leave(EXP + 1)
            dve.wait_ge(wa_hi, UNITS + 1)
            split_lo(wo[1][:].rearrange("p a b -> p (a b)"), st_a[:], wo[0][:].rearrange("p a b -> p (a b)"), wa_lo)
            with dve.Fori(0, NT // 2) as i:
                order.enter(i, 2 * 3)
                roots.enter(i, 2)
                for p in range(2):
                    k = 2 * i + p
                    ln_stats(2 * NT + k, k, p)
                    ln_low(2 * NT + k, k, 4 + p)
                order.leave(NT // 2)
                roots.leave(NT // 2)
            order(V.memset(Fm["V1"][:, :, :, HD:HD + 1], 1.0))
            with dve.Fori(0, CH) as i:
                order.enter(i, 5 * 2 + 4 * 3 + 1)
                order(V.tensor_copy(Fm["nTc_hi"][:], nT[0][:, :, ds(i * CW, CW)]))
                V.tensor_copy(Fm["nTc_lo"][:], nT[1][:, :, ds(i * CW, CW)]).then_inc(f_x, 1)
                for j in range(5):
                    dve.wait_ge(f_ev, ready(22 * i + j))
                    dve.sem_inc(passed, 1)
                    qsh = Fm[("qsh", "qcs")[j % 2]]
                    order(V.stream_shuffle(qsh[:], Fm["qraw"][:, j, :], [(x + HD // 2) % HD for x in range(HD)]))
                    order(V.tensor_tensor(qsh[:], qsh[:], sinT[:], ALU.mult))
                    dve.wait_ge(f_cos, 5 * i + j + 1)
                    ins = V.tensor_tensor(Fm["qr"][:, j, :], Fm["qr"][:, j, :], qsh[:], ALU.add)
                ins.then_inc(f_rope, 1)

                def shifted(a):
                    n = 4 * i + a
                    dve.wait_ge(f_sc, n + 2)
                    if a:
                        dve.wait_ge(f_ex, n)
                    order(V.tensor_tensor(Sc[0:AT].rearrange("p (g j) s -> p g (j s)", g=G4).rearrange("p g (j s) -> p g j s", j=J4),
                                          ps[0:AT, 2:6, 0:CW].rearrange("p g (j s) -> p g j s", j=J4),
                                          maskT[0:AT].unsqueeze(1).unsqueeze(1).broadcast_to([AT, G4, J4, AT]), ALU.add))
                    order(V.tensor_reduce(Fm["mx"][0:AT], Sc[0:AT], AX.X, ALU.max))
                    V.tensor_tensor(Sc[0:AT], Sc[0:AT], Fm["mx"][0:AT].unsqueeze(2).broadcast_to([AT, 16, AT]),
                                    ALU.subtract).then_inc(f_s, 1)

                shifted(0)
                for a in range(4):
                    n = 4 * i + a
                    if a < 3:
                        shifted(a + 1)
                    dve.wait_ge(f_av, n + 1)
                    y = ps[0:AT, 6:8, 0:8 * (HD + 1)].rearrange("p b (x d) -> p b x d", d=HD + 1)
                    order(V.reciprocal(Fm["rd"][0:AT].rearrange("p (b x) -> p b x", b=2), y[:, :, :, HD]))
                    V.tensor_tensor(Fm["yo"][0:AT].rearrange("p (b x) d -> p b x d", b=2), y[:, :, :, 0:HD],
                                    Fm["rd"][0:AT].rearrange("p (b x) -> p b x", b=2).unsqueeze(3).broadcast_to([AT, 2, 8, HD]),
                                    ALU.mult).then_inc(f_yn, 1)
                    dve.wait_ge(f_hi, n + 1)
                    cols = ds(i * CW + a * AT, AT)
                    V.tensor_tensor(nT[1][:, :, cols], ps[:, 6, 0:CW].rearrange("p (b t) -> p b t", b=KD),
                                    nT[0][:, :, cols], ALU.subtract).then_inc(f_lo, 1)
                order.leave(CH)

            def quantize(p, src, dst, last, used):
                sm, am = Gm["sm"], Gm["am"]
                order(V.tensor_scalar(sm[:, p, 0:1], am[:, p:p + 1], rt_out[:, 0:1], 1e-5, ALU.mult, ALU.max))
                order(V.reciprocal(sm[:, p, 1:2], sm[:, p, 0:1]))
                order(V.scalar_tensor_tensor(sm[:, p, 2:3], sm[:, p, 1:2], 127.0, rt_out[:], ALU.mult, ALU.mult))
                order(V.tensor_scalar(src, src, sm[:, p, 2:3], MAGIC, ALU.mult, ALU.add))
                if used is not None:
                    dve.wait_ge(*used)
                V.tensor_scalar(dst, src, MAGIC, 127.0, ALU.subtract, ALU.min).then_inc(last, 1)

            with dve.Fori(0, NT // 2) as i:
                order.enter(i, 2 * 10)
                roots.enter(i, 4)
                for p in range(2):
                    k = 2 * i + p
                    n = 3 * NT + k
                    dve.wait_ge(w_mm, ready(k))
                    order(V.scalar_tensor_tensor(row(k), ps[:, p, :], 1.0 / (WS * AS), row(k), ALU.mult, ALU.add))
                    dve.sem_inc(w_h, 1)
                    ln_stats(n, k, p)
                    dve.wait_ge(ln_nr, ready(n))
                    order(V.tensor_reduce(Gm["am"][:, p:p + 1], nrm[:, p, :], AX.X, ALU.max, apply_absolute_value=True))
                    dve.wait_ge(w_sq, k + 1)
                    root(Gm["ssq"][:, p:p + 1], 1.0 / D, 1e-6)
                    quantize(p, nrm[:, p, :], Gm["qi"][:, p, :], w_q, None)
                    order(V.tensor_scalar(Gm["dq"][:, ds(k, 1)], Gm["sm"][:, p, 0:1], 1.0 / 127.0, None, ALU.mult))
                order.leave(NT // 2)
                roots.leave(NT // 2)

            def gated(k, p):
                order(V.tensor_copy(Gm["dqc"][:], Gm["dq"][:, ds(k, 1)]))
                V.tensor_scalar(Gm["dqe"][:, p, :], wdq[:, 0:2], Gm["dqc"][:, 0:1], None, ALU.mult).then_inc(x_dq, 1)
                dve.wait_ge(x_dq, k + 1)
                for f in range(NF):
                    dve.wait_ge(x_sg, 4 * k + f + 1)
                    V.scalar_tensor_tensor(ff[:, p, f * 512:(f + 1) * 512], ps[:, 2 * (f % 2) + 1, :],
                                           Gm["dqe"][:, p, 1:2], sgl[:, f % 2, :], ALU.mult, ALU.mult).then_inc(x_t, 1)

            def requantize(k, p):
                dve.wait_ge(x_t, ready(4 * k + 3))
                order(V.tensor_reduce(Gm["am"][:, p:p + 1], ff[:, p, :], AX.X, ALU.max, apply_absolute_value=True))
                dve.wait_ge(x_sq, 4 * k + 4)
                order(V.tensor_reduce(Gm["ssq"][:, p:p + 1], Gm["ssf"][:, p, :], AX.X, ALU.add))
                root(Gm["ssq"][:, p:p + 1], 1.0 / FF, 1e-6)
                quantize(p, ff[:, p, :], fi[:], x_q, (x_tr, 2 * k + 2))

            def finish(i, k, p):
                order(V.tensor_scalar(Gm["dqd"][:, p:p + 1], Gm["sm"][:, p, 0:1], wdq[:, 2:3], 1.0 / 127.0, ALU.mult, ALU.mult))
                dve.wait_ge(x_dn, k + 2)
                dve.wait_ge(out_st[p], 16 * (i + 1))
                V.scalar_tensor_tensor(og[:, p, :], ps[:, 6 + p, :], Gm["dqd"][:, p:p + 1], row(k), ALU.mult,
                                       ALU.add).then_inc(x_og, 1)

            gated(0, 0)
            with dve.Fori(0, NT // 2 - 1) as i:
                order.enter(i, 2 * 8)
                roots.enter(i, 2)
                for p in range(2):
                    k = 2 * i + p
                    requantize(k, p)
                    gated(k + 1, 1 - p)
                    finish(i, k, p)
                order.leave(NT // 2 - 1)
                roots.leave(NT // 2 - 1)
            requantize(NT - 2, 0)
            gated(NT - 1, 1)
            finish(NT // 2 - 1, NT - 2, 0)
            requantize(NT - 1, 1)
            finish(NT // 2 - 1, NT - 1, 1)


_CONSTS = {}


def constants():
    pos = np.arange(AT) % SL
    seq = np.arange(AT) // SL
    same = seq[:, None] == seq[None, :]
    causal = same & (pos[:, None] <= pos[None, :])
    tri = causal.astype(np.float32)
    mask = np.where(causal, 0.0, NEG).astype(np.float32)
    inv = np.power(np.float32(10000.0), np.float32(-2.0) * np.arange(HD // 2, dtype=np.float32) / np.float32(HD))
    ang = np.arange(SL, dtype=np.float32)[:, None] * inv[None, :].astype(np.float32)
    cos = np.tile(np.cos(ang), (1, 2)).astype(np.float32)
    sin = np.tile(np.sin(ang), (1, 2)).astype(np.float32)
    sin[:, :HD // 2] *= -1.0
    lane = np.arange(P) % HD
    p = np.arange(CW) % SL
    return dict(ident=np.eye(P, dtype=np.float32), tri=tri, mask=mask, maskT=np.ascontiguousarray(mask.T),
                cos=np.ascontiguousarray(cos[p][:, lane].T), sin=np.ascontiguousarray(sin[p][:, lane].T))


def kernel(**inp):
    import concourse.bacc as bacc
    from concourse.bass_utils import run_bass_kernel_spmd

    f = {k: np.asarray(v) for k, v in inp.items()}

    def kmaj(w):
        return w.reshape(w.shape[0] // P, P, w.shape[1]).transpose(1, 0, 2)

    x = np.zeros((TP, DIN), np.float32)
    x[:T] = f["x"][:, :SL * 16].reshape(T, DIN)
    wt = kmaj(f["L0_tok_W"])
    wa = np.zeros((UNITS, P, KD, 512), np.float32)
    wb = np.zeros((UNITS, P, 1024), np.float32)
    q, k, v, c = (kmaj(f["L0_attn_W" + n]) for n in "qkvc")
    for n in range(HEADS):
        wa[n, :, :, 0:256] = q[:, :, 256 * n:256 * (n + 1)]
        wa[n, :, :, 256:384] = k[:, :, P * n:P * (n + 1)]
        wa[n, :, :, 384:512] = v[:, :, P * n:P * (n + 1)]
        wb[n] = c[:, 2 * n:2 * n + 2].reshape(P, 1024)
    for e in range(EXP + 1):
        g, u, d = ((f["L0_ffn_w_gate"][e], f["L0_ffn_w_up"][e], f["L0_ffn_w_down"][e]) if e < EXP else
                   (f["L0_ffn_sw_gate"], f["L0_ffn_sw_up"], f["L0_ffn_sw_down"]))
        wa[HEADS + e, :, :, 0:256] = kmaj(g.T)
        wa[HEADS + e, :, :, 256:512] = kmaj(u.T)
        wb[HEADS + e] = kmaj(d.T).reshape(P, 1024)
    wq1 = f["L1_attn_Wq"].reshape(D, G4, J4, HD).transpose(0, 2, 1, 3).reshape(D, D)
    wa[UNITS - 1] = kmaj(wq1)
    wb[UNITS - 1] = np.concatenate([kmaj(f["L1_attn_Wk"]), kmaj(f["L1_attn_Wv"])], axis=2).reshape(P, 1024)
    arrays = {
        "x": x.reshape(NT, P, DIN), "wt": wt.transpose(1, 0, 2).reshape(2, 4, P, D).transpose(0, 2, 1, 3).reshape(2, P, 2048),
        "g1": f["L0_tok_g1"], "b1": f["L0_tok_b1"], "tb": f["L0_tok_b"], "g2": f["L0_tok_g2"], "b2": f["L0_tok_b2"],
        "bcol": f["L0_attn_bc"].reshape(KD, P).T, "ebias": f["L0_ffn_expert_bias"],
        "gst": np.concatenate([kmaj(f["L0_attn_Wg"]), kmaj(f["L0_ffn_gate_w"].T)], axis=2),
        "wa": wa.reshape(UNITS, P, 2048), "wb": wb,
        "wo": kmaj(f["L1_attn_Wo"]).reshape(P, 2048),
        "ffq": np.stack([kmaj(f["L1_ffn_w_gate"].T).reshape(P, 8, 1024), kmaj(f["L1_ffn_w_up"].T).reshape(P, 8, 1024),
                         kmaj(f["L1_ffn_w_down"].T).reshape(P, 8, 1024)]).transpose(0, 2, 1, 3),
    }
    arrays.update(constants())
    nc = bacc.Bacc("TRN2", target_bir_lowering=False, num_devices=1)
    t = {}
    for name in list(arrays):
        a = arrays.pop(name)
        a = np.ascontiguousarray(a)
        arrays[f"in_{name}"] = a
        t[name] = nc.dram_tensor(f"in_{name}", a.shape, mybir.dt.from_np(a.dtype), kind="ExternalInput").ap()
    out = nc.dram_tensor("out", (T, D), F32, kind="ExternalOutput").ap()
    build(nc, t, out)
    r = run_bass_kernel_spmd(nc, [arrays], core_ids=[0])
    return np.asarray(r.results[0]["out"]).reshape(SEQS, SL, D)
```

```python
from contextlib import ExitStack

import numpy as np

import concourse.bass as bass
from concourse import mybir

P = 128
SEQS, SL = 64, 23
T = SEQS * SL
NT = (T + P - 1) // P
TP = NT * P
AT = 4 * SL
CW = 4 * AT
CH = T // CW
DIN, D = 1024, 512
KI, KD = DIN // P, D // P
HEADS, REP, DH = 8, 2, 128
EXP = 16
FI = 256
TOPK = 4
G4, J4, HD = 4, 4, 32
FF = 2048
NF = FF // 512
UNITS = HEADS + EXP + 1 + 1
WS = 256.0
AS = 16.0
MAGIC = 12582912.0
NEG = -1.0e30

F32 = mybir.dt.float32
F16 = mybir.dt.float16
BF16 = mybir.dt.bfloat16
ALU = mybir.AluOpType
ACT = mybir.ActivationFunctionType
AX = mybir.AxisListType
ds = bass.ds


def free(n):
    return n + 1


def ready(n):
    return n + 3


class Order:

    def __init__(self, eng, sem):
        self.eng, self.sem, self.at, self.n = eng, sem, 0, 0

    def __call__(self, ins):
        self.n += 1
        ins.then_inc(self.sem, 1)
        self.eng.wait_ge(self.sem, self.at + self.n)

    def enter(self, i, per):
        self.base, self.per = self.at + self.n, per
        self.at, self.n = self.base + i * per, 0

    def leave(self, count):
        assert self.n == self.per, ("ordered instructions of the loop body", self.n, self.per)
        self.at, self.n = self.base + count * self.per, 0


def pipeline(eng, n, steps, order=None, ordered=0):
    lags = max(lag for lag, _ in steps)
    first = lags + lags % 2

    def turn(t):
        for lag, step in steps:
            if 0 <= t - lag < n:
                step(t - lag, (t - lag) % 2, (t - lag) // 2)

    for t in range(first):
        turn(t)
    with eng.Fori(0, (n - first) // 2) as i:
        if order:
            order.enter(i, 2 * ordered)
        for u in range(2):
            for lag, step in steps:
                c = first + u - lag
                step(2 * i + c, c % 2, i + c // 2)
        if order:
            order.leave((n - first) // 2)
    for t in range(n, n + lags):
        turn(t)


def build(nc, t, out):
    ctx = ExitStack()
    with ctx:
        def sb(name, shape, dt=F32):
            return ctx.enter_context(nc.sbuf_tensor(name, shape, dt))

        def sem(name):
            return ctx.enter_context(nc.semaphore(name))

        h = sb("h", [P, NT, D])
        nT = [sb(f"nT_{x}", [P, KD, TP], F16) for x in ("hi", "lo")]
        st_a = sb("st_a", [P, 2048])
        st_b = sb("st_b", [P, 1024])
        wa = [sb(f"wa_{x}", [P, 4, 512], F16) for x in ("hi", "lo")]
        wb = [sb(f"wb_{x}", [P, 2, 512], F16) for x in ("hi", "lo")]
        wo = [sb(f"wo_{x}", [P, KD, D], F16) for x in ("hi", "lo")]
        ident = sb("ident", [P, P])
        identb = sb("identb", [P, P], BF16)
        ones = sb("ones", [P, P])
        tri = sb("tri", [P, AT])
        mask = sb("mask", [P, AT])
        maskT = sb("maskT", [P, AT])
        cosT = sb("cosT", [P, CW])
        sinT = sb("sinT", [P, CW])
        bcol = sb("bcol", [P, KD])
        ebias = sb("ebias", [P, EXP])
        gst = sb("gst", [P, KD, HEADS + EXP])
        gw = [sb(f"gw_{x}", [P, KD, HEADS + EXP], F16) for x in ("hi", "lo")]
        rt_in = sb("rt_in", [P, NT])
        rt_out = sb("rt_out", [P, NT])
        rq_in = sb("rq_in", [P, NT])
        rq_out = sb("rq_out", [P, NT])
        neg_half = sb("neg_half", [P, NT])
        bst12 = sb("bst12", [P, NT, 6])
        mv12 = sb("mv12", [P, NT, 2])
        nb12 = sb("nb12", [P, NT])
        nrm = sb("nrm", [P, 2, D])
        cw = sb("cw", [P, EXP + 1, NT])
        cwe = sb("cwe", [P, NT])
        asum = sb("asum", [P, 3])
        apart = sb("apart", [P, 3])
        wsc = sb("wsc", [P, 3])
        wdq = sb("wdq", [P, 3])
        wq_st = sb("wq_st", [P, 3, 1024])
        big = sb("big", [P, KD, TP])
        hact = [big[:, x, :].bitcast(F16).rearrange("p (i t) -> p i t", i=2) for x in range(2)]
        Sc, Pr, PT = [big[:].rearrange("p a b -> p (a b)")[:, x * 16 * AT:(x + 1) * 16 * AT]
                      .rearrange("p (h s) -> p h s", h=16) for x in range(3)]
        flat = big[:].rearrange("p a b -> p (a b)")
        ff = flat[:, 0:2 * FF].rearrange("p (a b) -> p a b", a=2)
        fi = flat[:, 2 * FF:2 * FF + FF // 2].bitcast(BF16)
        xn = flat.rearrange("p (k d) -> p k d", d=D)
        fT = nT[0][:].rearrange("p a b -> p (a b)")[:, 0:2 * FF].bitcast(BF16).rearrange("p (x a b) -> p x a b", x=2, b=P)
        og, sgl = [st_a[:, x * 1024:(x + 1) * 1024].rearrange("p (a b) -> p a b", a=2) for x in range(2)]
        ps = ctx.enter_context(nc.psum_tensor("ps", [P, 8, 512], F32))

        def phase(specs):
            with ExitStack() as c:
                return {n: c.enter_context(nc.sbuf_tensor(n, s, d)) for n, s, d in specs}

        A = phase([("xt", [P, 2, DIN], F32), ("xh", [P, 2, DIN], F32), ("g1", [P, KI], F32), ("g1s", [P, KI], F32),
                   ("b1", [P, KI], F32), ("b1b", [P, KI, P], F32), ("bst", [P, 6, 2, 6], F32), ("mv", [P, 6, 2], F32),
                   ("nb", [P, 6], F32), ("tb", [P, D], F32), ("g2", [P, D], F32), ("b2", [P, D], F32),
                   ("wt_hi", [P, KI, D], F16), ("wt_lo", [P, KI, D], F16), ("z", [P, 2, D], F32),
                   ("xT_hi", [P, 2, KI, P], F16), ("xT_lo", [P, 2, KI, P], F16)])
        B = phase([("lg", [P, HEADS, 16], F32), ("LG", [P, HEADS, 16], F32), ("lt", [P, 3, 128], F32),
                   ("lgh", [P, 16], F32), ("LGh", [P, 16], F32),
                   ("qk", [P, 3, CW], F32), ("v1", [P, 4, DH + 1], F32), ("Dg", [P, 4, AT], F32),
                   ("gt", [P, 4, AT], F32), ("E", [P, 4, AT], F32), ("sq", [P, 2, 2, REP, AT], F32),
                   ("a", [P, 2, 2, REP, AT], F32), ("rn", [P, 2, 2, REP], F32),
                   ("yn", [P, 2, 2, REP, DH], F32), ("yT_hi", [P, REP, CW], F16),
                   ("yT_lo", [P, REP, CW], F16),
                   ("cs", [P, 2, KD, P], F32), ("rt", [P, 8, NT, EXP], F32), ("m8", [P, NT, 8], F32),
                   ("need", [P, NT], F32)])
        with ExitStack() as c:
            DG = {n: c.enter_context(nc.sbuf_tensor(n, s, d)) for n, s, d in [
                ("qw", [P, 3, 8192], BF16)]}
            Dm = phase([("sg", [P, 2, CW], F32), ("ht", [P, 2, CW], F32)])
            Fm = phase([("nTc_hi", [P, KD, CW], F16), ("nTc_lo", [P, KD, CW], F16),
                        ("qraw", [P, 5, CW], F32), ("qsh", [P, CW], F32), ("qcs", [P, CW], F32),
                        ("qr", [P, 5, CW], F32), ("V1", [P, 4, G4, HD + 1], F32),
                        ("mx", [P, 16], F32), ("rd", [P, 16], F32), ("yo", [P, 16, HD], F32)])
            Gm = phase([("jk", [P, D], F32), ("ssq", [P, NT], F32), ("am", [P, NT], F32), ("sm", [P, 3, NT], F32),
                        ("qi", [P, 2, D], BF16), ("qT", [P, KD, TP], BF16), ("dq", [P, NT], F32),
                        ("dqe", [P, 2, 2], F32), ("dqc", [P, 1], F32), ("dqd", [P, 2], F32), ("ssf", [P, 2, NF], F32),
                        ("amf", [P, 2, NF], F32), ("amg", [P, 2], F32), ("ssg", [P, 2], F32), ("smg", [P, 3, 2], F32)])
            qw = DG["qw"]

        consts_in = sem("consts_in")
        rows_in = sem("rows_in")
        ones_set = sem("ones_set")
        x_in = [sem("x_in0"), sem("x_in1")]
        wa_in, wb_in = sem("wa_in"), sem("wb_in")
        wa_hi, wb_hi = sem("wa_hi"), sem("wb_hi")
        wa_lo, wb_lo = sem("wa_lo"), sem("wb_lo")
        wt_in, wt_hi, wt_lo = sem("wt_in"), sem("wt_hi"), sem("wt_lo")
        passed = sem("passed")
        rx_ask, rz_ask, rh_ask, rc_ask, re_ask, rf_ask, rq_ask, rg_ask = [sem(f"r{x}_ask") for x in "xzhcefqg"]
        rx_done, rz_done, rh_done, rc_done, re_done, rf_done, rq_done, rg_done = [sem(f"r{x}_done") for x in "xzhcefqg"]
        dve_o, act_o, pool_o = sem("dve_o"), sem("act_o"), sem("pool_o")
        gw_hi, gw_lo = sem("gw_hi"), sem("gw_lo")
        a_norm, a_tr, a_hi, a_lo = sem("a_norm"), sem("a_tr"), sem("a_hi"), sem("a_lo")
        a_sx, a_sz, a_zn, a_row, a_b1, a_tb, a_g1 = [sem(f"a_{x}") for x in ("sx", "sz", "zn", "row", "b1", "tb", "g1")]
        a_mm, a_h = sem("a_mm"), sem("a_h")
        ln_st, ln_nr, ln_tr = sem("ln_st"), sem("ln_nr"), sem("ln_tr")
        ln_hi, ln_lo = sem("ln_hi"), sem("ln_lo")
        g_mm, g_e1, g_ln, g_lg, g_cum, g_done = [sem(f"gate_{x}") for x in
                                                ("mm", "exp", "ln", "log", "cum", "done")]
        b_pj, b_ev = sem("b_pj"), sem("b_ev")
        b_D, b_g, b_E = sem("b_D"), sem("b_g"), sem("b_E")
        b_sc, b_sq, b_a = sem("b_sc"), sem("b_sq"), sem("b_a")
        b_av, b_yn, b_yt, b_hi, b_lo = [sem(f"b_{x}") for x in ("av", "yn", "yt", "hi", "lo")]
        b_wc, b_acc = sem("b_wc"), sem("b_acc")
        acc_set = sem("acc_set")
        q_in, q_abs, q_sum, q_tot, q_scl = [sem(f"q_{x}") for x in ("in", "abs", "sum", "tot", "scl")]
        c_cp, c_tr, c_h = sem("c_cp"), sem("c_tr"), sem("c_h")
        r_mm, r_exp, r_done = sem("r_mm"), sem("r_exp"), sem("r_done")
        m_gu, m_sg, m_t, m_hi, m_lo = [sem(f"m_{x}") for x in ("gu", "sg", "t", "hi", "lo")]
        m_dn, m_acc, m_pad = sem("m_dn"), sem("m_acc"), sem("m_pad")
        pool_z = sem("pool_z")
        t_in, t_done = [sem("t_in0"), sem("t_in1")], sem("t_done")
        f_x, f_pj, f_ev, f_cos, f_rope, f_sc, f_s = [sem(f"f_{x}") for x in
                                                    ("x", "pj", "ev", "cos", "rope", "sc", "s")]
        f_ex, f_av, f_yn, f_yt, f_hi, f_lo = [sem(f"f_{x}") for x in ("ex", "av", "yn", "yt", "hi", "lo")]
        w_mm, w_h, w_sq, w_q, w_tr, w_ev = [sem(f"w_{x}") for x in ("mm", "h", "sq", "q", "tr", "ev")]
        w_n, w_am, w_r, x_am = sem("w_n"), sem("w_am"), sem("w_r"), sem("x_am")
        x_gu, x_dq, x_sg, x_t, x_sq, x_q = [sem(f"x_{x}") for x in ("gu", "dq", "sg", "t", "sq", "q")]
        x_tr, x_ev, x_dn, x_og = [sem(f"x_{x}") for x in ("tr", "ev", "dn", "og")]
        out_st = [sem("out_st0"), sem("out_st1")]

        block = ctx.enter_context(nc.Block())

        @block.sync
        def _(sp):
            def unit_a(n):
                sp.dma_start(st_a[:], t["wa"][n]).then_inc(wa_in, 16)

            def unit_b(n):
                sp.dma_start(st_b[:], t["wb"][n]).then_inc(wb_in, 16)

            for p in range(2):
                sp.sem_inc(out_st[p], 16)
            for k in range(2):
                sp.dma_start(A["xt"][:, k, :], t["x"][k]).then_inc(x_in[k], 16)
            sp.dma_start(A["g1"][:], t["g1"]).then_inc(rows_in, 16)
            sp.dma_start(A["b1"][:], t["b1"]).then_inc(rows_in, 16)
            for x in ("tb", "g2", "b2"):
                sp.dma_start(A[x][:], t[x].rearrange("(a n) -> a n", a=1).broadcast_to([P, D])).then_inc(rows_in, 16)
            sp.dma_start(st_a[:], t["wt"][0]).then_inc(wt_in, 16)
            for dst, src in ((ident, "ident"), (cosT, "cos"), (sinT, "sin"), (gst, "gst"), (bcol, "bcol")):
                sp.dma_start(dst[:], t[src]).then_inc(consts_in, 16)
            sp.dma_start(tri[0:AT, :], t["tri"]).then_inc(consts_in, 16)
            sp.dma_start(mask[0:AT, :], t["mask"]).then_inc(consts_in, 16)
            sp.dma_start(maskT[0:AT, :], t["maskT"]).then_inc(consts_in, 16)
            sp.dma_start(ebias[:], t["ebias"].rearrange("(a n) -> a n", a=1).broadcast_to([P, EXP])).then_inc(consts_in, 16)
            sp.wait_ge(wt_lo, 1)
            sp.wait_ge(a_tb, 1)
            sp.dma_start(st_a[:], t["wt"][1]).then_inc(wt_in, 16)
            unit_b(0)
            with sp.Fori(0, NT // 2 - 1) as i:
                for p in range(2):
                    sp.wait_ge(a_norm, 2 * i + p + 1)
                    sp.dma_start(A["xt"][:, p, :], t["x"][2 * i + p + 2]).then_inc(x_in[p], 16)
            sp.wait_ge(wt_lo, 2)
            sp.wait_ge(a_tb, 2)
            unit_a(0)
            with sp.Fori(0, HEADS) as i:
                sp.wait_ge(q_abs, 3 * i + 1)
                for m in range(3):
                    sp.dma_start(wq_st[:, m, :], t["ffq"][m, i]).then_inc(q_in, 16)
                sp.wait_ge(wa_lo, i + 1)
                unit_a(i + 1)
                sp.wait_ge(wb_lo, i + 1)
                unit_b(i + 1)
            with sp.Fori(HEADS, UNITS - 1) as i:
                sp.wait_ge(wa_lo, i + 1)
                unit_a(i + 1)
                sp.wait_ge(wb_lo, i + 1)
                unit_b(i + 1)
            sp.wait_ge(wa_lo, UNITS)
            sp.dma_start(st_a[:], t["wo"]).then_inc(wa_in, 16)
            with sp.Fori(0, NT // 2 - 1) as i:
                for p in range(2):
                    k = 2 * i + p
                    sp.wait_ge(x_og, ready(k))
                    sp.dma_start(out[ds(k * P, P), :], og[:, p, :]).then_inc(out_st[p], 16)
            for k in (NT - 2, NT - 1):
                rows = T - k * P if k == NT - 1 else P
                sp.wait_ge(x_og, ready(k))
                sp.dma_start(out[k * P:k * P + rows, :], og[0:rows, k % 2, :]).then_inc(out_st[k % 2], 16)
            for p in range(2):
                sp.wait_ge(out_st[p], 16 * (NT // 2) + 16)
        @block.gpsimd
        def _(pool):
            nc.gpsimd.memset(ones[:], 1.0).then_inc(ones_set, 1)
            nc.gpsimd.memset(neg_half[:], -0.5).then_inc(ones_set, 1)
            pool.wait_ge(ones_set, 2)

            def root(ask, n, src, dst, done):
                pool.wait_ge(ask, n + 1)
                nc.gpsimd.tensor_tensor(dst, src, neg_half[:, 0:src.shape[1]], ALU.pow).then_inc(done, 1)

            def root_of(ask, kind, done):
                return lambda k, p, half: root(ask, k, rt_in[:, 2 * kind + p:2 * kind + p + 1],
                                               rt_out[:, 2 * kind + p:2 * kind + p + 1], done)

            def affine(k, p, half):
                pool.wait_ge(a_zn, k + 1)
                nc.gpsimd.tensor_tensor(A["z"][:, p, :], A["z"][:, p, :], A["g2"][:], ALU.mult).then_inc(pool_z, 1)
                pool.wait_ge(pool_z, k + 1)
                pool.sem_inc(passed, 1)
                nc.gpsimd.tensor_tensor(h[:, ds(k, 1), :].rearrange("p a b -> p (a b)"), A["z"][:, p, :], A["b2"][:],
                                        ALU.add).then_inc(a_row, 1)

            pool.wait_ge(rows_in, 80)
            pipeline(pool, NT, [(3, root_of(rz_ask, 1, rz_done)), (0, root_of(rx_ask, 0, rx_done)),
                                (4, root_of(rh_ask, 2, rh_done)), (3, affine)])
            root(rc_ask, 0, rt_in[:], rt_out[:], rc_done)
            pool.wait_ge(q_scl, 1)
            pool.wait_ge(r_done, 1)
            porder = Order(pool, pool_o)
            for m in range(3):
                with pool.Fori(0, 4) as i:
                    porder.enter(i, 6)
                    for p in range(2):
                        pool.dma_start(wq_st[:, p, :], t["ffq"][m, 2 * i + p]).then_inc(t_in[p], 16)
                    for p in range(2):
                        pool.wait_ge(t_in[p], 16 * (4 * m + i + 1))
                        pool.sem_inc(passed, 1)
                        porder(nc.gpsimd.tensor_scalar(wq_st[:, 2, :], wq_st[:, p, :], wsc[:, m:m + 1], 0.5,
                                                       ALU.mult, ALU.is_gt))
                        pool.sem_inc(passed, 1)
                        porder(nc.gpsimd.tensor_scalar(wq_st[:, p, :], wq_st[:, p, :], wsc[:, m:m + 1], -0.5,
                                                       ALU.mult, ALU.is_lt))
                        pool.sem_inc(passed, 1)
                        porder(nc.gpsimd.tensor_tensor(qw[:, m, ds((2 * i + p) * 1024, 1024)], wq_st[:, 2, :],
                                                       wq_st[:, p, :], ALU.subtract))
                    porder.leave(4)
            pool.sem_inc(t_done, 1)
            root(re_ask, 0, rt_in[:], rt_out[:], re_done)
            with pool.Fori(0, CH) as i:
                pool.wait_ge(f_sc, 4 * i + 1)
                for j in range(5):
                    pool.wait_ge(f_ev, ready(22 * i + j))
                    nc.gpsimd.tensor_tensor(Fm["qr"][:, j, :], Fm["qraw"][:, j, :], cosT[:], ALU.mult).then_inc(f_cos, 1)
            root(rf_ask, 0, rt_in[:], rt_out[:], rf_done)
            root(rq_ask, 0, rq_in[:], rq_out[:], rq_done)
            pipeline(pool, NT, [(0, lambda k, p, half: root(rg_ask, k, rq_in[:, p:p + 1], rq_out[:, p:p + 1], rg_done))])

        @block.scalar
        def _(act):
            act.sem_inc(ln_nr, 2)
            act.sem_inc(b_ev, 2)
            act.sem_inc(q_abs, 1)
            act.sem_inc(f_ev, 2)
            act.sem_inc(w_ev, 2)
            act.sem_inc(w_sq, 1)
            act.sem_inc(x_sq, 1)
            act.sem_inc(x_ev, 2)
            act.wait_ge(ones_set, 1)

            def split_hi(dst, src, scale, into, sem_out):
                nc.scalar.activation(dst, src, ACT.Copy, scale=scale).then_inc(sem_out, 1)

            def unit_a_hi(n, used=None, count=0):
                act.wait_ge(wa_in, 16 * (n + 1))
                if used is not None:
                    act.wait_ge(used, count)
                nc.scalar.activation(wa[0][:].rearrange("p a b -> p (a b)"), st_a[:], ACT.Copy, scale=WS).then_inc(wa_hi, 1)

            def unit_b_hi(n, used=None, count=0):
                act.wait_ge(wb_in, 16 * (n + 1))
                if used is not None:
                    act.wait_ge(used, count)
                nc.scalar.activation(wb[0][:].rearrange("p a b -> p (a b)"), st_b[:], ACT.Copy, scale=WS).then_inc(wb_hi, 1)

            def ln_norm(use, k, p):
                act.wait_ge(ln_tr, free(use * NT + k))
                nc.scalar.activation(nrm[:, p, :], h[:, ds(k, 1), :].rearrange("p a b -> p (a b)"), ACT.Identity,
                                     bias=nb12[:, ds(k, 1)], scale=rt_out[:, ds(k, 1)]).then_inc(ln_nr, 1)

            def ln_rows(use):
                act.wait_ge(ln_st, use + NT)
                pipeline(act, NT, [(0, lambda k, p, half: ln_norm(use, k, p)),
                                   (1, lambda k, p, half: ln_high(use * NT + k, k, 4 + p))])

            def ln_high(n, k, bank):
                act.wait_ge(ln_tr, ready(n))
                nc.scalar.activation(nT[0][:, :, ds(k * P, P)],
                                     ps[:, bank, :].rearrange("p (a b) -> p a b", a=KD), ACT.Copy).then_inc(ln_hi, 1)

            for j in range(2):
                act.wait_ge(wt_in, 16 * (j + 1))
                act.wait_ge(a_g1, 1)
                for b in range(4):
                    ins = nc.scalar.activation(A["wt_hi"][:, 4 * j + b, :], st_a[:, b * D:(b + 1) * D], ACT.Identity,
                                               scale=A["g1s"][:, 4 * j + b:4 * j + b + 1])
                ins.then_inc(wt_hi, 1)
            act.wait_ge(consts_in, 144)
            nc.scalar.activation(gw[0][:], gst[:], ACT.Copy, scale=WS).then_inc(gw_hi, 1)

            def tok_high(k, p, half):
                act.wait_ge(a_mm, free(k))
                for j in range(2):
                    act.wait_ge(a_tr, 2 * k + j + 1)
                    nc.scalar.activation(A["xT_hi"][:, p, 4 * j:4 * j + 4, :],
                                         ps[:, j, :].rearrange("p (a b) -> p a b", a=4), ACT.Copy).then_inc(a_hi, 1)

            def x_norm(k, p, half):
                act.wait_ge(a_sx, k + 1)
                nc.scalar.activation(A["xh"][:, p, :], A["xt"][:, p, :], ACT.Identity, bias=A["nb"][:, p:p + 1],
                                     scale=rt_out[:, p:p + 1]).then_inc(a_norm, 1)

            def z_norm(k, p, half):
                act.wait_ge(a_sz, k + 1)
                nc.scalar.activation(A["z"][:, p, :], A["z"][:, p, :], ACT.Identity, bias=A["nb"][:, 2 + p:3 + p],
                                     scale=rt_out[:, 2 + p:3 + p]).then_inc(a_zn, 1)

            def h_norm(k, p, half):
                act.wait_ge(ln_st, k + 1)
                act.wait_ge(ln_tr, free(k))
                nc.scalar.activation(nrm[:, p, :], h[:, ds(k, 1), :].rearrange("p a b -> p (a b)"), ACT.Identity,
                                     bias=A["nb"][:, 4 + p:5 + p], scale=rt_out[:, 4 + p:5 + p]).then_inc(ln_nr, 1)

            pipeline(act, NT, [(1, tok_high), (0, x_norm), (3, z_norm), (4, h_norm),
                               (5, lambda k, p, half: ln_high(k, k, 4 + p))])
            unit_a_hi(0)
            unit_b_hi(0)
            act.wait_ge(g_mm, 2)
            nc.scalar.activation(B["lt"][0:AT, 1, :], B["lt"][0:AT, 1, :], ACT.Exp, scale=-1.0).then_inc(g_e1, 1)
            act.wait_ge(g_e1, 1)
            nc.scalar.activation(B["lt"][0:AT, 1, :], B["lt"][0:AT, 1, :], ACT.Ln, bias=1.0).then_inc(g_ln, 1)
            oh = B["yT_hi"]
            with act.Fori(0, HEADS) as i:
                for c in range(CH):
                    g = CH * i + c
                    for j in range(3):
                        act.wait_ge(b_pj, 5 * g + j + 1)
                        nc.scalar.activation(B["qk"][:, j, :], ps[:, (5 * c + j) % 2, 0:CW], ACT.Copy,
                                             scale=1.0 / WS).then_inc(b_ev, 1)
                    act.wait_ge(b_pj, 5 * g + 4)
                    nc.scalar.activation(B["gt"][0:AT].rearrange("p a b -> p (a b)"),
                                         ps[0:AT, (5 * c + 3) % 2, 0:CW], ACT.Copy).then_inc(b_ev, 1)
                    act.wait_ge(b_pj, 5 * g + 5)
                    nc.scalar.activation(B["v1"][0:AT, :, 0:DH],
                                         ps[0:AT, (5 * c + 4) % 2, :].rearrange("p (a b) -> p a b", a=4), ACT.Copy,
                                         scale=AS / WS).then_inc(b_ev, 1)
                    act.wait_ge(b_g, g + 1)
                    nc.scalar.activation(B["E"][0:AT], B["gt"][0:AT], ACT.Exp).then_inc(b_E, 1)
                    for j in range(2):
                        act.wait_ge(b_sc, 2 * g + j + 1)
                        nc.scalar.activation(B["sq"][0:AT, j].rearrange("p a r t -> p (a r t)"), ps[0:AT, 2 + j, 0:2 * REP * AT],
                                             ACT.Square, scale=float(DH) ** -0.5).then_inc(b_sq, 1)
                    for j in range(2):
                        act.wait_ge(b_yt, 2 * g + j + 1)
                        nc.scalar.activation(oh[:, :, j * 2 * AT:(j + 1) * 2 * AT],
                                             ps[:, 2 + j, 0:CW].rearrange("p (r t) -> p r t", r=REP), ACT.Copy).then_inc(b_hi, 1)
                    if c == 0:
                        for m in range(3):
                            if m == 0:
                                act.wait_ge(q_in, 48 * (i + 1))
                                act.wait_ge(q_sum, i + 1)
                            nc.scalar.activation(wq_st[:, m, :], wq_st[:, m, :], ACT.Abs,
                                                 accum_out=apart[:, m:m + 1]).then_inc(q_abs, 1)
                unit_a_hi(i + 1, b_pj, 5 * CH * (i + 1))
                unit_b_hi(i + 1, b_wc, 4 * CH * (i + 1))
            act.wait_ge(b_acc, 4 * CH * HEADS + 2)

            def c_copy(k, p, half):
                act.wait_ge(c_tr, free(k))
                nc.scalar.activation(B["cs"][:, p], big[:, :, ds(k * P, P)], ACT.Copy).then_inc(c_cp, 1)

            pipeline(act, NT, [(0, c_copy)])
            ln_rows(1)
            act.wait_ge(r_mm, 1)
            nc.scalar.activation(B["rt"][:, 0], ps[:, 6, 0:NT * EXP].rearrange("p (a b) -> p a b", a=NT), ACT.Exp,
                                 scale=-1.0 / WS).then_inc(r_exp, 1)
            with act.Fori(0, EXP + 1) as e:
                for r0 in range(8):
                    r = 8 * e + r0
                    c, ib = r0 // 2, r0 % 2
                    act.wait_ge(m_gu, r + 1)
                    act.wait_ge(m_t, free(r))
                    nc.scalar.activation(Dm["sg"][:, r0 % 2, :], ps[:, 2 * (r0 % 2), 0:CW], ACT.Silu,
                                         scale=1.0 / WS).then_inc(m_sg, 1)
                    if r0 == 0:
                        act.wait_ge(m_acc, NT * e + 4)
                    act.wait_ge(m_t, ready(r))
                    nc.scalar.activation(hact[0][:, ib, c * CW:(c + 1) * CW], Dm["ht"][:, r0 % 2, :],
                                         ACT.Copy).then_inc(m_hi, 1)
                unit_a_hi(HEADS + e + 1, m_gu, 8 * (e + 1))
                unit_b_hi(HEADS + e + 1, m_dn, NT * (e + 1))
            act.wait_ge(wa_in, 16 * (UNITS + 1))
            nc.scalar.activation(wo[0][:].rearrange("p a b -> p (a b)"), st_a[:], ACT.Copy, scale=WS).then_inc(wa_hi, 1)
            ln_rows(2)
            with act.Fori(0, CH) as i:
                for j in range(5):
                    act.wait_ge(f_pj, 22 * i + j + 1)
                    nc.scalar.activation(Fm["qraw"][:, j, :], ps[:, j % 2, 0:CW], ACT.Copy, scale=1.0 / WS).then_inc(f_ev, 1)
                act.wait_ge(f_pj, 22 * i + 6)
                nc.scalar.activation(Fm["V1"][0:AT, :, :, 0:HD],
                                     ps[0:AT, 1, :].rearrange("p (a g d) -> p a g d", a=4, g=G4), ACT.Copy,
                                     scale=AS / WS).then_inc(f_ev, 1)
                for a in range(4):
                    n = 4 * i + a
                    act.wait_ge(f_s, ready(n) - 1)
                    nc.scalar.activation(Pr[0:AT], Sc[0:AT], ACT.Exp, scale=float(HD) ** -0.5).then_inc(f_ex, 1)
                    for g in range(G4):
                        m = 22 * i + 6 + 4 * a + g
                        act.wait_ge(f_pj, m + 1)
                        nc.scalar.activation(PT[0:AT, 4 * g:4 * g + 4, :].rearrange("p a b -> p (a b)"),
                                             ps[0:AT, g % 2, 0:CW], ACT.Copy).then_inc(f_ev, 1)
                    act.wait_ge(f_yt, n + 1)
                    nc.scalar.activation(nT[0][:, :, ds(i * CW + a * AT, AT)],
                                         ps[:, 6, 0:CW].rearrange("p (b t) -> p b t", b=KD), ACT.Copy).then_inc(f_hi, 1)
            act.wait_ge(ln_st, NT + 3)

            def f_norm(k, p, half):
                nc.scalar.activation(xn[:, ds(k, 1), :].rearrange("p a b -> p (a b)"),
                                     h[:, ds(k, 1), :].rearrange("p a b -> p (a b)"), ACT.Identity,
                                     bias=nb12[:, ds(k, 1)], scale=rt_out[:, ds(k, 1)]).then_inc(w_n, 1)

            def f_square(k, p, half):
                act.wait_ge(w_n, k + 1)
                act.wait_ge(w_sq, k + 1)
                nc.scalar.activation(Gm["jk"][:], xn[:, ds(k, 1), :].rearrange("p a b -> p (a b)"), ACT.Square,
                                     accum_out=Gm["ssq"][:, ds(k, 1)]).then_inc(w_sq, 1)

            def f_turned_rows(k, p, half):
                act.wait_ge(w_tr, k + 1)
                nc.scalar.activation(Gm["qT"][:, :, ds(k * P, P)],
                                     ps[:, 2 + p, 0:256].bitcast(BF16).rearrange("p (a b) -> p a b", a=KD),
                                     ACT.Copy).then_inc(w_ev, 1)

            pipeline(act, NT, [(0, f_norm), (1, f_square)])
            pipeline(act, NT, [(0, f_turned_rows)])

            def gated(k, p, half):
                def silu(f):
                    act.wait_ge(x_gu, 4 * k + f + 1)
                    act.wait_ge(x_t, free(4 * k + f))
                    if f == 0:
                        act.wait_ge(x_dq, k + 1)
                    nc.scalar.activation(sgl[:, f % 2, :], ps[:, 2 * (f % 2), :], ACT.Silu,
                                         scale=Gm["dqe"][:, p, 0:1]).then_inc(x_sg, 1)

                def square(f):
                    act.wait_ge(x_t, ready(4 * k + f))
                    act.wait_ge(x_sq, 4 * k + f + 1)
                    nc.scalar.activation(Gm["jk"][:], ff[:, p, f * 512:(f + 1) * 512], ACT.Square,
                                         accum_out=Gm["ssf"][:, p, f:f + 1]).then_inc(x_sq, 1)

                silu(0)
                for f in range(1, NF):
                    silu(f)
                    square(f - 1)
                square(NF - 1)

            def f_turned(k, p, half):
                act.wait_ge(x_dn, free(k))
                for j in range(2):
                    act.wait_ge(x_tr, 2 * k + j + 3)
                    nc.scalar.activation(fT[:, p, 8 * j:8 * j + 8, :].rearrange("p a b -> p (a b)"),
                                         ps[:, 4 + j, :].bitcast(BF16), ACT.Copy).then_inc(x_ev, 1)

            pipeline(act, NT, [(0, gated), (1, f_turned)])

        @block.tensor
        def _(pe):
            pe.sem_inc(ln_tr, 2)
            pe.sem_inc(c_tr, 2)
            pe.sem_inc(f_sc, 1)
            pe.sem_inc(a_mm, 2)
            pe.sem_inc(x_tr, 2)
            pe.sem_inc(x_dn, 2)
            pe.wait_ge(consts_in, 144)
            pe.wait_ge(ones_set, 1)

            def ln_turn(n, p, bank):
                pe.wait_ge(ln_nr, ready(n))
                pe.wait_ge(ln_lo, free(n))
                for b in range(KD):
                    ins = nc.tensor.transpose(ps[:, bank, b * P:(b + 1) * P], nrm[:, p, b * P:(b + 1) * P], ident[:])
                ins.then_inc(ln_tr, 1)

            def split3(dst, lhs, rhs, start, stop):
                nc.tensor.matmul(dst, lhs[0], rhs[0], start=start, stop=False)
                nc.tensor.matmul(dst, lhs[0], rhs[1], start=False, stop=False)
                return nc.tensor.matmul(dst, lhs[1], rhs[0], start=False, stop=stop)

            def tok_turn(k, p, half):
                pe.wait_ge(a_norm, k + 1)
                for j in range(2):
                    pe.wait_ge(a_lo, 2 * k + j + 1)
                    for b in range(4):
                        ins = nc.tensor.transpose(ps[:, j, b * P:(b + 1) * P],
                                                  A["xh"][:, p, (4 * j + b) * P:(4 * j + b + 1) * P], ident[:])
                    ins.then_inc(a_tr, 1)

            def tok_mm(k, p, half):
                pe.wait_ge(a_lo, 2 * k + 4)
                pe.wait_ge(a_h, free(k))
                for b in range(KI):
                    ins = split3(ps[:, 2 + p, :], [A["xT_hi"][:, p, b, :], A["xT_lo"][:, p, b, :]],
                                 [A["wt_hi"][:, b, :], A["wt_lo"][:, b, :]], b == 0, b == KI - 1)
                ins.then_inc(a_mm, 1)

            pe.wait_ge(a_b1, 1)
            for j in range(2):
                pe.wait_ge(wt_in, 16 * (j + 1))
                for b in range(4):
                    ins = nc.tensor.matmul(ps[:, 7, :], A["b1b"][:, 4 * j + b, :], st_a[:, b * D:(b + 1) * D],
                                           start=j == 0 and b == 0, stop=j == 1 and b == 3)
                ins.then_inc(a_tb, 1)
            pe.wait_ge(wt_lo, 2)
            pipeline(pe, NT, [(1, tok_turn), (2, tok_mm), (5, lambda k, p, half: ln_turn(k, p, 4 + p))])
            pe.wait_ge(ln_lo, ready(NT - 1))
            pe.wait_ge(gw_lo, 1)
            for a in range(T // AT):
                for b in range(KD):
                    x = [nT[0][:, b, a * AT:(a + 1) * AT], nT[1][:, b, a * AT:(a + 1) * AT]]
                    ins = split3(ps[0:AT, 0, a * HEADS:(a + 1) * HEADS], x,
                                 [gw[0][:, b, 0:HEADS], gw[1][:, b, 0:HEADS]], b == 0, b == KD - 1)
            ins.then_inc(g_mm, 1)
            pe.wait_ge(g_lg, 1)
            nc.tensor.matmul(ps[0:AT, 1, 0:16 * HEADS], tri[0:AT, :], B["lg"][0:AT].rearrange("p a b -> p (a b)"),
                             start=True, stop=True).then_inc(g_cum, 1)

            def out_proj(g, c):
                pe.wait_ge(b_lo, 2 * g + 4)
                for blk in range(4):
                    pe.wait_ge(b_acc, free(4 * g + blk))
                    for r in range(REP):
                        ins = split3(ps[:, 6 + blk % 2, 0:CW],
                                     [wb[x][:, r, blk * P:(blk + 1) * P] for x in range(2)],
                                     [B["yT_hi"][:, r, :], B["yT_lo"][:, r, :]], r == 0, r == REP - 1)
                    ins.then_inc(b_wc, 1)

            pe.wait_ge(g_done, 1)
            with pe.Fori(0, HEADS) as i:
                pe.wait_ge(wa_lo, i + 1)
                for c in range(CH):
                    g = CH * i + c
                    cols = slice(c * CW, (c + 1) * CW)
                    for j in range(3):
                        pe.wait_ge(b_ev, free(5 * g + j))
                        for b in range(KD):
                            ins = split3(ps[:, (5 * c + j) % 2, 0:CW], [wa[x][:, b, j * P:(j + 1) * P] for x in range(2)],
                                         [nT[x][:, b, cols] for x in range(2)], b == 0, b == KD - 1)
                        ins.then_inc(b_pj, 1)
                    pe.wait_ge(b_ev, free(5 * g + 3))
                    pe.wait_ge(b_D, g + 1)
                    nc.tensor.matmul(ps[0:AT, (5 * c + 3) % 2, 0:CW], ones[0:AT, 0:AT], B["Dg"][0:AT].rearrange("p a b -> p (a b)"),
                                     start=True, stop=True).then_inc(b_pj, 1)
                    pe.wait_ge(b_ev, free(5 * g + 4))
                    for a in range(4):
                        tok = slice(c * CW + a * AT, c * CW + (a + 1) * AT)
                        for b in range(KD):
                            ins = split3(ps[0:AT, (5 * c + 4) % 2, a * P:(a + 1) * P], [nT[x][:, b, tok] for x in range(2)],
                                         [wa[x][:, b, 3 * P:4 * P] for x in range(2)], b == 0, b == KD - 1)
                    ins.then_inc(b_pj, 1)
                    pe.wait_ge(b_ev, ready(5 * g + 2))
                    for j in range(2):
                        pe.wait_ge(b_lo, free(2 * g + j))
                        for a in range(2):
                            tok = slice((2 * j + a) * AT, (2 * j + a + 1) * AT)
                            ins = nc.tensor.matmul(ps[0:AT, 2 + j, a * REP * AT:(a + 1) * REP * AT],
                                                   B["qk"][:, 2, tok], B["qk"][:, 0:2, tok], start=True, stop=True)
                        ins.then_inc(b_sc, 1)
                    if c:
                        if c == 1:
                            pe.wait_ge(wb_lo, i + 1)
                        out_proj(g - 1, c - 1)
                    pe.wait_ge(b_ev, ready(5 * g + 4))
                    for j in range(2):
                        pe.wait_ge(b_a, 2 * g + j + 1)
                        if j == 1:
                            pe.wait_ge(b_acc, 4 * g + 2)
                        for a in range(2):
                            for r in range(REP):
                                ins = nc.tensor.matmul(ps[0:AT, 4 + 2 * j + a, r * (DH + 1):(r + 1) * (DH + 1)],
                                                       B["a"][0:AT, j, a, r, :], B["v1"][0:AT, 2 * j + a, :],
                                                       start=True, stop=True)
                        ins.then_inc(b_av, 1)
                    for j in range(2):
                        pe.wait_ge(b_yn, 2 * g + j + 1)
                        for r in range(REP):
                            for a in range(2):
                                ins = nc.tensor.transpose(ps[:, 2 + j, (2 * r + a) * AT:(2 * r + a + 1) * AT],
                                                          B["yn"][0:AT, j, a, r, :], ident[0:AT, 0:AT])
                        ins.then_inc(b_yt, 1)
                out_proj(g, c)
            pe.wait_ge(q_sum, HEADS + 1)
            nc.tensor.matmul(ps[:, 0, 0:3], ones[:], asum[:], start=True, stop=True).then_inc(q_tot, 1)

            def route(k):
                pe.wait_ge(ln_lo, ready(NT + k))
                for b in range(KD):
                    ins = split3(ps[:, 6, ds(k * EXP, EXP)], [nT[x][:, b, ds(k * P, P)] for x in range(2)],
                                 [gw[x][:, b, HEADS:] for x in range(2)], b == 0, b == KD - 1)
                return ins

            def c_turn(k, p, half):
                pe.wait_ge(c_cp, k + 1)
                pe.wait_ge(c_h, free(k))
                for b in range(KD):
                    ins = nc.tensor.transpose(ps[:, 2 + p, b * P:(b + 1) * P], B["cs"][:, p, b, :], ident[:])
                ins.then_inc(c_tr, 1)

            pipeline(pe, NT, [(0, c_turn)])
            pipeline(pe, NT, [(0, lambda k, p, half: ln_turn(NT + k, p, 4 + p))])
            for k in range(NT):
                ins = route(k)
            ins.then_inc(r_mm, 1)
            with pe.Fori(0, EXP + 1) as e:
                pe.wait_ge(wa_lo, HEADS + e + 1)
                for r0 in range(8):
                    r, c, ib = 8 * e + r0, r0 // 2, r0 % 2
                    pe.wait_ge(m_t, free(r))
                    for q in range(2):
                        for b in range(KD):
                            ins = split3(ps[:, 2 * (r0 % 2) + q, 0:CW],
                                         [wa[x][:, b, q * FI + ib * P:q * FI + (ib + 1) * P] for x in range(2)],
                                         [nT[x][:, b, c * CW:(c + 1) * CW] for x in range(2)], b == 0, b == KD - 1)
                    ins.then_inc(m_gu, 1)
                pe.wait_ge(wb_lo, HEADS + e + 1)
                pe.wait_ge(m_pad, 2)
                for k in range(NT):
                    last = min((k * P + P - 1) // CW, CH - 1)
                    pe.wait_ge(m_lo, 8 * e + 2 * last + 2)
                    pe.wait_ge(m_acc, NT * e + k + 1)
                    for ib in range(2):
                        ins = split3(ps[:, 4 + k % 4, :], [hact[x][:, ib, k * P:(k + 1) * P] for x in range(2)],
                                     [wb[x][:, ib, :] for x in range(2)], ib == 0, ib == 1)
                    ins.then_inc(m_dn, 1)
            pipeline(pe, NT, [(0, lambda k, p, half: ln_turn(2 * NT + k, p, 4 + p))])
            wkv = [wb[x][:].rearrange("p a b -> p (a b)").rearrange("p (a b) -> p a b", a=KD) for x in range(2)]
            nc_ = [Fm["nTc_hi"], Fm["nTc_lo"]]
            pe.wait_ge(wa_lo, UNITS)
            pe.wait_ge(wb_lo, UNITS)
            with pe.Fori(0, CH) as i:
                pe.wait_ge(f_x, i + 1)
                for j in range(5):
                    pe.wait_ge(f_ev, free(22 * i + j))
                    for b in range(KD):
                        w = [wa[x][:, b, j * P:(j + 1) * P] if j < 4 else wkv[x][:, b, 0:P] for x in range(2)]
                        ins = split3(ps[:, j % 2, 0:CW], w, [nc_[x][:, b, :] for x in range(2)], b == 0, b == KD - 1)
                    ins.then_inc(f_pj, 1)
                pe.wait_ge(f_ev, free(22 * i + 5))
                for a in range(4):
                    for b in range(KD):
                        ins = split3(ps[0:AT, 1, a * P:(a + 1) * P], [nc_[x][:, b, a * AT:(a + 1) * AT] for x in range(2)],
                                     [wkv[x][:, b, P:2 * P] for x in range(2)], b == 0, b == KD - 1)
                ins.then_inc(f_pj, 1)
                pe.wait_ge(f_rope, i + 1)

                def scores(a):
                    pe.wait_ge(f_s, 4 * i + a + 1)
                    tok = slice(a * AT, (a + 1) * AT)
                    for j in range(J4):
                        for g in range(G4):
                            r = slice(HD * g, HD * (g + 1))
                            ins = nc.tensor.matmul(ps[0:AT, 2 + g, j * AT:(j + 1) * AT], Fm["qr"][r, j, tok],
                                                   Fm["qr"][r, 4, tok], start=True, stop=True)
                    ins.then_inc(f_sc, 1)

                scores(0)
                for a in range(4):
                    n = 4 * i + a
                    if a < 3:
                        scores(a + 1)
                    pe.wait_ge(f_ex, n + 1)
                    for g in range(G4):
                        m = 22 * i + 6 + 4 * a + g
                        pe.wait_ge(f_ev, free(m))
                        for j in range(J4):
                            ins = nc.tensor.transpose(ps[0:AT, g % 2, j * AT:(j + 1) * AT], Pr[0:AT, 4 * g + j, :],
                                                      ident[0:AT, 0:AT])
                        ins.then_inc(f_pj, 1)
                    pe.wait_ge(f_lo, n + 1)
                    for g in range(G4):
                        pe.wait_ge(f_ev, ready(22 * i + 6 + 4 * a + g))
                        for j in range(J4):
                            c0 = ((g % 2) * J4 + j) * (HD + 1)
                            ins = nc.tensor.matmul(ps[0:AT, 6 + g // 2, c0:c0 + HD + 1], PT[0:AT, 4 * g + j, :],
                                                   Fm["V1"][0:AT, a, g, :], start=True, stop=True)
                    ins.then_inc(f_av, 1)
                    pe.wait_ge(f_yn, n + 1)
                    for b in range(KD):
                        ins = nc.tensor.transpose(ps[:, 6, b * AT:(b + 1) * AT],
                                                  Fm["yo"][0:AT].rearrange("p h d -> p (h d)")[:, b * P:(b + 1) * P],
                                                  ident[0:AT, 0:AT])
                    ins.then_inc(f_yt, 1)
            pe.wait_ge(wa_lo, UNITS + 1)
            def out_rows(k, p, half):
                pe.wait_ge(w_h, free(k))
                for b in range(KD):
                    ins = split3(ps[:, p, :], [nT[x][:, b, ds(k * P, P)] for x in range(2)],
                                 [wo[x][:, b, :] for x in range(2)], b == 0, b == KD - 1)
                ins.then_inc(w_mm, 1)

            def q_turn(k, p, half):
                pe.wait_ge(w_q, k + 1)
                pe.wait_ge(w_ev, free(k))
                for b in range(KD):
                    ins = nc.tensor.transpose(ps[:, 2 + p, 64 * b:64 * b + 64].bitcast(BF16), Gm["qi"][:, p, b * P:(b + 1) * P],
                                              identb[:])
                ins.then_inc(w_tr, 1)

            pipeline(pe, NT, [(0, out_rows)])
            pipeline(pe, NT, [(0, q_turn)])

            def gate_up(k, fs):
                for f in fs:
                    pe.wait_ge(x_t, free(4 * k + f))
                    for q in range(2):
                        for b in range(KD):
                            ins = nc.tensor.matmul(ps[:, 2 * (f % 2) + q, :], Gm["qT"][:, b, ds(k * P, P)],
                                                   qw[:, q, b * FF + f * 512:b * FF + (f + 1) * 512],
                                                   start=b == 0, stop=b == KD - 1)
                    ins.then_inc(x_gu, 1)

            def f_turn(k, p, half):
                pe.wait_ge(x_q, k + 1)
                for j in range(2):
                    pe.wait_ge(x_ev, 2 * k + j + 1)
                    for b in range(8):
                        ins = nc.tensor.transpose(ps[:, 4 + j, 64 * b:64 * b + 64].bitcast(BF16),
                                                  fi[:, (8 * j + b) * P:(8 * j + b + 1) * P], identb[:])
                    ins.then_inc(x_tr, 1)

            def down(k, p, half):
                pe.wait_ge(x_og, free(k))
                pe.wait_ge(x_ev, 2 * k + 4)
                for b in range(FF // P):
                    ins = nc.tensor.matmul(ps[:, 6 + p, :], fT[:, p, b, :], qw[:, 2, b * D:(b + 1) * D],
                                           start=b == 0, stop=b == FF // P - 1)
                ins.then_inc(x_dn, 1)

            pe.wait_ge(t_done, 1)
            pe.wait_ge(w_ev, NT + 2)
            pipeline(pe, NT, [(0, lambda k, p, half: gate_up(k, (0, 1))), (2, down),
                              (0, lambda k, p, half: gate_up(k, (2, 3))), (1, f_turn)])

        @block.vector
        def _(dve):
            V = nc.vector
            dve.sem_inc(ln_lo, 2)
            dve.sem_inc(a_lo, 2)
            dve.sem_inc(a_h, 2)
            dve.sem_inc(b_lo, 2)
            dve.sem_inc(c_h, 2)
            dve.sem_inc(q_sum, 1)
            dve.sem_inc(f_s, 1)
            dve.sem_inc(f_lo, 1)
            dve.sem_inc(w_h, 2)
            dve.sem_inc(x_t, 2)
            dve.sem_inc(x_og, 2)
            dve.sem_inc(b_acc, 2)
            dve.sem_inc(m_acc, 4)
            dve.wait_ge(ones_set, 2)
            order = Order(dve, dve_o)

            def split_lo(dst, src, hi, sem_out):
                V.scalar_tensor_tensor(dst, src, WS, hi, ALU.mult, ALU.subtract).then_inc(sem_out, 1)

            def unit_a_lo(n):
                dve.wait_ge(wa_hi, n + 1)
                split_lo(wa[1][:].rearrange("p a b -> p (a b)"), st_a[:], wa[0][:].rearrange("p a b -> p (a b)"), wa_lo)

            def unit_b_lo(n):
                dve.wait_ge(wb_hi, n + 1)
                split_lo(wb[1][:].rearrange("p a b -> p (a b)"), st_b[:], wb[0][:].rearrange("p a b -> p (a b)"), wb_lo)

            def ask(src, scale, eps, dst, sem_out):
                V.tensor_scalar(dst, src, scale, eps, ALU.mult, ALU.add).then_inc(sem_out, 1)

            def row(k):
                return h[:, ds(k, 1), :].rearrange("p a b -> p (a b)")

            def ln_stats(use, asked, done):
                dve.sem_inc(passed, 1)
                for k in range(NT):
                    ins = V.bn_stats(bst12[:, k, :], h[:, k, :])
                order(ins)
                dve.sem_inc(passed, 1)
                for k in range(NT):
                    ins = V.bn_aggr(mv12[:, k, :], bst12[:, k, :])
                order(ins)
                ask(mv12[:, :, 1], 1.0, 1e-5, rt_in[:], asked)
                dve.wait_ge(done, 1)
                V.scalar_tensor_tensor(nb12[:], mv12[:, :, 0], -1.0, rt_out[:], ALU.mult, ALU.mult).then_inc(ln_st, 1)

            def ln_low(n, k, bank):
                dve.wait_ge(ln_hi, n + 1)
                V.tensor_tensor(nT[1][:, :, ds(k * P, P)], ps[:, bank, :].rearrange("p (a b) -> p a b", a=KD),
                                nT[0][:, :, ds(k * P, P)], ALU.subtract).then_inc(ln_lo, 1)

            dve.wait_ge(rows_in, 80)
            V.tensor_scalar(A["g1s"][:], A["g1"][:], WS, None, ALU.mult).then_inc(a_g1, 1)
            for b in range(KI):
                ins = V.tensor_scalar(A["b1b"][:, b, :], ones[:], A["b1"][:, b:b + 1], None, ALU.mult)
            ins.then_inc(a_b1, 1)
            for j in range(2):
                dve.wait_ge(wt_hi, j + 1)
                for b in range(4):
                    ins = V.scalar_tensor_tensor(A["wt_lo"][:, 4 * j + b, :], st_a[:, b * D:(b + 1) * D],
                                                 A["g1s"][:, 4 * j + b:4 * j + b + 1], A["wt_hi"][:, 4 * j + b, :],
                                                 ALU.mult, ALU.subtract)
                ins.then_inc(wt_lo, 1)
            dve.wait_ge(gw_hi, 1)
            split_lo(gw[1][:], gst[:], gw[0][:], gw_lo)
            dve.wait_ge(a_tb, 2)
            order(V.tensor_tensor(A["tb"][:], A["tb"][:], ps[:, 7, :], ALU.add))

            def moments(rows, kind, p, n, sem_out, eps):
                s = 2 * kind + p
                dve.sem_inc(passed, 1)
                for j in range(n):
                    ins = V.bn_stats(A["bst"][:, s, j, :], rows[:, j * 512:(j + 1) * 512] if n > 1 else rows)
                order(ins)
                dve.sem_inc(passed, 1)
                order(V.bn_aggr(A["mv"][:, s, :], A["bst"][:, s, 0:n, :].rearrange("p a b -> p (a b)")))
                ask(A["mv"][:, s, 1:2], 1.0, eps, rt_in[:, s:s + 1], sem_out)

            def shift(kind, done, sem_out):
                def step(k, p, half):
                    s = 2 * kind + p
                    dve.wait_ge(done, k + 1)
                    V.scalar_tensor_tensor(A["nb"][:, s:s + 1], A["mv"][:, s, 0:1], -1.0, rt_out[:, s:s + 1], ALU.mult,
                                           ALU.mult).then_inc(sem_out, 1)
                return step

            def x_stats(k, p, half):
                dve.wait_ge(x_in[p], 16 * (half + 1))
                moments(A["xt"][:, p, :], 0, p, 2, rx_ask, 1e-6)

            def x_low(k, p, half):
                for j in range(2):
                    dve.wait_ge(a_hi, 2 * k + j + 1)
                    V.tensor_tensor(A["xT_lo"][:, p, 4 * j:4 * j + 4, :], ps[:, j, :].rearrange("p (a b) -> p a b", a=4),
                                    A["xT_hi"][:, p, 4 * j:4 * j + 4, :], ALU.subtract).then_inc(a_lo, 1)

            def z_stats(k, p, half):
                dve.wait_ge(a_mm, ready(k))
                z = A["z"][:, p, :]
                order(V.scalar_tensor_tensor(z, ps[:, 2 + p, :], 1.0 / WS, A["tb"][:], ALU.mult, ALU.add))
                dve.sem_inc(a_h, 1)
                moments(z, 1, p, 1, rz_ask, 1e-6)

            def h_stats(k, p, half):
                dve.wait_ge(a_row, k + 1)
                moments(row(k), 2, p, 1, rh_ask, 1e-5)

            pipeline(dve, NT, [(3, z_stats), (0, x_stats), (3, shift(1, rz_done, a_sz)), (0, shift(0, rx_done, a_sx)),
                               (4, h_stats), (1, x_low), (4, shift(2, rh_done, ln_st)),
                               (5, lambda k, p, half: ln_low(k, k, 4 + p))], order, 7)
            unit_a_lo(0)
            unit_b_lo(0)
            dve.wait_ge(consts_in, 144)
            order(V.tensor_copy(identb[:], ident[:]))
            dve.wait_ge(g_mm, 1)
            lt = B["lt"]
            order(V.tensor_scalar(lt[0:AT, 0, :], ps[0:AT, 0, 0:128], 1.0 / WS, 6.906768, ALU.mult, ALU.add))
            V.scalar_tensor_tensor(lt[0:AT, 1, :], lt[0:AT, 0, :], -1.0, lt[0:AT, 0, :], ALU.mult, ALU.max).then_inc(g_mm, 1)
            dve.wait_ge(g_ln, 1)
            V.scalar_tensor_tensor(B["lg"][0:AT], lt[0:AT, 0, :].rearrange("p (a h) -> p h a", h=HEADS), 0.0,
                                   lt[0:AT, 1, :].rearrange("p (a h) -> p h a", h=HEADS), ALU.min,
                                   ALU.subtract).then_inc(g_lg, 1)
            dve.wait_ge(g_cum, 1)
            order(V.tensor_copy(B["LG"][0:AT].rearrange("p a b -> p (a b)"), ps[0:AT, 1, 0:128]))
            order(V.memset(B["v1"][:, :, DH:DH + 1], 1.0))
            order(V.memset(asum[:], 0.0))
            order(V.memset(big[:], 0.0))
            for blk in range(KD):
                ins = V.tensor_scalar(big[:, blk, :], big[:, blk, :], bcol[:, blk:blk + 1], None, ALU.add)
            order(ins)
            dve.sem_inc(g_done, 1)

            def accumulate(g, c):
                for blk in range(4):
                    dve.wait_ge(b_wc, 4 * g + blk + 1)
                    acc = big[:, blk, c * CW:(c + 1) * CW]
                    V.scalar_tensor_tensor(acc, ps[:, 6 + blk % 2, 0:CW], 1.0 / (WS * AS), acc, ALU.mult,
                                           ALU.add).then_inc(b_acc, 1)

            with dve.Fori(0, HEADS) as i:
                order.enter(i, 2 + CH * 5 + 1)
                order(V.tensor_copy(B["lgh"][0:AT], B["lg"][0:AT, ds(i, 1), :].rearrange("p a b -> p (a b)")))
                order(V.tensor_copy(B["LGh"][0:AT], B["LG"][0:AT, ds(i, 1), :].rearrange("p a b -> p (a b)")))
                for c in range(CH):
                    g = CH * i + c
                    V.tensor_tensor(B["Dg"][0:AT], B["lgh"][0:AT, 4 * c:4 * c + 4].unsqueeze(2).broadcast_to([AT, 4, AT]),
                                    tri[0:AT].unsqueeze(1).broadcast_to([AT, 4, AT]), ALU.mult).then_inc(b_D, 1)
                    dve.wait_ge(b_ev, ready(5 * g + 3))
                    order(V.tensor_tensor(B["gt"][0:AT], B["gt"][0:AT],
                                          B["LGh"][0:AT, 4 * c:4 * c + 4].unsqueeze(2).broadcast_to([AT, 4, AT]), ALU.subtract))
                    V.tensor_tensor(B["gt"][0:AT], B["gt"][0:AT], mask[0:AT].unsqueeze(1).broadcast_to([AT, 4, AT]),
                                    ALU.add).then_inc(b_g, 1)
                    dve.wait_ge(b_E, g + 1)
                    for j in range(2):
                        dve.wait_ge(b_sq, 2 * g + j + 1)
                        V.tensor_tensor(B["a"][0:AT, j], B["sq"][0:AT, j],
                                        B["E"][0:AT, 2 * j:2 * j + 2].unsqueeze(2).broadcast_to([AT, 2, REP, AT]),
                                        ALU.mult).then_inc(b_a, 1)
                    if c:
                        accumulate(g - 1, c - 1)
                    for j in range(2):
                        dve.wait_ge(b_av, 2 * g + j + 1)
                        y = ps[0:AT, 4 + 2 * j:6 + 2 * j, 0:REP * (DH + 1)].rearrange("p a (r d) -> p a r d", r=REP)
                        order(V.tensor_scalar(B["rn"][0:AT, j], y[:, :, :, DH], 1e-6, None, ALU.add))
                        order(V.reciprocal(B["rn"][0:AT, j], B["rn"][0:AT, j]))
                        V.tensor_tensor(B["yn"][0:AT, j], y[:, :, :, 0:DH],
                                        B["rn"][0:AT, j].unsqueeze(3).broadcast_to([AT, 2, REP, DH]), ALU.mult).then_inc(b_yn, 1)
                    for j in range(2):
                        dve.wait_ge(b_hi, 2 * g + j + 1)
                        V.tensor_tensor(B["yT_lo"][:, :, j * 2 * AT:(j + 1) * 2 * AT],
                                        ps[:, 2 + j, 0:CW].rearrange("p (r t) -> p r t", r=REP),
                                        B["yT_hi"][:, :, j * 2 * AT:(j + 1) * 2 * AT], ALU.subtract).then_inc(b_lo, 1)
                dve.wait_ge(q_abs, 3 * i + 4)
                order(V.tensor_tensor(asum[:], asum[:], apart[:], ALU.add))
                dve.sem_inc(q_sum, 1)
                unit_a_lo(i + 1)
                accumulate(g, c)
                unit_b_lo(i + 1)
                order.leave(HEADS)
            dve.wait_ge(q_tot, 1)
            order(V.tensor_scalar(wdq[:], ps[:, 0, 0:3], 1.0 / (D * FF), 1e-5, ALU.mult, ALU.max))
            V.reciprocal(wsc[:], wdq[:]).then_inc(q_scl, 1)
            def c_add(k, p, half):
                dve.wait_ge(c_tr, ready(k))
                V.tensor_tensor(row(k), ps[:, 2 + p, :], row(k), ALU.add).then_inc(c_h, 1)

            pipeline(dve, NT, [(0, c_add)])
            dve.wait_ge(c_h, NT + 2)
            ln_stats(1, rc_ask, rc_done)
            pipeline(dve, NT, [(0, lambda k, p, half: ln_low(NT + k, k, 4 + p))])

            rt = B["rt"]
            E1, sc, sbz, gt_, eq, ca, cb, sel = [rt[:, x] for x in range(8)]
            dve.wait_ge(r_exp, 1)
            order(V.tensor_scalar(sc, E1, 1.0, None, ALU.add))
            order(V.reciprocal(sc, sc))
            order(V.tensor_tensor(sbz, sc, ebias[:].unsqueeze(1).broadcast_to([P, NT, EXP]), ALU.add))
            for k in range(NT):
                ins = V.max(B["m8"][:, k, :], sbz[:, k, :])
            order(ins)
            thr = B["m8"][:, :, TOPK - 1:TOPK].broadcast_to([P, NT, EXP])
            V.tensor_tensor(gt_, sbz, thr, ALU.is_gt)
            order(V.tensor_tensor(eq, sbz, thr, ALU.is_equal))
            V.tensor_reduce(B["need"][:], gt_, AX.X, ALU.add)
            src, dst = eq, ca
            for s in (1, 2, 4, 8):
                V.tensor_copy(dst[:, :, 0:s], src[:, :, 0:s])
                order(V.tensor_tensor(dst[:, :, s:], src[:, :, s:], src[:, :, 0:EXP - s], ALU.add))
                src, dst = dst, (cb if dst is ca else ca)
            order(V.tensor_tensor(src, src, B["need"][:].unsqueeze(2).broadcast_to([P, NT, EXP]), ALU.add))
            order(V.scalar_tensor_tensor(src, src, TOPK + 0.5, eq, ALU.is_lt, ALU.mult))
            order(V.tensor_tensor(sel, src, gt_, ALU.add))
            order(V.tensor_tensor(sel, sel, sc, ALU.mult))
            order(V.tensor_reduce(B["need"][:], sel, AX.X, ALU.add))
            order(V.reciprocal(B["need"][:], B["need"][:]))
            V.memset(cw[:, EXP, :], 1.0)
            order(V.tensor_tensor(cw[:, 0:EXP, :].rearrange("p e k -> p k e"), sel,
                                  B["need"][:].unsqueeze(2).broadcast_to([P, NT, EXP]), ALU.mult))
            dve.sem_inc(r_done, 1)
            for x in range(2):
                V.memset(hact[x][:, :, T:TP], 0.0).then_inc(m_pad, 1)
            dve.sem_inc(m_t, 2)
            with dve.Fori(0, EXP + 1) as e:
                order.enter(e, 1)
                dve.wait_ge(m_acc, 4 + NT * e)
                order(V.tensor_scalar(cwe[:], cw[:, ds(e, 1), :].rearrange("p a b -> p (a b)"), 1.0 / (WS * AS), None, ALU.mult))
                for r0 in range(8):
                    r, c, ib = 8 * e + r0, r0 // 2, r0 % 2
                    dve.wait_ge(m_sg, r + 1)
                    V.scalar_tensor_tensor(Dm["ht"][:, r0 % 2, :], ps[:, 2 * (r0 % 2) + 1, 0:CW], AS / WS,
                                           Dm["sg"][:, r0 % 2, :], ALU.mult, ALU.mult).then_inc(m_t, 1)
                    dve.wait_ge(m_hi, r + 1)
                    V.tensor_tensor(hact[1][:, ib, c * CW:(c + 1) * CW], Dm["ht"][:, r0 % 2, :],
                                    hact[0][:, ib, c * CW:(c + 1) * CW], ALU.subtract).then_inc(m_lo, 1)
                unit_a_lo(HEADS + e + 1)
                for k in range(NT):
                    dve.wait_ge(m_dn, NT * e + k + 1)
                    V.scalar_tensor_tensor(h[:, k, :], ps[:, 4 + k % 4, :], cwe[:, k:k + 1], h[:, k, :], ALU.mult,
                                           ALU.add).then_inc(m_acc, 1)
                unit_b_lo(HEADS + e + 1)
                order.leave(EXP + 1)
            dve.wait_ge(wa_hi, UNITS + 1)
            split_lo(wo[1][:].rearrange("p a b -> p (a b)"), st_a[:], wo[0][:].rearrange("p a b -> p (a b)"), wa_lo)
            dve.wait_ge(m_acc, 4 + NT * (EXP + 1))
            ln_stats(2, re_ask, re_done)
            pipeline(dve, NT, [(0, lambda k, p, half: ln_low(2 * NT + k, k, 4 + p))])
            order(V.memset(Fm["V1"][:, :, :, HD:HD + 1], 1.0))
            with dve.Fori(0, CH) as i:
                order.enter(i, 5 * 2 + 4 * 3 + 1)
                order(V.tensor_copy(Fm["nTc_hi"][:], nT[0][:, :, ds(i * CW, CW)]))
                V.tensor_copy(Fm["nTc_lo"][:], nT[1][:, :, ds(i * CW, CW)]).then_inc(f_x, 1)
                for j in range(5):
                    dve.wait_ge(f_ev, ready(22 * i + j))
                    dve.sem_inc(passed, 1)
                    qsh = Fm[("qsh", "qcs")[j % 2]]
                    order(V.stream_shuffle(qsh[:], Fm["qraw"][:, j, :], [(x + HD // 2) % HD for x in range(HD)]))
                    order(V.tensor_tensor(qsh[:], qsh[:], sinT[:], ALU.mult))
                    dve.wait_ge(f_cos, 5 * i + j + 1)
                    ins = V.tensor_tensor(Fm["qr"][:, j, :], Fm["qr"][:, j, :], qsh[:], ALU.add)
                ins.then_inc(f_rope, 1)

                def shifted(a):
                    n = 4 * i + a
                    dve.wait_ge(f_sc, n + 2)
                    if a:
                        dve.wait_ge(f_ex, n)
                    order(V.tensor_tensor(Sc[0:AT].rearrange("p (g j) s -> p g (j s)", g=G4).rearrange("p g (j s) -> p g j s", j=J4),
                                          ps[0:AT, 2:6, 0:CW].rearrange("p g (j s) -> p g j s", j=J4),
                                          maskT[0:AT].unsqueeze(1).unsqueeze(1).broadcast_to([AT, G4, J4, AT]), ALU.add))
                    order(V.tensor_reduce(Fm["mx"][0:AT], Sc[0:AT], AX.X, ALU.max))
                    V.tensor_tensor(Sc[0:AT], Sc[0:AT], Fm["mx"][0:AT].unsqueeze(2).broadcast_to([AT, 16, AT]),
                                    ALU.subtract).then_inc(f_s, 1)

                shifted(0)
                for a in range(4):
                    n = 4 * i + a
                    if a < 3:
                        shifted(a + 1)
                    dve.wait_ge(f_av, n + 1)
                    y = ps[0:AT, 6:8, 0:8 * (HD + 1)].rearrange("p b (x d) -> p b x d", d=HD + 1)
                    order(V.reciprocal(Fm["rd"][0:AT].rearrange("p (b x) -> p b x", b=2), y[:, :, :, HD]))
                    V.tensor_tensor(Fm["yo"][0:AT].rearrange("p (b x) d -> p b x d", b=2), y[:, :, :, 0:HD],
                                    Fm["rd"][0:AT].rearrange("p (b x) -> p b x", b=2).unsqueeze(3).broadcast_to([AT, 2, 8, HD]),
                                    ALU.mult).then_inc(f_yn, 1)
                    dve.wait_ge(f_hi, n + 1)
                    cols = ds(i * CW + a * AT, AT)
                    V.tensor_tensor(nT[1][:, :, cols], ps[:, 6, 0:CW].rearrange("p (b t) -> p b t", b=KD),
                                    nT[0][:, :, cols], ALU.subtract).then_inc(f_lo, 1)
                order.leave(CH)

            def w_add(k, p, half):
                dve.wait_ge(w_mm, k + 1)
                V.scalar_tensor_tensor(row(k), ps[:, p, :], 1.0 / (WS * AS), row(k), ALU.mult, ALU.add).then_inc(w_h, 1)

            pipeline(dve, NT, [(0, w_add)])
            dve.wait_ge(w_h, NT + 2)
            ln_stats(3, rf_ask, rf_done)

            def largest(k, p, half):
                dve.wait_ge(w_n, k + 1)
                V.tensor_reduce(Gm["am"][:, ds(k, 1)], xn[:, ds(k, 1), :].rearrange("p a b -> p (a b)"), AX.X, ALU.max,
                                apply_absolute_value=True).then_inc(w_am, 1)

            pipeline(dve, NT, [(0, largest)])
            dve.wait_ge(w_am, NT)

            def scales(am, root, sm):
                order(V.tensor_tensor(sm[0], am, root, ALU.mult))
                order(V.tensor_scalar(sm[0], sm[0], 1e-5, None, ALU.max))
                order(V.reciprocal(sm[1], sm[0]))
                order(V.scalar_tensor_tensor(sm[2], sm[1], 127.0, root, ALU.mult, ALU.mult))

            dve.wait_ge(w_sq, NT + 1)
            ask(Gm["ssq"][:], 1.0 / D, 1e-6, rq_in[:], rq_ask)
            dve.wait_ge(rq_done, 1)
            sm = [Gm["sm"][:, x, :] for x in range(3)]
            scales(Gm["am"][:], rq_out[:], sm)
            order(V.tensor_scalar(Gm["dq"][:], sm[0], 1.0 / 127.0, None, ALU.mult))

            def quantize(k, p, half):
                src = xn[:, ds(k, 1), :].rearrange("p a b -> p (a b)")
                V.tensor_scalar(src, src, Gm["sm"][:, 2, ds(k, 1)], MAGIC, ALU.mult, ALU.add).then_inc(w_r, 1)

            def integers(k, p, half):
                dve.wait_ge(w_r, k + 1)
                dve.wait_ge(w_ev, free(k))
                V.tensor_scalar(Gm["qi"][:, p, :], xn[:, ds(k, 1), :].rearrange("p a b -> p (a b)"), MAGIC, 127.0,
                                ALU.subtract, ALU.min).then_inc(w_q, 1)

            pipeline(dve, NT, [(0, quantize), (1, integers)])

            def dequantizers(k, p, half):
                order(V.tensor_copy(Gm["dqc"][:], Gm["dq"][:, ds(k, 1)]))
                V.tensor_scalar(Gm["dqe"][:, p, :], wdq[:, 0:2], Gm["dqc"][:, 0:1], None, ALU.mult).then_inc(x_dq, 1)
                dve.wait_ge(x_dq, k + 1)

            def product(f):
                def step(k, p, half):
                    dve.wait_ge(x_sg, 4 * k + f + 1)
                    V.scalar_tensor_tensor(ff[:, p, f * 512:(f + 1) * 512], ps[:, 2 * (f % 2) + 1, :],
                                           Gm["dqe"][:, p, 1:2], sgl[:, f % 2, :], ALU.mult, ALU.mult).then_inc(x_t, 1)
                return step

            def chunk_max(f):
                def step(k, p, half):
                    dve.wait_ge(x_t, ready(4 * k + f))
                    V.tensor_reduce(Gm["amf"][:, p, f:f + 1], ff[:, p, f * 512:(f + 1) * 512], AX.X, ALU.max,
                                    apply_absolute_value=True).then_inc(x_am, 1)
                return step

            def ask_root(k, p, half):
                dve.wait_ge(x_am, 4 * k + 4)
                order(V.tensor_reduce(Gm["amg"][:, p:p + 1], Gm["amf"][:, p, :], AX.X, ALU.max))
                dve.wait_ge(x_sq, 4 * k + 5)
                order(V.tensor_reduce(Gm["ssg"][:, p:p + 1], Gm["ssf"][:, p, :], AX.X, ALU.add))
                ask(Gm["ssg"][:, p:p + 1], 1.0 / FF, 1e-6, rq_in[:, p:p + 1], rg_ask)

            def rescale(k, p, half):
                dve.wait_ge(rg_done, k + 1)
                g = [Gm["smg"][:, x, p:p + 1] for x in range(3)]
                scales(Gm["amg"][:, p:p + 1], rq_out[:, p:p + 1], g)
                order(V.tensor_scalar(Gm["dqd"][:, p:p + 1], g[0], wdq[:, 2:3], 1.0 / 127.0, ALU.mult, ALU.mult))
                order(V.tensor_scalar(ff[:, p, :], ff[:, p, :], g[2], MAGIC, ALU.mult, ALU.add))

            def f_integers(k, p, half):
                dve.wait_ge(x_tr, 2 * k + 2)
                V.tensor_scalar(fi[:], ff[:, p, :], MAGIC, 127.0, ALU.subtract, ALU.min).then_inc(x_q, 1)

            def finish(k, p, half):
                dve.wait_ge(x_dn, ready(k))
                dve.wait_ge(out_st[p], 16 * (half + 1))
                V.scalar_tensor_tensor(og[:, p, :], ps[:, 6 + p, :], Gm["dqd"][:, p:p + 1], row(k), ALU.mult,
                                       ALU.add).then_inc(x_og, 1)

            pipeline(dve, NT, [(0, dequantizers), (0, product(0)), (0, product(1)), (1, rescale), (1, f_integers),
                               (0, product(2)), (0, chunk_max(0)), (0, chunk_max(1)), (0, product(3)),
                               (0, chunk_max(2)), (0, chunk_max(3)), (0, ask_root), (2, finish)], order, 1 + 2 + 4 + 2)


_CONSTS = {}


def constants():
    pos = np.arange(AT) % SL
    seq = np.arange(AT) // SL
    same = seq[:, None] == seq[None, :]
    causal = same & (pos[:, None] <= pos[None, :])
    tri = causal.astype(np.float32)
    mask = np.where(causal, 0.0, NEG).astype(np.float32)
    inv = np.power(np.float32(10000.0), np.float32(-2.0) * np.arange(HD // 2, dtype=np.float32) / np.float32(HD))
    ang = np.arange(SL, dtype=np.float32)[:, None] * inv[None, :].astype(np.float32)
    cos = np.tile(np.cos(ang), (1, 2)).astype(np.float32)
    sin = np.tile(np.sin(ang), (1, 2)).astype(np.float32)
    sin[:, :HD // 2] *= -1.0
    lane = np.arange(P) % HD
    p = np.arange(CW) % SL
    return dict(ident=np.eye(P, dtype=np.float32), tri=tri, mask=mask, maskT=np.ascontiguousarray(mask.T),
                cos=np.ascontiguousarray(cos[p][:, lane].T), sin=np.ascontiguousarray(sin[p][:, lane].T))


def kernel(**inp):
    import concourse.bacc as bacc
    from concourse.bass_utils import run_bass_kernel_spmd

    f = {k: np.asarray(v) for k, v in inp.items()}

    def kmaj(w):
        return w.reshape(w.shape[0] // P, P, w.shape[1]).transpose(1, 0, 2)

    x = np.zeros((TP, DIN), np.float32)
    x[:T] = f["x"][:, :SL * 16].reshape(T, DIN)
    wt = kmaj(f["L0_tok_W"])
    wa = np.zeros((UNITS, P, KD, 512), np.float32)
    wb = np.zeros((UNITS, P, 1024), np.float32)
    q, k, v, c = (kmaj(f["L0_attn_W" + n]) for n in "qkvc")
    for n in range(HEADS):
        wa[n, :, :, 0:256] = q[:, :, 256 * n:256 * (n + 1)]
        wa[n, :, :, 256:384] = k[:, :, P * n:P * (n + 1)]
        wa[n, :, :, 384:512] = v[:, :, P * n:P * (n + 1)]
        wb[n] = c[:, 2 * n:2 * n + 2].reshape(P, 1024)
    for e in range(EXP + 1):
        g, u, d = ((f["L0_ffn_w_gate"][e], f["L0_ffn_w_up"][e], f["L0_ffn_w_down"][e]) if e < EXP else
                   (f["L0_ffn_sw_gate"], f["L0_ffn_sw_up"], f["L0_ffn_sw_down"]))
        wa[HEADS + e, :, :, 0:256] = kmaj(g.T)
        wa[HEADS + e, :, :, 256:512] = kmaj(u.T)
        wb[HEADS + e] = kmaj(d.T).reshape(P, 1024)
    wq1 = f["L1_attn_Wq"].reshape(D, G4, J4, HD).transpose(0, 2, 1, 3).reshape(D, D)
    wa[UNITS - 1] = kmaj(wq1)
    wb[UNITS - 1] = np.concatenate([kmaj(f["L1_attn_Wk"]), kmaj(f["L1_attn_Wv"])], axis=2).reshape(P, 1024)
    arrays = {
        "x": x.reshape(NT, P, DIN), "wt": wt.transpose(1, 0, 2).reshape(2, 4, P, D).transpose(0, 2, 1, 3).reshape(2, P, 2048),
        "g1": f["L0_tok_g1"].reshape(KI, P).T, "b1": f["L0_tok_b1"].reshape(KI, P).T, "tb": f["L0_tok_b"], "g2": f["L0_tok_g2"], "b2": f["L0_tok_b2"],
        "bcol": f["L0_attn_bc"].reshape(KD, P).T, "ebias": f["L0_ffn_expert_bias"],
        "gst": np.concatenate([kmaj(f["L0_attn_Wg"]), kmaj(f["L0_ffn_gate_w"].T)], axis=2),
        "wa": wa.reshape(UNITS, P, 2048), "wb": wb,
        "wo": kmaj(f["L1_attn_Wo"]).reshape(P, 2048),
        "ffq": np.stack([kmaj(f["L1_ffn_w_gate"].T).reshape(P, 8, 1024), kmaj(f["L1_ffn_w_up"].T).reshape(P, 8, 1024),
                         kmaj(f["L1_ffn_w_down"].T).reshape(P, 8, 1024)]).transpose(0, 2, 1, 3),
    }
    arrays.update(constants())
    nc = bacc.Bacc("TRN2", target_bir_lowering=False, num_devices=1)
    t = {}
    for name in list(arrays):
        a = arrays.pop(name)
        a = np.ascontiguousarray(a)
        arrays[f"in_{name}"] = a
        t[name] = nc.dram_tensor(f"in_{name}", a.shape, mybir.dt.from_np(a.dtype), kind="ExternalInput").ap()
    out = nc.dram_tensor("out", (T, D), F32, kind="ExternalOutput").ap()
    build(nc, t, out)
    r = run_bass_kernel_spmd(nc, [arrays], core_ids=[0])
    return np.asarray(r.results[0]["out"]).reshape(SEQS, SL, D)
```

```python
from contextlib import ExitStack

import numpy as np

import concourse.bass as bass
from concourse import mybir

P = 128
SEQS, SL = 64, 23
T = SEQS * SL
NT = (T + P - 1) // P
TP = NT * P
AT = 4 * SL
CW = 4 * AT
CH = T // CW
DIN, D = 1024, 512
KI, KD = DIN // P, D // P
HEADS, REP, DH = 8, 2, 128
EXP = 16
FI = 256
TOPK = 4
G4, J4, HD = 4, 4, 32
FF = 2048
NF = FF // 512
EARLY = 8
UNITS = HEADS + EXP + 1 + 1
WS = 256.0
GATE_OFFSET = 6.906768
AS = 16.0
MAGIC = 12582912.0
NEG = -1.0e30

F32 = mybir.dt.float32
F16 = mybir.dt.float16
BF16 = mybir.dt.bfloat16
ALU = mybir.AluOpType
ACT = mybir.ActivationFunctionType
AX = mybir.AxisListType
ds = bass.ds


def free(n):
    return n + 1


def ready(n):
    return n + 3


class Order:

    def __init__(self, eng, sem):
        self.eng, self.sem, self.at, self.n = eng, sem, 0, 0

    def __call__(self, ins):
        self.n += 1
        ins.then_inc(self.sem, 1)
        self.eng.wait_ge(self.sem, self.at + self.n)

    def enter(self, i, per):
        self.base, self.per = self.at + self.n, per
        self.at, self.n = self.base + i * per, 0

    def leave(self, count):
        assert self.n == self.per, ("ordered instructions of the loop body", self.n, self.per)
        self.at, self.n = self.base + count * self.per, 0


def pipeline(eng, n, steps, order=None, ordered=0, turns=2, after=None):
    lags = max(lag for lag, _ in steps)
    first = -(-lags // turns) * turns

    def turn(t):
        for lag, step in steps:
            if 0 <= t - lag < n:
                step(t - lag, (t - lag) % turns, (t - lag) // turns)

    for t in range(first):
        turn(t)
        if after and t in after:
            after[t]()
    with eng.Fori(0, (n - first) // turns) as i:
        if order:
            order.enter(i, turns * ordered)
        for u in range(turns):
            for lag, step in steps:
                c = first + u - lag
                step(turns * i + c, c % turns, i + c // turns)
        if order:
            order.leave((n - first) // turns)
    for t in range(n, n + lags):
        turn(t)
        if after and t in after:
            after[t]()


def build(nc, t, out):
    ctx = ExitStack()
    with ctx:
        def sb(name, shape, dt=F32):
            return ctx.enter_context(nc.sbuf_tensor(name, shape, dt))

        def sem(name):
            return ctx.enter_context(nc.semaphore(name))

        h = sb("h", [P, NT, D])
        nT = [sb(f"nT_{x}", [P, KD, TP], F16) for x in ("hi", "lo")]
        st_a = sb("st_a", [P, 2048])
        st_b = sb("st_b", [P, 1024])
        wa = [sb(f"wa_{x}", [P, 4, 512], F16) for x in ("hi", "lo")]
        wb = [sb(f"wb_{x}", [P, 2, 512], F16) for x in ("hi", "lo")]
        wo = [sb(f"wo_{x}", [P, KD, D], F16) for x in ("hi", "lo")]
        ident = sb("ident", [P, P])
        identb = sb("identb", [P, P], BF16)
        ones = sb("ones", [P, P])
        tri = sb("tri", [P, AT])
        mask = sb("mask", [P, AT])
        maskT = sb("maskT", [P, AT])
        cosT = sb("cosT", [P, CW])
        sinT = sb("sinT", [P, CW])
        bcol = sb("bcol", [P, KD])
        ebias = sb("ebias", [P, EXP])
        gst = sb("gst", [P, KD, HEADS + EXP])
        gw = [sb(f"gw_{x}", [P, KD, HEADS + EXP], F16) for x in ("hi", "lo")]
        rt_in = sb("rt_in", [P, NT])
        rt_out = sb("rt_out", [P, NT])
        rq_in = sb("rq_in", [P, NT])
        rq_out = sb("rq_out", [P, NT])
        neg_half = sb("neg_half", [P, NT])
        bst12 = sb("bst12", [P, NT, 6])
        mv12 = sb("mv12", [P, NT, 2])
        nb12 = sb("nb12", [P, NT])
        nrm = sb("nrm", [P, 2, D])
        cw = sb("cw", [P, EXP + 1, NT])
        cwe = sb("cwe", [P, NT])
        asum = sb("asum", [P, 3])
        apart = sb("apart", [P, 3])
        wsc = sb("wsc", [P, 3])
        wdq = sb("wdq", [P, 3])
        wq_st = sb("wq_st", [P, 3, 1024])
        wt_st = [st_a[:], wq_st[:, 0:2, :].rearrange("p a b -> p (a b)")]
        big = sb("big", [P, KD, TP])
        hact = [big[:, x, :].bitcast(F16).rearrange("p (i t) -> p i t", i=2) for x in range(2)]
        Sc = [big[:].rearrange("p a b -> p (a b)")[:, x * 16 * AT:(x + 1) * 16 * AT]
              .rearrange("p (h s) -> p h s", h=16) for x in range(4)]
        PT = st_a[:, 0:16 * AT].rearrange("p (h s) -> p h s", h=16)
        flat = big[:].rearrange("p a b -> p (a b)")
        xn = flat.rearrange("p (k d) -> p k d", d=D)
        fT = nT[0][:].rearrange("p a b -> p (a b)")[:, 0:2 * FF].bitcast(BF16).rearrange("p (x a b) -> p x a b", x=2, b=P)
        qi = nT[1][:].rearrange("p a b -> p (a b)").bitcast(BF16).rearrange("p (k d) -> p k d", d=D)
        og, sgl = [st_a[:, x * 1024:(x + 1) * 1024].rearrange("p (a b) -> p a b", a=2) for x in range(2)]
        ps = ctx.enter_context(nc.psum_tensor("ps", [P, 8, 512], F32))

        def phase(specs):
            with ExitStack() as c:
                return {n: c.enter_context(nc.sbuf_tensor(n, s, d)) for n, s, d in specs}

        A = phase([("xt", [P, 2, DIN], F32), ("xh", [P, 2, DIN], F32), ("g1", [P, KI], F32), ("g1s", [P, KI], F32),
                   ("b1", [P, KI], F32), ("b1b", [P, KI, P], F32), ("bst", [P, 6, 2, 6], F32), ("mv", [P, 6, 2], F32),
                   ("nb", [P, 6], F32), ("tb", [P, D], F32), ("g2", [P, D], F32), ("b2", [P, D], F32),
                   ("wt_hi", [P, KI, D], F16), ("wt_lo", [P, KI, D], F16), ("z", [P, 2, D], F32),
                   ("xT_hi", [P, 2, KI, P], F16), ("xT_lo", [P, 2, KI, P], F16)])
        B = phase([("lg", [P, HEADS, 16], F32), ("LG", [P, HEADS, 16], F32), ("lt", [P, 3, 128], F32),
                   ("lgh", [P, 16], F32), ("LGh", [P, 16], F32),
                   ("qk", [P, 3, CW], F32), ("v1", [P, 4, DH + 1], F32), ("Dg", [P, 4, AT], F32),
                   ("gt", [P, 4, AT], F32), ("E", [P, 4, AT], F32), ("sq", [P, 2, 2, REP, AT], F32),
                   ("a", [P, 2, 2, REP, AT], F32), ("rn", [P, 2, 2, REP], F32),
                   ("yn", [P, 2, 2, REP, DH], F32), ("yT_hi", [P, REP, CW], F16),
                   ("yT_lo", [P, REP, CW], F16),
                   ("rt", [P, 8, NT, EXP], F32), ("m8", [P, NT, 8], F32),
                   ("need", [P, NT], F32)])
        with ExitStack() as c:
            DG = {n: c.enter_context(nc.sbuf_tensor(n, s, d)) for n, s, d in [
                ("qw", [P, 3, 8192], BF16)]}
            Dm = phase([("sg", [P, 2, CW], F32), ("ht", [P, 2, CW], F32)])
            Fm = phase([("qraw", [P, 5, CW], F32), ("qs", [P, 5, CW], F32), ("qr", [P, 5, CW], F32),
                        ("V1", [P, 4, G4 * HD], F32), ("mx", [P, 4, 16], F32), ("rd", [P, 4, 16], F32)])
            Gm = phase([("ff", [P, 2, FF], F32),
                        ("jk", [P, D], F32), ("ssq", [P, NT], F32), ("am", [P, NT], F32), ("sm", [P, 3, NT], F32),
                        ("qT", [P, KD, TP], BF16), ("dq", [P, NT], F32),
                        ("dqe", [P, 2, 2], F32), ("dqc", [P, 1], F32), ("dqd", [P, 2], F32), ("ssf", [P, 2, NF], F32),
                        ("amf", [P, 2, NF], F32), ("amg", [P, 2], F32), ("ssg", [P, 2], F32), ("smg", [P, 3, 2], F32)])
            qw, ff = DG["qw"], Gm["ff"]
            fi = nrm[:].rearrange("p a b -> p (a b)").bitcast(BF16)

        def sems(prefix, names):
            return [sem(f"{prefix}_{x}") for x in names.split()]

        consts_in, ident_in = sem("consts_in"), sem("ident_in")
        rows_in, g1_in, b1_in = sem("rows_in"), sem("g1_in"), sem("b1_in")
        ones_set, big_set = sem("ones_set"), sem("big_set")
        x_in = sems("x_in", "0 1")
        wt_in = sems("wt_in", "0 1")
        wt_hi, wt_lo = sem("wt_hi"), sem("wt_lo")
        gw_hi, gw_lo = sem("gw_hi"), sem("gw_lo")
        wa_in, wb_in = sem("wa_in"), sem("wb_in")
        wa_hi, wb_hi = sem("wa_hi"), sem("wb_hi")
        wa_lo, wb_lo = sem("wa_lo"), sem("wb_lo")
        passed = sem("passed")
        dve_o, pool_o = sem("dve_o"), sem("pool_o")
        rx_ask, rz_ask, rh_ask, rc_ask, re_ask, rf_ask, rq_ask, rg_ask = [sem(f"r{x}_ask") for x in "xzhcefqg"]
        rx_done, rz_done, rh_done, rc_done, re_done, rf_done, rq_done, rg_done = [sem(f"r{x}_done") for x in "xzhcefqg"]
        a_norm, a_tr, a_hi, a_lo = sems("a", "norm tr hi lo")
        a_sx, a_sz, a_zn, a_g1, a_b1, a_tb = sems("a", "sx sz zn g1 b1 tb")
        a_mm, a_h = sems("a", "mm h")
        a_zg, a_row = sems("a", "zg row")
        ln_bs, ln_st, ln_nr, ln_tr, ln_hi, ln_lo = sems("ln", "bs st nr tr hi lo")
        ln_sh = sem("ln_sh")
        g_mm, g_e1, g_ln, g_lg, g_cum = sems("gate", "mm exp ln log cum")
        b_pj, b_ev = sems("b", "pj ev")
        b_D, b_g, b_E = sems("b", "D g E")
        b_sc, b_sq, b_a = sems("b", "sc sq a")
        b_av, b_yn, b_yt = sems("b", "av yn yt")
        b_hi, b_lo = sems("b", "hi lo")
        acc_set, b_wc, b_acc = sem("acc_set"), sem("b_wc"), sem("b_acc")
        c_tr, c_h = sems("c", "tr h")
        q_in, q_abs, q_sum, q_tot, q_scl = sems("q", "in abs sum tot scl")
        t_in, t_done = sems("t_in", "0 1"), sem("t_done")
        r_mm, r_exp, r_done = sems("r", "mm exp done")
        m_gu, m_sg, m_t, m_hi, m_lo, m_dn, m_acc, m_pad = sems("m", "gu sg t hi lo dn acc pad")
        f_pj, f_ev, f_sh, f_cos, f_rope = sems("f", "pj ev sh cos rope")
        f_sc, f_md, f_mx, f_sb, f_ex, f_s = sems("f", "sc md mx sb ex s")
        f_pt, f_pe, f_av, f_hi, f_lo = sems("f", "pt pe av hi lo")
        w_mm, w_h, w_n, w_sq, w_am, w_r, w_q, w_tr, w_ev = sems("w", "mm h n sq am r q tr ev")
        x_gu, x_dq, x_sg, x_t, x_sq, x_am, x_q, x_tr, x_ev, x_dn, x_og = sems("x", "gu dq sg t sq am q tr ev dn og")
        out_st = sems("out_st", "0 1")

        block = ctx.enter_context(nc.Block())

        @block.sync
        def _(sp):
            def unit_a(n):
                sp.dma_start(st_a[:], t["wa"][n]).then_inc(wa_in, 16)

            def unit_b(n):
                sp.dma_start(st_b[:], t["wb"][n]).then_inc(wb_in, 16)

            for p in range(2):
                sp.sem_inc(out_st[p], 16)
            sp.dma_start(A["g1"][:], t["g1"]).then_inc(g1_in, 16)
            sp.dma_start(A["b1"][:], t["b1"]).then_inc(b1_in, 16)
            sp.dma_start(ident[:], t["ident"]).then_inc(ident_in, 16)
            for j in range(2):
                sp.dma_start(A["xt"][:, j, :], t["x"][j]).then_inc(x_in[j], 16)
                sp.dma_start(wt_st[j], t["wt"][j]).then_inc(wt_in[j], 16)
            for x in ("tb", "g2", "b2"):
                sp.dma_start(A[x][:], t[x].rearrange("(a n) -> a n", a=1).broadcast_to([P, D])).then_inc(rows_in, 16)
            for dst, src in ((cosT, "cos"), (sinT, "sin"), (gst, "gst"), (bcol, "bcol")):
                sp.dma_start(dst[:], t[src]).then_inc(consts_in, 16)
            sp.dma_start(tri[0:AT, :], t["tri"]).then_inc(consts_in, 16)
            sp.dma_start(mask[0:AT, :], t["mask"]).then_inc(consts_in, 16)
            sp.dma_start(maskT[0:AT, :], t["maskT"]).then_inc(consts_in, 16)
            sp.dma_start(ebias[:], t["ebias"].rearrange("(a n) -> a n", a=1).broadcast_to([P, EXP])).then_inc(consts_in, 16)
            unit_b(0)
            with sp.Fori(0, NT // 2 - 1) as i:
                for p in range(2):
                    sp.wait_ge(a_norm, 2 * i + p + 1)
                    sp.dma_start(A["xt"][:, p, :], t["x"][2 * i + p + 2]).then_inc(x_in[p], 16)
            sp.wait_ge(wt_lo, 2)
            sp.wait_ge(a_tb, 2)
            unit_a(0)
            with sp.Fori(0, HEADS) as i:
                sp.wait_ge(q_abs, 3 * i + 1)
                for m in range(3):
                    sp.dma_start(wq_st[:, m, :], t["ffq"][m, i]).then_inc(q_in, 16)
                sp.wait_ge(wa_lo, i + 1)
                unit_a(i + 1)
                sp.wait_ge(wb_lo, i + 1)
                unit_b(i + 1)
            with sp.Fori(HEADS, UNITS - 1) as i:
                sp.wait_ge(wa_lo, i + 1)
                unit_a(i + 1)
                sp.wait_ge(wb_lo, i + 1)
                unit_b(i + 1)
            sp.wait_ge(wa_lo, UNITS)
            sp.dma_start(st_a[:], t["wo"]).then_inc(wa_in, 16)
            with sp.Fori(0, NT // 2 - 1) as i:
                for p in range(2):
                    k = 2 * i + p
                    sp.wait_ge(x_og, k + 2)
                    sp.dma_start(out[ds(k * P, P), :], og[:, p, :]).then_inc(out_st[p], 16)
            for k in (NT - 2, NT - 1):
                rows = T - k * P if k == NT - 1 else P
                sp.wait_ge(x_og, k + 2)
                sp.dma_start(out[k * P:k * P + rows, :], og[0:rows, k % 2, :]).then_inc(out_st[k % 2], 16)
            for p in range(2):
                sp.wait_ge(out_st[p], 16 * (NT // 2) + 16)

        @block.gpsimd
        def _(pool):
            nc.gpsimd.memset(ones[:], 1.0).then_inc(ones_set, 1)
            nc.gpsimd.memset(neg_half[:], -0.5).then_inc(ones_set, 1)
            nc.gpsimd.memset(big[:], 0.0).then_inc(big_set, 1)
            pool.wait_ge(ones_set, 2)

            def root(ask, n, src, dst, done):
                pool.wait_ge(ask, n + 1)
                nc.gpsimd.tensor_tensor(dst, src, neg_half[:, 0:src.shape[1]], ALU.pow).then_inc(done, 1)

            def root_of(ask, kind, done):
                return lambda k, p, half: root(ask, k, rt_in[:, 2 * kind + p:2 * kind + p + 1],
                                               rt_out[:, 2 * kind + p:2 * kind + p + 1], done)

            def affine(k, p, half):
                pool.wait_ge(rows_in, 48)
                pool.wait_ge(a_zn, k + 1)
                nc.gpsimd.tensor_tensor(A["z"][:, p, :], A["z"][:, p, :], A["g2"][:], ALU.mult).then_inc(a_zg, 1)
                pool.wait_ge(a_zg, k + 1)
                pool.sem_inc(passed, 1)
                nc.gpsimd.tensor_tensor(h[:, ds(k, 1), :].rearrange("p a b -> p (a b)"), A["z"][:, p, :], A["b2"][:],
                                        ALU.add).then_inc(a_row, 1)

            pipeline(pool, NT, [(3, root_of(rz_ask, 1, rz_done)), (0, root_of(rx_ask, 0, rx_done)),
                                (4, root_of(rh_ask, 2, rh_done)), (3, affine)])
            for n, x in enumerate((slice(0, EARLY), slice(EARLY, NT))):
                root(rc_ask, n, rt_in[:, x], rt_out[:, x], rc_done)
            pool.wait_ge(q_scl, 1)
            pool.wait_ge(r_done, 1)
            porder = Order(pool, pool_o)
            for m in range(3):
                with pool.Fori(0, 4) as i:
                    porder.enter(i, 6)
                    for p in range(2):
                        pool.dma_start(wq_st[:, p, :], t["ffq"][m, 2 * i + p]).then_inc(t_in[p], 16)
                    for p in range(2):
                        pool.wait_ge(t_in[p], 16 * (4 * m + i + 1))
                        pool.sem_inc(passed, 1)
                        porder(nc.gpsimd.tensor_scalar(wq_st[:, 2, :], wq_st[:, p, :], wsc[:, m:m + 1], 0.5,
                                                       ALU.mult, ALU.is_gt))
                        pool.sem_inc(passed, 1)
                        porder(nc.gpsimd.tensor_scalar(wq_st[:, p, :], wq_st[:, p, :], wsc[:, m:m + 1], -0.5,
                                                       ALU.mult, ALU.is_lt))
                        pool.sem_inc(passed, 1)
                        porder(nc.gpsimd.tensor_tensor(qw[:, m, ds((2 * i + p) * 1024, 1024)], wq_st[:, 2, :],
                                                       wq_st[:, p, :], ALU.subtract))
                    porder.leave(4)
            pool.sem_inc(t_done, 1)
            for n, x in enumerate((slice(0, EARLY), slice(EARLY, NT))):
                root(re_ask, n, rt_in[:, x], rt_out[:, x], re_done)
            def cosine(c, j, first=False):
                pool.wait_ge(f_sh, 5 * c + j + 1)
                nc.gpsimd.tensor_tensor(Fm["qraw"][:, j, :], Fm["qraw"][:, j, :], cosT[:], ALU.mult).then_inc(f_cos, 1)
                if not first:
                    nc.gpsimd.tensor_tensor(Fm["qs"][:, j, :], Fm["qs"][:, j, :], sinT[:], ALU.mult).then_inc(f_cos, 1)

            def lower(n, a):
                pool.wait_ge(f_mx, n + 1)
                nc.gpsimd.tensor_tensor(Sc[a][0:AT], Sc[a][0:AT], Fm["mx"][0:AT, a].unsqueeze(2).broadcast_to([AT, 16, AT]),
                                        ALU.subtract).then_inc(f_sb, 1)

            for j in range(5):
                cosine(0, j, True)
            lower(0, 0)
            lower(1, 1)

            def rotary(i, last):
                for a in range(4):
                    for j in () if last else ((0, 1), (4,), (), ())[a]:
                        cosine(i + 1, j)
                    if not last or a < 2:
                        lower(4 * i + a + 2, (a + 2) % 4)
                    for j in () if last else ((2, 3), (), (), ())[a]:
                        cosine(i + 1, j)

            with pool.Fori(0, CH - 1) as i:
                rotary(i, False)
            rotary(CH - 1, True)
            pipeline(pool, NT, [(0, lambda k, p, half: root(rf_ask, k, rt_in[:, p:p + 1], rt_out[:, p:p + 1], rf_done))])
            for n, x in enumerate((slice(0, EARLY), slice(EARLY, NT))):
                root(rq_ask, n, rq_in[:, x], rq_out[:, x], rq_done)
            pipeline(pool, NT, [(0, lambda k, p, half: root(rg_ask, k, rq_in[:, p:p + 1], rq_out[:, p:p + 1], rg_done))])

        @block.scalar
        def _(act):
            act.sem_inc(ln_nr, 2)
            act.sem_inc(b_ev, 2)
            act.sem_inc(q_abs, 1)
            act.sem_inc(f_ev, 1)
            act.sem_inc(f_pe, 2)
            act.sem_inc(w_ev, 1)
            act.sem_inc(w_sq, 1)
            act.sem_inc(x_sq, 1)
            act.sem_inc(x_ev, 2)
            act.wait_ge(ones_set, 1)

            def unit_a_hi(n, used=None, count=0):
                act.wait_ge(wa_in, 16 * (n + 1))
                if used is not None:
                    act.wait_ge(used, count)
                nc.scalar.activation(wa[0][:].rearrange("p a b -> p (a b)"), st_a[:], ACT.Copy, scale=WS).then_inc(wa_hi, 1)

            def unit_b_hi(n, used=None, count=0):
                act.wait_ge(wb_in, 16 * (n + 1))
                if used is not None:
                    act.wait_ge(used, count)
                nc.scalar.activation(wb[0][:].rearrange("p a b -> p (a b)"), st_b[:], ACT.Copy, scale=WS).then_inc(wb_hi, 1)

            def ln_norm(use, k, p):
                act.wait_ge(ln_tr, free(use * NT + k))
                nc.scalar.activation(nrm[:, p, :], h[:, ds(k, 1), :].rearrange("p a b -> p (a b)"), ACT.Identity,
                                     bias=nb12[:, ds(k, 1)], scale=rt_out[:, ds(k, 1)]).then_inc(ln_nr, 1)

            def ln_high(n, k, bank):
                act.wait_ge(ln_tr, ready(n))
                nc.scalar.activation(nT[0][:, :, ds(k * P, P)],
                                     ps[:, bank, :].rearrange("p (a b) -> p a b", a=KD), ACT.Copy).then_inc(ln_hi, 1)

            def tok_weights():
                for j in range(2):
                    act.wait_ge(wt_in[j], 16)
                    act.wait_ge(a_g1, 1)
                    for b in range(4):
                        ins = nc.scalar.activation(A["wt_hi"][:, 4 * j + b, :], wt_st[j][:, b * D:(b + 1) * D],
                                                   ACT.Identity, scale=A["g1s"][:, 4 * j + b:4 * j + b + 1])
                    ins.then_inc(wt_hi, 1)
                act.wait_ge(consts_in, 128)
                nc.scalar.activation(gw[0][:], gst[:], ACT.Copy, scale=WS).then_inc(gw_hi, 1)

            def tok_high(k, p, half):
                act.wait_ge(a_mm, free(k))
                for j in range(2):
                    act.wait_ge(a_tr, 2 * k + j + 1)
                    nc.scalar.activation(A["xT_hi"][:, p, 4 * j:4 * j + 4, :],
                                         ps[:, j, :].rearrange("p (a b) -> p a b", a=4), ACT.Copy).then_inc(a_hi, 1)

            def x_norm(k, p, half):
                act.wait_ge(a_sx, k + 1)
                nc.scalar.activation(A["xh"][:, p, :], A["xt"][:, p, :], ACT.Identity, bias=A["nb"][:, p:p + 1],
                                     scale=rt_out[:, p:p + 1]).then_inc(a_norm, 1)

            def z_norm(k, p, half):
                act.wait_ge(a_sz, k + 1)
                nc.scalar.activation(A["z"][:, p, :], A["z"][:, p, :], ACT.Identity, bias=A["nb"][:, 2 + p:3 + p],
                                     scale=rt_out[:, 2 + p:3 + p]).then_inc(a_zn, 1)

            def h_norm(k, p, half):
                act.wait_ge(ln_st, k + 1)
                act.wait_ge(ln_tr, free(k))
                nc.scalar.activation(nrm[:, p, :], h[:, ds(k, 1), :].rearrange("p a b -> p (a b)"), ACT.Identity,
                                     bias=A["nb"][:, 4 + p:5 + p], scale=rt_out[:, 4 + p:5 + p]).then_inc(ln_nr, 1)

            pipeline(act, NT, [(1, tok_high), (6, lambda k, p, half: ln_high(k, k, 4 + p)), (0, x_norm), (3, z_norm),
                               (4, h_norm)], after={0: tok_weights})
            unit_a_hi(0)
            act.wait_ge(big_set, 1)
            for blk in range(KD):
                ins = nc.scalar.activation(big[:, blk, :], big[:, blk, :], ACT.Identity, bias=bcol[:, blk:blk + 1])
            ins.then_inc(acc_set, 1)
            act.wait_ge(g_mm, 2)
            nc.scalar.activation(B["lt"][0:AT, 1, :], B["lt"][0:AT, 1, :], ACT.Exp, scale=-1.0).then_inc(g_e1, 1)
            act.wait_ge(g_e1, 1)
            nc.scalar.activation(B["lt"][0:AT, 1, :], B["lt"][0:AT, 1, :], ACT.Ln, bias=1.0).then_inc(g_ln, 1)
            oh = B["yT_hi"]

            def head_moved(g, c, j):
                act.wait_ge(b_pj, 5 * g + j + 1)
                nc.scalar.activation(B["qk"][:, j, :], ps[:, (5 * c + j) % 2, 0:CW], ACT.Copy,
                                     scale=1.0 / WS).then_inc(b_ev, 1)

            with act.Fori(0, HEADS) as i:
                for c in range(CH):
                    g = CH * i + c
                    for j in range(1 if c == 1 else 0, 3):
                        head_moved(g, c, j)
                    act.wait_ge(b_pj, 5 * g + 4)
                    nc.scalar.activation(B["gt"][0:AT].rearrange("p a b -> p (a b)"),
                                         ps[0:AT, (5 * c + 3) % 2, 0:CW], ACT.Copy).then_inc(b_ev, 1)
                    if c:
                        if c == 1:
                            act.wait_ge(q_in, 48 * (i + 1))
                            act.wait_ge(q_sum, i + 1)
                        nc.scalar.activation(wq_st[:, c - 1, :], wq_st[:, c - 1, :], ACT.Abs,
                                             accum_out=apart[:, c - 1:c]).then_inc(q_abs, 1)
                    act.wait_ge(b_pj, 5 * g + 5)
                    nc.scalar.activation(B["v1"][0:AT, :, 0:DH],
                                         ps[0:AT, (5 * c + 4) % 2, :].rearrange("p (a b) -> p a b", a=4), ACT.Copy,
                                         scale=AS / WS).then_inc(b_ev, 1)
                    act.wait_ge(b_g, g + 1)
                    nc.scalar.activation(B["E"][0:AT], B["gt"][0:AT], ACT.Exp).then_inc(b_E, 1)
                    for j in range(2):
                        act.wait_ge(b_sc, 2 * g + j + 1)
                        nc.scalar.activation(B["sq"][0:AT, j].rearrange("p a r t -> p (a r t)"), ps[0:AT, 2 + j, 0:2 * REP * AT],
                                             ACT.Square, scale=float(DH) ** -0.5).then_inc(b_sq, 1)
                    if c == 0:
                        unit_b_hi(i, b_wc, 4 * CH * i + 1)
                    if c == CH - 1:
                        unit_a_hi(i + 1, b_pj, 5 * CH * (i + 1))
                    if c == 0:
                        head_moved(g + 1, 1, 0)
                    for j in range(2):
                        act.wait_ge(b_yt, 2 * g + j + 1)
                        nc.scalar.activation(oh[:, :, j * 2 * AT:(j + 1) * 2 * AT],
                                             ps[:, 2 + j, 0:CW].rearrange("p (r t) -> p r t", r=REP), ACT.Copy).then_inc(b_hi, 1)
            unit_b_hi(HEADS, b_wc, 4 * CH * HEADS + 1)
            act.wait_ge(ln_sh, 1)
            pipeline(act, NT, [(0, lambda k, p, half: ln_norm(1, k, p % 2)),
                               (1, lambda k, p, half: ln_high(NT + k, k, 2 + p))], turns=4,
                     after={3: lambda: act.wait_ge(ln_sh, 2)})
            act.wait_ge(r_mm, NT)
            nc.scalar.activation(B["rt"][:, 0], ps[:, 6, 0:NT * EXP].rearrange("p (a b) -> p a b", a=NT), ACT.Exp,
                                 scale=-1.0 / WS).then_inc(r_exp, 1)
            def expert(e, last):
                for r0 in range(8):
                    r = 8 * e + r0
                    c, ib = r0 // 2, r0 % 2
                    act.wait_ge(m_gu, r + 1)
                    act.wait_ge(m_t, free(r))
                    nc.scalar.activation(Dm["sg"][:, r0 % 2, :], ps[:, 2 * (r0 % 2), 0:CW], ACT.Silu,
                                         scale=1.0 / WS).then_inc(m_sg, 1)
                    if r0 == 0:
                        act.wait_ge(m_acc, NT * e + 4)
                    act.wait_ge(m_t, ready(r))
                    nc.scalar.activation(hact[0][:, ib, c * CW:(c + 1) * CW], Dm["ht"][:, r0 % 2, :],
                                         ACT.Copy).then_inc(m_hi, 1)
                unit_a_hi(HEADS + e + 1, m_gu, 8 * (e + 1))
                if not last:
                    unit_b_hi(HEADS + e + 1, m_dn, NT * (e + 1))

            with act.Fori(0, EXP) as e:
                expert(e, False)
            expert(EXP, True)

            def moved(c, j, first=False):
                act.wait_ge(f_pj, 6 * c + j + 1)
                if j == 5:
                    if not first:
                        act.wait_ge(f_av, 4 * c + 1)
                    nc.scalar.activation(Fm["V1"][0:AT], ps[0:AT, 7, :].rearrange("p (a d) -> p a d", a=4), ACT.Copy,
                                         scale=AS / WS).then_inc(f_ev, 1)
                else:
                    if not first:
                        act.wait_ge(f_rope, c)
                    nc.scalar.activation(Fm["qraw"][:, j, :], ps[:, 7, 0:CW], ACT.Copy, scale=1.0 / WS).then_inc(f_ev, 1)

            def exponential(n, a):
                act.wait_ge(f_sb, n + 1)
                nc.scalar.activation(Sc[a][0:AT], Sc[a][0:AT], ACT.Exp, scale=float(HD) ** -0.5).then_inc(f_ex, 1)

            for k in range(NT + 1):
                if k in (0, EARLY):
                    act.wait_ge(ln_sh, 3 + k // EARLY)
                if k < NT:
                    ln_norm(2, k, k % 2)
                if k:
                    ln_high(2 * NT + k - 1, k - 1, 2 + (k - 1) % 4)
                if k in (8, 10, 12):
                    moved(0, (k - 8) // 2, True)
                if k == EARLY:
                    unit_b_hi(UNITS - 1, m_dn, NT * (EXP + 1))
            for j in range(3, 6):
                moved(0, j, True)
            act.wait_ge(wa_in, 16 * (UNITS + 1))
            nc.scalar.activation(wo[0][:].rearrange("p a b -> p (a b)"), st_a[:], ACT.Copy, scale=WS).then_inc(wa_hi, 1)
            exponential(0, 0)
            act.wait_ge(wa_lo, UNITS + 1)

            def rotary(i, last):
                for a in range(4):
                    n = 4 * i + a
                    more = () if last else (i + 1,)
                    for c in more if a == 0 else ():
                        moved(c, 0)
                    if a != 2 and (not last or a < 3):
                        exponential(n + 1, (a + 1) % 4)
                    for c in more if a < 2 else ():
                        moved(c, (1, 4)[a])
                    for g in range(G4):
                        act.wait_ge(f_pt, 4 * n + g + 1)
                        if g == 0:
                            act.wait_ge(f_av, n + 1)
                        nc.scalar.activation(PT[0:AT, 4 * g:4 * g + 4, :].rearrange("p a b -> p (a b)"),
                                             ps[0:AT, g % 2, 0:CW], ACT.Copy).then_inc(f_pe, 1)
                    if a == 2:
                        exponential(n + 1, (a + 1) % 4)
                    for c in more if a == 0 else ():
                        moved(c, 2)
                    act.wait_ge(f_av, n + 2)
                    nc.scalar.activation(nT[0][:, :, ds(i * CW + a * AT, AT)],
                                         ps[:, 6, 0:CW].rearrange("p (b t) -> p b t", b=KD), ACT.Copy).then_inc(f_hi, 1)
                    for c in more:
                        if a in (0, 3):
                            moved(c, (3, None, None, 5)[a])

            with act.Fori(0, CH - 1) as i:
                rotary(i, False)
            rotary(CH - 1, True)

            def f_square(k, p, half):
                act.wait_ge(w_n, k + 1)
                act.wait_ge(w_sq, k + 1)
                nc.scalar.activation(Gm["jk"][:], xn[:, ds(k, 1), :].rearrange("p a b -> p (a b)"), ACT.Square,
                                     accum_out=Gm["ssq"][:, ds(k, 1)]).then_inc(w_sq, 1)

            def f_turned_rows(k, p, half):
                act.wait_ge(w_tr, k + 1)
                nc.scalar.activation(Gm["qT"][:, :, ds(k * P, P)],
                                     ps[:, 7, 0:256].bitcast(BF16).rearrange("p (a b) -> p a b", a=KD),
                                     ACT.Copy).then_inc(w_ev, 1)

            pipeline(act, NT, [(0, f_square)])

            def gated(k, p, half):
                def silu(f):
                    act.wait_ge(x_gu, 4 * k + f + 1)
                    act.wait_ge(x_t, free(4 * k + f))
                    if f == 0:
                        act.wait_ge(x_dq, k + 1)
                    nc.scalar.activation(sgl[:, f % 2, :], ps[:, 2 * (f % 2), :], ACT.Silu,
                                         scale=Gm["dqe"][:, p, 0:1]).then_inc(x_sg, 1)

                def square(f):
                    act.wait_ge(x_t, ready(4 * k + f))
                    act.wait_ge(x_sq, 4 * k + f + 1)
                    nc.scalar.activation(Gm["jk"][:], ff[:, p, f * 512:(f + 1) * 512], ACT.Square,
                                         accum_out=Gm["ssf"][:, p, f:f + 1]).then_inc(x_sq, 1)

                silu(0)
                for f in range(1, NF):
                    silu(f)
                    square(f - 1)
                square(NF - 1)

            def f_turned(k, p, half):
                act.wait_ge(x_dn, free(k))
                for j in range(2):
                    act.wait_ge(x_tr, 2 * k + j + 3)
                    nc.scalar.activation(fT[:, p, 8 * j:8 * j + 8, :].rearrange("p a b -> p (a b)"),
                                         ps[:, 4 + j, :].bitcast(BF16), ACT.Copy).then_inc(x_ev, 1)

            pipeline(act, NT, [(0, f_turned_rows), (1, gated), (2, f_turned)])

        @block.tensor
        def _(pe):
            pe.sem_inc(ln_tr, 2)
            pe.sem_inc(c_tr, 2)
            pe.sem_inc(f_av, 1)
            pe.sem_inc(a_mm, 2)
            pe.sem_inc(b_wc, 1)
            pe.sem_inc(x_tr, 2)
            pe.sem_inc(x_dn, 2)
            pe.wait_ge(ones_set, 1)

            def ln_turn(n, p, bank, split=None):
                pe.wait_ge(ln_nr, ready(n))
                pe.wait_ge(ln_lo, free(n) if split is None else split)
                for b in range(KD):
                    ins = nc.tensor.transpose(ps[:, bank, b * P:(b + 1) * P], nrm[:, p, b * P:(b + 1) * P], ident[:])
                ins.then_inc(ln_tr, 1)

            def split3(dst, lhs, rhs, start, stop):
                nc.tensor.matmul(dst, lhs[0], rhs[0], start=start, stop=False)
                nc.tensor.matmul(dst, lhs[0], rhs[1], start=False, stop=False)
                return nc.tensor.matmul(dst, lhs[1], rhs[0], start=False, stop=stop)

            def tok_turn(k, p, half):
                pe.wait_ge(a_norm, k + 1)
                for j in range(2):
                    pe.wait_ge(a_lo, 2 * k + j + 1)
                    for b in range(4):
                        ins = nc.tensor.transpose(ps[:, j, b * P:(b + 1) * P],
                                                  A["xh"][:, p, (4 * j + b) * P:(4 * j + b + 1) * P], ident[:])
                    ins.then_inc(a_tr, 1)

            def tok_mm(k, p, half):
                pe.wait_ge(wt_lo, 2)
                pe.wait_ge(a_lo, 2 * k + 4)
                pe.wait_ge(a_h, free(k))
                for b in range(KI):
                    ins = split3(ps[:, 2 + p, :], [A["xT_hi"][:, p, b, :], A["xT_lo"][:, p, b, :]],
                                 [A["wt_hi"][:, b, :], A["wt_lo"][:, b, :]], b == 0, b == KI - 1)
                ins.then_inc(a_mm, 1)

            def tok_shift():
                pe.wait_ge(a_b1, 1)
                for j in range(2):
                    pe.wait_ge(wt_in[j], 16)
                    for b in range(4):
                        ins = nc.tensor.matmul(ps[:, 7, :], A["b1b"][:, 4 * j + b, :], wt_st[j][:, b * D:(b + 1) * D],
                                               start=j == 0 and b == 0, stop=j == 1 and b == 3)
                    ins.then_inc(a_tb, 1)

            pe.wait_ge(ident_in, 16)

            def gate_logits(a0, a1):
                pe.wait_ge(ln_lo, ready((a1 * AT - 1) // P))
                pe.wait_ge(gw_lo, 1)
                for a in range(a0, a1):
                    for b in range(KD):
                        x = [nT[0][:, b, a * AT:(a + 1) * AT], nT[1][:, b, a * AT:(a + 1) * AT]]
                        ins = split3(ps[0:AT, 0, a * HEADS:(a + 1) * HEADS], x,
                                     [gw[0][:, b, 0:HEADS], gw[1][:, b, 0:HEADS]], b == 0, b == KD - 1)
                return ins

            pipeline(pe, NT, [(1, tok_turn), (6, lambda k, p, half: ln_turn(k, p, 4 + p)), (2, tok_mm)],
                     after={0: tok_shift, NT + 2: lambda: gate_logits(0, 5), NT + 3: lambda: gate_logits(5, 10),
                            NT + 4: lambda: gate_logits(10, 13)})
            gate_logits(13, T // AT).then_inc(g_mm, 1)
            pe.wait_ge(g_lg, 1)
            nc.tensor.matmul(ps[0:AT, 7, 0:16 * HEADS], tri[0:AT, :], B["lg"][0:AT].rearrange("p a b -> p (a b)"),
                             start=True, stop=True).then_inc(g_cum, 1)

            def out_proj(g, c):
                pe.wait_ge(b_lo, 2 * g + 4)
                for blk in range(4):
                    pe.wait_ge(b_acc, free(4 * g + blk))
                    for r in range(REP):
                        ins = split3(ps[:, 6 + blk % 2, 0:CW],
                                     [wb[x][:, r, blk * P:(blk + 1) * P] for x in range(2)],
                                     [B["yT_hi"][:, r, :], B["yT_lo"][:, r, :]], r == 0, r == REP - 1)
                    ins.then_inc(b_wc, 1)

            def head_project(g, c, j):
                pe.wait_ge(b_ev, free(5 * g + j))
                cols = slice(c * CW, (c + 1) * CW)
                for b in range(KD):
                    ins = split3(ps[:, (5 * c + j) % 2, 0:CW], [wa[x][:, b, j * P:(j + 1) * P] for x in range(2)],
                                 [nT[x][:, b, cols] for x in range(2)], b == 0, b == KD - 1)
                ins.then_inc(b_pj, 1)

            def head(i, last):
                for c in range(CH):
                    g = CH * i + c
                    for j in range((2, 2, 1, 1)[c], 3):
                        head_project(g, c, j)
                    pe.wait_ge(b_ev, free(5 * g + 3))
                    pe.wait_ge(b_D, g + 1)
                    nc.tensor.matmul(ps[0:AT, (5 * c + 3) % 2, 0:CW], ones[0:AT, 0:AT], B["Dg"][0:AT].rearrange("p a b -> p (a b)"),
                                     start=True, stop=True).then_inc(b_pj, 1)
                    pe.wait_ge(b_ev, free(5 * g + 4))
                    for a in range(4):
                        tok = slice(c * CW + a * AT, c * CW + (a + 1) * AT)
                        for b in range(KD):
                            ins = split3(ps[0:AT, (5 * c + 4) % 2, a * P:(a + 1) * P], [nT[x][:, b, tok] for x in range(2)],
                                         [wa[x][:, b, 3 * P:4 * P] for x in range(2)], b == 0, b == KD - 1)
                    ins.then_inc(b_pj, 1)
                    pe.wait_ge(b_ev, ready(5 * g + 2))
                    for j in range(2):
                        pe.wait_ge(b_lo, free(2 * g + j))
                        for a in range(2):
                            tok = slice((2 * j + a) * AT, (2 * j + a + 1) * AT)
                            ins = nc.tensor.matmul(ps[0:AT, 2 + j, a * REP * AT:(a + 1) * REP * AT],
                                                   B["qk"][:, 2, tok], B["qk"][:, 0:2, tok], start=True, stop=True)
                        ins.then_inc(b_sc, 1)
                    if c == 0:
                        head_project(g + 1, 1, 0)
                    else:
                        if c == 1:
                            pe.wait_ge(wb_lo, i + 1)
                        out_proj(g - 1, c - 1)
                    pe.wait_ge(b_ev, ready(5 * g + 4))
                    for j in range(2):
                        pe.wait_ge(b_a, 2 * g + j + 1)
                        if j == 1:
                            pe.wait_ge(b_acc, 4 * g + 2)
                        for a in range(2):
                            for r in range(REP):
                                ins = nc.tensor.matmul(ps[0:AT, 4 + 2 * j + a, r * (DH + 1):(r + 1) * (DH + 1)],
                                                       B["a"][0:AT, j, a, r, :], B["v1"][0:AT, 2 * j + a, :],
                                                       start=True, stop=True)
                        ins.then_inc(b_av, 1)
                    if c == 0:
                        head_project(g + 1, 1, 1)
                    elif c < CH - 1:
                        head_project(g + 1, c + 1, 0)
                    elif not last:
                        pe.wait_ge(wa_lo, i + 2)
                        head_project(g + 1, 0, 0)
                    for j in range(2):
                        pe.wait_ge(b_yn, 2 * g + j + 1)
                        for r in range(REP):
                            for a in range(2):
                                ins = nc.tensor.transpose(ps[:, 2 + j, (2 * r + a) * AT:(2 * r + a + 1) * AT],
                                                          B["yn"][0:AT, j, a, r, :], ident[0:AT, 0:AT])
                        ins.then_inc(b_yt, 1)
                if not last:
                    head_project(g + 1, 0, 1)
                out_proj(g, c)

            pe.wait_ge(wa_lo, 1)
            for j in range(2):
                head_project(0, 0, j)
            with pe.Fori(0, HEADS - 1) as i:
                head(i, False)
            head(HEADS - 1, True)
            pe.wait_ge(q_sum, HEADS + 1)
            nc.tensor.matmul(ps[:, 0, 0:3], ones[:], asum[:], start=True, stop=True).then_inc(q_tot, 1)

            def route(k, p, half):
                pe.wait_ge(ln_lo, ready(NT + k))
                for b in range(KD):
                    ins = split3(ps[:, 6, ds(k * EXP, EXP)], [nT[x][:, b, ds(k * P, P)] for x in range(2)],
                                 [gw[x][:, b, HEADS:] for x in range(2)], b == 0, b == KD - 1)
                ins.then_inc(r_mm, 1)

            def c_turn(k, p, half):
                pe.wait_ge(c_h, free(k))
                for b in range(KD):
                    ins = nc.tensor.transpose(ps[:, 2 + p, b * P:(b + 1) * P], big[:, b, k * P:(k + 1) * P], ident[:])
                ins.then_inc(c_tr, 1)

            pe.wait_ge(b_acc, 4 * CH * HEADS + 2)
            for k in range(NT):
                c_turn(k, k % 2, k // 2)
            pipeline(pe, NT, [(0, lambda k, p, half: ln_turn(NT + k, p % 2, 2 + p, NT + k - 1)), (2, route)], turns=4)
            with pe.Fori(0, EXP + 1) as e:
                pe.wait_ge(wa_lo, HEADS + e + 1)
                for r0 in range(8):
                    r, c, ib = 8 * e + r0, r0 // 2, r0 % 2
                    pe.wait_ge(m_t, free(r))
                    for q in range(2):
                        for b in range(KD):
                            ins = split3(ps[:, 2 * (r0 % 2) + q, 0:CW],
                                         [wa[x][:, b, q * FI + ib * P:q * FI + (ib + 1) * P] for x in range(2)],
                                         [nT[x][:, b, c * CW:(c + 1) * CW] for x in range(2)], b == 0, b == KD - 1)
                    ins.then_inc(m_gu, 1)
                pe.wait_ge(wb_lo, HEADS + e + 1)
                pe.wait_ge(m_pad, 2)
                for k in range(NT):
                    last = min((k * P + P - 1) // CW, CH - 1)
                    pe.wait_ge(m_lo, 8 * e + 2 * last + 2)
                    pe.wait_ge(m_acc, NT * e + k + 1)
                    for ib in range(2):
                        ins = split3(ps[:, 4 + k % 4, :], [hact[x][:, ib, k * P:(k + 1) * P] for x in range(2)],
                                     [wb[x][:, ib, :] for x in range(2)], ib == 0, ib == 1)
                    ins.then_inc(m_dn, 1)
            wkv = [wb[x][:].rearrange("p a b -> p (a b)").rearrange("p (a b) -> p a b", a=KD) for x in range(2)]

            def project(c, j):
                pe.wait_ge(f_ev, 6 * c + j + 1)
                if j == 5:
                    for a in range(4):
                        for b in range(KD):
                            ins = split3(ps[0:AT, 7, a * P:(a + 1) * P], [nT[x][:, b, ds(c * CW + a * AT, AT)] for x in range(2)],
                                         [wkv[x][:, b, P:2 * P] for x in range(2)], b == 0, b == KD - 1)
                else:
                    for b in range(KD):
                        w = [wa[x][:, b, j * P:(j + 1) * P] if j < 4 else wkv[x][:, b, 0:P] for x in range(2)]
                        ins = split3(ps[:, 7, 0:CW], w, [nT[x][:, b, ds(c * CW, CW)] for x in range(2)], b == 0, b == KD - 1)
                ins.then_inc(f_pj, 1)

            def scores(c, n, a):
                pe.wait_ge(f_rope, c + 1)
                pe.wait_ge(f_md, n + 1)
                tok = slice(a * AT, (a + 1) * AT)
                for j in range(J4):
                    for g in range(G4):
                        r = slice(HD * g, HD * (g + 1))
                        ins = nc.tensor.matmul(ps[0:AT, 2 + g, j * AT:(j + 1) * AT], Fm["qr"][r, j, tok],
                                               Fm["qr"][r, 4, tok], start=True, stop=True)
                ins.then_inc(f_sc, 1)

            def turn(n, a):
                pe.wait_ge(f_s, n + 1)
                for g in range(G4):
                    pe.wait_ge(f_pe, free(4 * n + g))
                    for j in range(J4):
                        ins = nc.tensor.transpose(ps[0:AT, g % 2, j * AT:(j + 1) * AT], Sc[a][0:AT, 4 * g + j, :],
                                                  ident[0:AT, 0:AT])
                    ins.then_inc(f_pt, 1)

            def weighted(c, n, a):
                pe.wait_ge(f_lo, n + 1)
                pe.wait_ge(f_ev, 6 * c + 7)
                for g in range(G4):
                    pe.wait_ge(f_pe, ready(4 * n + g))
                    ins = nc.tensor.matmul(ps[HD * g:HD * (g + 1), 6, 0:CW], Fm["V1"][0:AT, a, HD * g:HD * (g + 1)],
                                           PT[0:AT, 4 * g:4 * g + 4, :].rearrange("p a b -> p (a b)"), start=True, stop=True)
                ins.then_inc(f_av, 1)

            for k in range(NT):
                ln_turn(2 * NT + k, k % 2, 2 + k % 4, 2 * NT + k - 1)
                if k == 6:
                    pe.wait_ge(wa_lo, UNITS)
                if k in (6, 8, 10):
                    project(0, (k - 6) // 2)
            pe.wait_ge(wb_lo, UNITS)
            for j in range(3, 6):
                project(0, j)
            scores(0, 0, 0)
            scores(0, 1, 1)

            def rotary(i, last):
                for a in range(4):
                    n = 4 * i + a
                    ahead = lambda: scores(i + (a + 2) // 4, n + 2, (a + 2) % 4)
                    if not last and a == 0:
                        project(i + 1, 0)
                    if a < 2 or a == 3 and not last:
                        ahead()
                    if not last and a < 2:
                        project(i + 1, (1, 4)[a])
                    turn(n, a)
                    if not last and a != 1:
                        [lambda: project(i + 1, 2), None, ahead, lambda: project(i + 1, 5)][a]()
                    weighted(i, n, a)
                    if a == 0 and not last:
                        project(i + 1, 3)

            with pe.Fori(0, CH - 1) as i:
                rotary(i, False)
            rotary(CH - 1, True)
            pe.wait_ge(wa_lo, UNITS + 1)

            def out_rows(k, p, half):
                pe.wait_ge(w_h, free(k))
                for b in range(KD):
                    ins = split3(ps[:, p, :], [nT[x][:, b, ds(k * P, P)] for x in range(2)],
                                 [wo[x][:, b, :] for x in range(2)], b == 0, b == KD - 1)
                ins.then_inc(w_mm, 1)

            def q_turn(k, p, half):
                pe.wait_ge(w_q, k + 1)
                pe.wait_ge(w_ev, k + 1)
                for b in range(KD):
                    ins = nc.tensor.transpose(ps[:, 7, 64 * b:64 * b + 64].bitcast(BF16), qi[:, ds(k, 1), b * P:(b + 1) * P].rearrange("p a b -> p (a b)"),
                                              identb[:])
                ins.then_inc(w_tr, 1)

            pipeline(pe, NT, [(0, out_rows)])

            def gate_up(k, fs):
                if fs[0] == 0:
                    pe.wait_ge(w_ev, k + 2)
                for f in fs:
                    pe.wait_ge(x_t, free(4 * k + f))
                    for q in range(2):
                        for b in range(KD):
                            ins = nc.tensor.matmul(ps[:, 2 * (f % 2) + q, :], Gm["qT"][:, b, ds(k * P, P)],
                                                   qw[:, q, b * FF + f * 512:b * FF + (f + 1) * 512],
                                                   start=b == 0, stop=b == KD - 1)
                    ins.then_inc(x_gu, 1)

            def f_turn(k, p, half):
                pe.wait_ge(x_q, k + 1)
                for j in range(2):
                    pe.wait_ge(x_ev, 2 * k + j + 1)
                    for b in range(8):
                        ins = nc.tensor.transpose(ps[:, 4 + j, 64 * b:64 * b + 64].bitcast(BF16),
                                                  fi[:, (8 * j + b) * P:(8 * j + b + 1) * P], identb[:])
                    ins.then_inc(x_tr, 1)

            def down(k, p, half):
                pe.wait_ge(x_og, k + 1)
                pe.wait_ge(x_ev, 2 * k + 4)
                for b in range(FF // P):
                    ins = nc.tensor.matmul(ps[:, 6, :], fT[:, p, b, :], qw[:, 2, b * D:(b + 1) * D],
                                           start=b == 0, stop=b == FF // P - 1)
                ins.then_inc(x_dn, 1)

            pe.wait_ge(t_done, 1)
            pipeline(pe, NT, [(0, q_turn), (1, lambda k, p, half: gate_up(k, (0, 1))), (3, down),
                              (1, lambda k, p, half: gate_up(k, (2, 3))), (2, f_turn)])

        @block.vector
        def _(dve):
            V = nc.vector
            dve.sem_inc(ln_lo, 2)
            dve.sem_inc(a_lo, 2)
            dve.sem_inc(a_h, 2)
            dve.sem_inc(b_lo, 2)
            dve.sem_inc(c_h, 2)
            dve.sem_inc(q_sum, 1)
            dve.sem_inc(f_md, 1)
            dve.sem_inc(f_lo, 1)
            dve.sem_inc(w_h, 2)
            dve.sem_inc(x_t, 2)
            dve.sem_inc(x_og, 1)
            dve.sem_inc(b_acc, 2)
            dve.sem_inc(m_acc, 4)
            dve.sem_inc(m_t, 2)
            dve.wait_ge(ones_set, 2)
            order = Order(dve, dve_o)

            def split_lo(dst, src, hi, sem_out):
                V.scalar_tensor_tensor(dst, src, WS, hi, ALU.mult, ALU.subtract).then_inc(sem_out, 1)

            def unit_a_lo(n):
                dve.wait_ge(wa_hi, n + 1)
                split_lo(wa[1][:].rearrange("p a b -> p (a b)"), st_a[:], wa[0][:].rearrange("p a b -> p (a b)"), wa_lo)

            def unit_b_lo(n):
                dve.wait_ge(wb_hi, n + 1)
                split_lo(wb[1][:].rearrange("p a b -> p (a b)"), st_b[:], wb[0][:].rearrange("p a b -> p (a b)"), wb_lo)

            def ask(src, scale, eps, dst, sem_out):
                V.tensor_scalar(dst, src, scale, eps, ALU.mult, ALU.add).then_inc(sem_out, 1)

            def row(k):
                return h[:, ds(k, 1), :].rearrange("p a b -> p (a b)")

            def tile_stats(k, p, half):
                V.bn_stats(bst12[:, ds(k, 1), :].rearrange("p a b -> p (a b)"), row(k)).then_inc(ln_bs, 1)

            def deviations(use, k0, k1, asked):
                dve.wait_ge(ln_bs, NT * (use - 1) + k1)
                dve.sem_inc(passed, 1)
                for k in range(k0, k1):
                    ins = V.bn_aggr(mv12[:, k, :], bst12[:, k, :])
                order(ins)
                ask(mv12[:, k0:k1, 1], 1.0, 1e-5, rt_in[:, k0:k1], asked)

            def shifts(n, k0, k1, done):
                dve.wait_ge(done, n + 1)
                V.scalar_tensor_tensor(nb12[:, k0:k1], mv12[:, k0:k1, 0], -1.0, rt_out[:, k0:k1], ALU.mult,
                                       ALU.mult).then_inc(ln_sh, 1)

            def ln_low(n, k, bank):
                dve.wait_ge(ln_hi, n + 1)
                V.tensor_tensor(nT[1][:, :, ds(k * P, P)], ps[:, bank, :].rearrange("p (a b) -> p a b", a=KD),
                                nT[0][:, :, ds(k * P, P)], ALU.subtract).then_inc(ln_lo, 1)

            dve.wait_ge(g1_in, 16)
            V.tensor_scalar(A["g1s"][:], A["g1"][:], WS, None, ALU.mult).then_inc(a_g1, 1)
            dve.wait_ge(b1_in, 16)
            for b in range(KI):
                ins = V.tensor_scalar(A["b1b"][:, b, :], ones[:], A["b1"][:, b:b + 1], None, ALU.mult)
            ins.then_inc(a_b1, 1)

            def tok_weights():
                for j in range(2):
                    dve.wait_ge(wt_hi, j + 1)
                    for b in range(4):
                        ins = V.scalar_tensor_tensor(A["wt_lo"][:, 4 * j + b, :], wt_st[j][:, b * D:(b + 1) * D],
                                                     A["g1s"][:, 4 * j + b:4 * j + b + 1], A["wt_hi"][:, 4 * j + b, :],
                                                     ALU.mult, ALU.subtract)
                    ins.then_inc(wt_lo, 1)

            def tok_bias():
                dve.wait_ge(gw_hi, 1)
                split_lo(gw[1][:], gst[:], gw[0][:], gw_lo)
                dve.wait_ge(a_tb, 2)
                dve.wait_ge(rows_in, 48)
                order(V.tensor_tensor(A["tb"][:], A["tb"][:], ps[:, 7, :], ALU.add))

            def moments(rows, kind, p, n, sem_out, eps):
                s = 2 * kind + p
                dve.sem_inc(passed, 1)
                for j in range(n):
                    ins = V.bn_stats(A["bst"][:, s, j, :], rows[:, j * 512:(j + 1) * 512] if n > 1 else rows)
                order(ins)
                dve.sem_inc(passed, 1)
                order(V.bn_aggr(A["mv"][:, s, :], A["bst"][:, s, 0:n, :].rearrange("p a b -> p (a b)")))
                ask(A["mv"][:, s, 1:2], 1.0, eps, rt_in[:, s:s + 1], sem_out)

            def shift(kind, done, sem_out):
                def step(k, p, half):
                    s = 2 * kind + p
                    dve.wait_ge(done, k + 1)
                    V.scalar_tensor_tensor(A["nb"][:, s:s + 1], A["mv"][:, s, 0:1], -1.0, rt_out[:, s:s + 1], ALU.mult,
                                           ALU.mult).then_inc(sem_out, 1)
                return step

            def x_stats(k, p, half):
                dve.wait_ge(x_in[p], 16 * (half + 1))
                moments(A["xt"][:, p, :], 0, p, 2, rx_ask, 1e-6)

            def x_low(k, p, half):
                for j in range(2):
                    dve.wait_ge(a_hi, 2 * k + j + 1)
                    V.tensor_tensor(A["xT_lo"][:, p, 4 * j:4 * j + 4, :], ps[:, j, :].rearrange("p (a b) -> p a b", a=4),
                                    A["xT_hi"][:, p, 4 * j:4 * j + 4, :], ALU.subtract).then_inc(a_lo, 1)

            def z_stats(k, p, half):
                dve.wait_ge(a_mm, ready(k))
                z = A["z"][:, p, :]
                order(V.scalar_tensor_tensor(z, ps[:, 2 + p, :], 1.0 / WS, A["tb"][:], ALU.mult, ALU.add))
                dve.sem_inc(a_h, 1)
                moments(z, 1, p, 1, rz_ask, 1e-6)

            def h_stats(k, p, half):
                dve.wait_ge(a_row, k + 1)
                moments(row(k), 2, p, 1, rh_ask, 1e-5)

            pipeline(dve, NT, [(3, z_stats), (0, x_stats), (3, shift(1, rz_done, a_sz)), (0, shift(0, rx_done, a_sx)),
                               (1, x_low), (6, lambda k, p, half: ln_low(k, k, 4 + p)), (4, h_stats),
                               (4, shift(2, rh_done, ln_st))], order, 7, after={0: tok_weights, 1: tok_bias})
            unit_a_lo(0)
            dve.wait_ge(consts_in, 128)
            dve.wait_ge(ident_in, 16)
            order(V.tensor_copy(identb[:], ident[:]))
            dve.wait_ge(g_mm, 1)
            lt = B["lt"]
            order(V.tensor_scalar(lt[0:AT, 0, :], ps[0:AT, 0, 0:128], 1.0 / WS, GATE_OFFSET, ALU.mult, ALU.add))
            V.scalar_tensor_tensor(lt[0:AT, 1, :], lt[0:AT, 0, :], -1.0, lt[0:AT, 0, :], ALU.mult, ALU.max).then_inc(g_mm, 1)
            dve.wait_ge(g_ln, 1)
            V.scalar_tensor_tensor(B["lg"][0:AT], lt[0:AT, 0, :].rearrange("p (a h) -> p h a", h=HEADS), 0.0,
                                   lt[0:AT, 1, :].rearrange("p (a h) -> p h a", h=HEADS), ALU.min,
                                   ALU.subtract).then_inc(g_lg, 1)
            dve.wait_ge(g_cum, 1)
            order(V.tensor_copy(B["LG"][0:AT].rearrange("p a b -> p (a b)"), ps[0:AT, 7, 0:128]))
            order(V.memset(B["v1"][:, :, DH:DH + 1], 1.0))
            order(V.memset(asum[:], 0.0))
            dve.wait_ge(acc_set, 1)

            def accumulate(g, c):
                for blk in range(4):
                    dve.wait_ge(b_wc, 4 * g + blk + 2)
                    acc = big[:, blk, c * CW:(c + 1) * CW]
                    V.scalar_tensor_tensor(acc, ps[:, 6 + blk % 2, 0:CW], 1.0 / (WS * AS), acc, ALU.mult,
                                           ALU.add).then_inc(b_acc, 1)

            with dve.Fori(0, HEADS) as i:
                order.enter(i, 2 + CH * 5 + 1)
                order(V.tensor_copy(B["lgh"][0:AT], B["lg"][0:AT, ds(i, 1), :].rearrange("p a b -> p (a b)")))
                order(V.tensor_copy(B["LGh"][0:AT], B["LG"][0:AT, ds(i, 1), :].rearrange("p a b -> p (a b)")))
                for c in range(CH):
                    g = CH * i + c
                    V.tensor_tensor(B["Dg"][0:AT], B["lgh"][0:AT, 4 * c:4 * c + 4].unsqueeze(2).broadcast_to([AT, 4, AT]),
                                    tri[0:AT].unsqueeze(1).broadcast_to([AT, 4, AT]), ALU.mult).then_inc(b_D, 1)
                    dve.wait_ge(b_ev, ready(5 * g + 3))
                    order(V.tensor_tensor(B["gt"][0:AT], B["gt"][0:AT],
                                          B["LGh"][0:AT, 4 * c:4 * c + 4].unsqueeze(2).broadcast_to([AT, 4, AT]), ALU.subtract))
                    V.tensor_tensor(B["gt"][0:AT], B["gt"][0:AT], mask[0:AT].unsqueeze(1).broadcast_to([AT, 4, AT]),
                                    ALU.add).then_inc(b_g, 1)
                    dve.wait_ge(b_E, g + 1)
                    for j in range(2):
                        dve.wait_ge(b_sq, 2 * g + j + 1)
                        V.tensor_tensor(B["a"][0:AT, j], B["sq"][0:AT, j],
                                        B["E"][0:AT, 2 * j:2 * j + 2].unsqueeze(2).broadcast_to([AT, 2, REP, AT]),
                                        ALU.mult).then_inc(b_a, 1)
                    if c:
                        accumulate(g - 1, c - 1)
                    else:
                        unit_b_lo(i)
                    if c == CH - 1:
                        unit_a_lo(i + 1)
                    for j in range(2):
                        dve.wait_ge(b_av, 2 * g + j + 1)
                        y = ps[0:AT, 4 + 2 * j:6 + 2 * j, 0:REP * (DH + 1)].rearrange("p a (r d) -> p a r d", r=REP)
                        order(V.tensor_scalar(B["rn"][0:AT, j], y[:, :, :, DH], 1e-6, None, ALU.add))
                        order(V.reciprocal(B["rn"][0:AT, j], B["rn"][0:AT, j]))
                        V.tensor_tensor(B["yn"][0:AT, j], y[:, :, :, 0:DH],
                                        B["rn"][0:AT, j].unsqueeze(3).broadcast_to([AT, 2, REP, DH]), ALU.mult).then_inc(b_yn, 1)
                    for j in range(2):
                        dve.wait_ge(b_hi, 2 * g + j + 1)
                        V.tensor_tensor(B["yT_lo"][:, :, j * 2 * AT:(j + 1) * 2 * AT],
                                        ps[:, 2 + j, 0:CW].rearrange("p (r t) -> p r t", r=REP),
                                        B["yT_hi"][:, :, j * 2 * AT:(j + 1) * 2 * AT], ALU.subtract).then_inc(b_lo, 1)
                dve.wait_ge(q_abs, 3 * i + 4)
                order(V.tensor_tensor(asum[:], asum[:], apart[:], ALU.add))
                dve.sem_inc(q_sum, 1)
                accumulate(g, c)
                order.leave(HEADS)
            unit_b_lo(HEADS)
            dve.wait_ge(q_tot, 1)
            order(V.tensor_scalar(wdq[:], ps[:, 0, 0:3], 1.0 / (D * FF), 1e-5, ALU.mult, ALU.max))
            V.reciprocal(wsc[:], wdq[:]).then_inc(q_scl, 1)

            def c_add(k, p, half):
                dve.wait_ge(c_tr, ready(k))
                V.tensor_tensor(row(k), ps[:, 2 + p, :], row(k), ALU.add).then_inc(c_h, 1)

            def c_stats(k, p, half):
                dve.wait_ge(c_h, k + 3)
                dve.sem_inc(passed, 1)
                tile_stats(k, p, half)

            for k in range(NT + 1):
                if k < NT:
                    c_add(k, k % 2, k // 2)
                if k:
                    c_stats(k - 1, (k - 1) % 2, (k - 1) // 2)
                if k == EARLY:
                    deviations(1, 0, EARLY, rc_ask)
                if k == NT - 1:
                    shifts(0, 0, EARLY, rc_done)
            deviations(1, EARLY, NT, rc_ask)
            shifts(1, EARLY, NT, rc_done)
            pipeline(dve, NT, [(0, lambda k, p, half: ln_low(NT + k, k, 2 + p))], turns=4)

            rt = B["rt"]
            E1, sc, sbz, gt_, eq, ca, cb, sel = [rt[:, x] for x in range(8)]
            dve.wait_ge(r_exp, 1)
            order(V.tensor_scalar(sc, E1, 1.0, None, ALU.add))
            order(V.reciprocal(sc, sc))
            order(V.tensor_tensor(sbz, sc, ebias[:].unsqueeze(1).broadcast_to([P, NT, EXP]), ALU.add))
            for k in range(NT):
                ins = V.max(B["m8"][:, k, :], sbz[:, k, :])
            order(ins)
            thr = B["m8"][:, :, TOPK - 1:TOPK].broadcast_to([P, NT, EXP])
            V.tensor_tensor(gt_, sbz, thr, ALU.is_gt)
            order(V.tensor_tensor(eq, sbz, thr, ALU.is_equal))
            V.tensor_reduce(B["need"][:], gt_, AX.X, ALU.add)
            src, dst = eq, ca
            for s in (1, 2, 4, 8):
                V.tensor_copy(dst[:, :, 0:s], src[:, :, 0:s])
                order(V.tensor_tensor(dst[:, :, s:], src[:, :, s:], src[:, :, 0:EXP - s], ALU.add))
                src, dst = dst, (cb if dst is ca else ca)
            order(V.tensor_tensor(src, src, B["need"][:].unsqueeze(2).broadcast_to([P, NT, EXP]), ALU.add))
            order(V.scalar_tensor_tensor(src, src, TOPK + 0.5, eq, ALU.is_lt, ALU.mult))
            order(V.tensor_tensor(sel, src, gt_, ALU.add))
            order(V.tensor_tensor(sel, sel, sc, ALU.mult))
            order(V.tensor_reduce(B["need"][:], sel, AX.X, ALU.add))
            order(V.reciprocal(B["need"][:], B["need"][:]))
            V.memset(cw[:, EXP, :], 1.0)
            order(V.tensor_tensor(cw[:, 0:EXP, :].rearrange("p e k -> p k e"), sel,
                                  B["need"][:].unsqueeze(2).broadcast_to([P, NT, EXP]), ALU.mult))
            dve.sem_inc(r_done, 1)
            for x in range(2):
                V.memset(hact[x][:, :, T:TP], 0.0).then_inc(m_pad, 1)

            def expert(e, last):
                dve.wait_ge(m_acc, 4 + NT * e)
                order(V.tensor_scalar(cwe[:], cw[:, ds(e, 1), :].rearrange("p a b -> p (a b)"), 1.0 / (WS * AS), None, ALU.mult))
                for r0 in range(8):
                    r, c, ib = 8 * e + r0, r0 // 2, r0 % 2
                    dve.wait_ge(m_sg, r + 1)
                    V.scalar_tensor_tensor(Dm["ht"][:, r0 % 2, :], ps[:, 2 * (r0 % 2) + 1, 0:CW], AS / WS,
                                           Dm["sg"][:, r0 % 2, :], ALU.mult, ALU.mult).then_inc(m_t, 1)
                    dve.wait_ge(m_hi, r + 1)
                    V.tensor_tensor(hact[1][:, ib, c * CW:(c + 1) * CW], Dm["ht"][:, r0 % 2, :],
                                    hact[0][:, ib, c * CW:(c + 1) * CW], ALU.subtract).then_inc(m_lo, 1)
                for k in range(NT):
                    if k == 4 and not last:
                        unit_a_lo(HEADS + e + 1)
                    dve.wait_ge(m_dn, NT * e + k + 1)
                    V.scalar_tensor_tensor(h[:, k, :], ps[:, 4 + k % 4, :], cwe[:, k:k + 1], h[:, k, :], ALU.mult,
                                           ALU.add).then_inc(m_acc, 1)
                    if last and k:
                        total_stats(e, k - 1)
                    if last and k == EARLY:
                        deviations(2, 0, EARLY, re_ask)
                    if last and k == NT - 1:
                        shifts(0, 0, EARLY, re_done)
                if last:
                    total_stats(e, NT - 1)
                    deviations(2, EARLY, NT, re_ask)
                    unit_a_lo(HEADS + e + 1)
                    shifts(1, EARLY, NT, re_done)
                else:
                    unit_b_lo(HEADS + e + 1)

            def total_stats(e, k):
                dve.wait_ge(m_acc, 4 + NT * e + k + 1)
                dve.sem_inc(passed, 1)
                tile_stats(k, k % 2, k // 2)

            with dve.Fori(0, EXP) as e:
                order.enter(e, 1)
                expert(e, False)
                order.leave(EXP)
            expert(EXP, True)

            def rotate(c, j, first=False):
                dve.wait_ge(f_ev, 6 * c + j + 2)
                dve.sem_inc(passed, 1)
                V.stream_shuffle(Fm["qs"][:, j, :], Fm["qraw"][:, j, :],
                                 [(x + HD // 2) % HD for x in range(HD)]).then_inc(f_sh, 1)
                if first:
                    dve.wait_ge(f_sh, j + 1)
                    V.tensor_tensor(Fm["qs"][:, j, :], Fm["qs"][:, j, :], sinT[:], ALU.mult).then_inc(f_cos, 1)

            def rotated(c, first=False):
                dve.wait_ge(f_cos, 10 * c + 10)
                if not first:
                    dve.wait_ge(f_sc, 4 * c)
                V.tensor_tensor(Fm["qr"][:], Fm["qraw"][:], Fm["qs"][:], ALU.add).then_inc(f_rope, 1)

            def masked(n, a):
                dve.wait_ge(f_sc, n + 1)
                V.tensor_tensor(Sc[a][0:AT].rearrange("p (g j) s -> p g j s", j=J4),
                                ps[0:AT, 2:6, 0:CW].rearrange("p g (j s) -> p g j s", j=J4),
                                maskT[0:AT].unsqueeze(1).unsqueeze(1).broadcast_to([AT, G4, J4, AT]), ALU.add).then_inc(f_md, 1)
                dve.wait_ge(f_md, n + 2)
                V.tensor_reduce(Fm["mx"][0:AT, a], Sc[a][0:AT], AX.X, ALU.max).then_inc(f_mx, 1)

            def weights(n, a):
                dve.wait_ge(f_ex, n + 1)
                order(V.tensor_reduce(Fm["rd"][0:AT, a], Sc[a][0:AT], AX.X, ALU.add))
                order(V.reciprocal(Fm["rd"][0:AT, a], Fm["rd"][0:AT, a]))
                V.tensor_tensor(Sc[a][0:AT], Sc[a][0:AT], Fm["rd"][0:AT, a].unsqueeze(2).broadcast_to([AT, 16, AT]),
                                ALU.mult).then_inc(f_s, 1)

            for k in range(NT):
                ln_low(2 * NT + k, k, 2 + k % 4)
                if k == EARLY:
                    unit_b_lo(UNITS - 1)
                if k in (9, 11):
                    rotate(0, (k - 9) // 2, True)
            for j in range(2, 5):
                rotate(0, j, True)
            rotated(0, True)
            masked(0, 0)
            dve.wait_ge(wa_hi, UNITS + 1)
            split_lo(wo[1][:].rearrange("p a b -> p (a b)"), st_a[:], wo[0][:].rearrange("p a b -> p (a b)"), wa_lo)
            masked(1, 1)
            weights(0, 0)

            def rotary(i, last):
                for a in range(4):
                    n = 4 * i + a
                    if a == 0 and not last:
                        rotate(i + 1, 0)
                    if not last or a < 3:
                        weights(n + 1, (a + 1) % 4)
                    if a < 2 and not last:
                        rotate(i + 1, (1, 4)[a])
                    if not last or a < 2:
                        masked(n + 2, (a + 2) % 4)
                    if a == 0 and not last:
                        rotate(i + 1, 2)
                    if a == 1 and not last:
                        rotated(i + 1)
                    dve.wait_ge(f_hi, n + 1)
                    cols = ds(i * CW + a * AT, AT)
                    V.tensor_tensor(nT[1][:, :, cols], ps[:, 6, 0:CW].rearrange("p (b t) -> p b t", b=KD),
                                    nT[0][:, :, cols], ALU.subtract).then_inc(f_lo, 1)
                    if a == 0 and not last:
                        rotate(i + 1, 3)

            with dve.Fori(0, CH - 1) as i:
                order.enter(i, 4 * 2)
                rotary(i, False)
                order.leave(CH - 1)
            rotary(CH - 1, True)

            def w_add(k, p, half):
                dve.wait_ge(w_mm, k + 1)
                V.scalar_tensor_tensor(row(k), ps[:, p, :], 1.0 / (WS * AS), row(k), ALU.mult, ALU.add).then_inc(w_h, 1)

            def w_moments(k, p, half):
                dve.wait_ge(w_h, k + 3)
                dve.sem_inc(passed, 1)
                order(V.bn_stats(bst12[:, p, :], row(k)))
                dve.sem_inc(passed, 1)
                order(V.bn_aggr(mv12[:, p, :], bst12[:, p, :]))
                ask(mv12[:, p, 1:2], 1.0, 1e-5, rt_in[:, p:p + 1], rf_ask)

            def f_norm(k, p, half):
                dve.wait_ge(rf_done, k + 1)
                V.tensor_scalar(xn[:, ds(k, 1), :].rearrange("p a b -> p (a b)"), row(k), mv12[:, p, 0:1],
                                rt_out[:, p:p + 1], ALU.subtract, ALU.mult).then_inc(w_n, 1)

            def largest(k, p, half):
                dve.wait_ge(w_n, k + 1)
                V.tensor_reduce(Gm["am"][:, ds(k, 1)], xn[:, ds(k, 1), :].rearrange("p a b -> p (a b)"), AX.X, ALU.max,
                                apply_absolute_value=True).then_inc(w_am, 1)

            def scales(am, root, sm):
                order(V.tensor_tensor(sm[0], am, root, ALU.mult))
                order(V.tensor_scalar(sm[0], sm[0], 1e-5, None, ALU.max))
                order(V.reciprocal(sm[1], sm[0]))
                order(V.scalar_tensor_tensor(sm[2], sm[1], 127.0, root, ALU.mult, ALU.mult))

            def ask_rows(k0, k1):
                dve.wait_ge(w_sq, k1 + 1)
                ask(Gm["ssq"][:, k0:k1], 1.0 / D, 1e-6, rq_in[:, k0:k1], rq_ask)

            def row_scales(n, k0, k1):
                dve.wait_ge(w_am, k1)
                dve.wait_ge(rq_done, n + 1)
                sm = [Gm["sm"][:, x, k0:k1] for x in range(3)]
                scales(Gm["am"][:, k0:k1], rq_out[:, k0:k1], sm)
                order(V.tensor_scalar(Gm["dq"][:, k0:k1], sm[0], 1.0 / 127.0, None, ALU.mult))

            pipeline(dve, NT, [(0, w_add), (2, f_norm), (1, w_moments), (3, largest)], order, 2,
                     after={NT: lambda: ask_rows(0, EARLY), NT + 1: lambda: row_scales(0, 0, EARLY)})
            ask_rows(EARLY, NT)

            def quantize(k, p, half):
                src = xn[:, ds(k, 1), :].rearrange("p a b -> p (a b)")
                V.tensor_scalar(src, src, Gm["sm"][:, 2, ds(k, 1)], MAGIC, ALU.mult, ALU.add).then_inc(w_r, 1)

            def integers(k, p, half):
                dve.wait_ge(w_r, k + 1)
                V.tensor_scalar(qi[:, ds(k, 1), :].rearrange("p a b -> p (a b)"), xn[:, ds(k, 1), :].rearrange("p a b -> p (a b)"), MAGIC, 127.0,
                                ALU.subtract, ALU.min).then_inc(w_q, 1)

            def dequantizers(k, p, half):
                order(V.tensor_copy(Gm["dqc"][:], Gm["dq"][:, ds(k, 1)]))
                V.tensor_scalar(Gm["dqe"][:, p, :], wdq[:, 0:2], Gm["dqc"][:, 0:1], None, ALU.mult).then_inc(x_dq, 1)
                dve.wait_ge(x_dq, k + 1)

            def product(f):
                def step(k, p, half):
                    dve.wait_ge(x_sg, 4 * k + f + 1)
                    V.scalar_tensor_tensor(ff[:, p, f * 512:(f + 1) * 512], ps[:, 2 * (f % 2) + 1, :],
                                           Gm["dqe"][:, p, 1:2], sgl[:, f % 2, :], ALU.mult, ALU.mult).then_inc(x_t, 1)
                return step

            def chunk_max(f):
                def step(k, p, half):
                    dve.wait_ge(x_t, ready(4 * k + f))
                    V.tensor_reduce(Gm["amf"][:, p, f:f + 1], ff[:, p, f * 512:(f + 1) * 512], AX.X, ALU.max,
                                    apply_absolute_value=True).then_inc(x_am, 1)
                return step

            def ask_root(k, p, half):
                dve.wait_ge(x_am, 4 * k + 4)
                order(V.tensor_reduce(Gm["amg"][:, p:p + 1], Gm["amf"][:, p, :], AX.X, ALU.max))
                dve.wait_ge(x_sq, 4 * k + 5)
                order(V.tensor_reduce(Gm["ssg"][:, p:p + 1], Gm["ssf"][:, p, :], AX.X, ALU.add))
                ask(Gm["ssg"][:, p:p + 1], 1.0 / FF, 1e-6, rq_in[:, p:p + 1], rg_ask)

            def rescale(k, p, half):
                dve.wait_ge(rg_done, k + 1)
                g = [Gm["smg"][:, x, p:p + 1] for x in range(3)]
                scales(Gm["amg"][:, p:p + 1], rq_out[:, p:p + 1], g)
                order(V.tensor_scalar(Gm["dqd"][:, p:p + 1], g[0], wdq[:, 2:3], 1.0 / 127.0, ALU.mult, ALU.mult))
                order(V.tensor_scalar(ff[:, p, :], ff[:, p, :], g[2], MAGIC, ALU.mult, ALU.add))

            def f_integers(k, p, half):
                dve.wait_ge(x_tr, 2 * k + 2)
                V.tensor_scalar(fi[:], ff[:, p, :], MAGIC, 127.0, ALU.subtract, ALU.min).then_inc(x_q, 1)

            def finish(k, p, half):
                dve.wait_ge(x_dn, ready(k))
                dve.wait_ge(out_st[p], 16 * (half + 1))
                V.scalar_tensor_tensor(og[:, p, :], ps[:, 6, :], Gm["dqd"][:, p:p + 1], row(k), ALU.mult,
                                       ALU.add).then_inc(x_og, 1)

            pipeline(dve, NT, [(0, quantize), (0, integers), (2, dequantizers), (2, product(0)), (2, product(1)),
                               (3, rescale), (3, f_integers), (2, product(2)), (2, chunk_max(0)), (2, chunk_max(1)),
                               (2, product(3)), (2, chunk_max(2)), (2, chunk_max(3)), (2, ask_root), (4, finish)],
                     order, 1 + 2 + 4 + 2, after={1: lambda: row_scales(1, EARLY, NT)})


def constants():
    pos = np.arange(AT) % SL
    seq = np.arange(AT) // SL
    same = seq[:, None] == seq[None, :]
    causal = same & (pos[:, None] <= pos[None, :])
    tri = causal.astype(np.float32)
    mask = np.where(causal, 0.0, NEG).astype(np.float32)
    inv = np.power(np.float32(10000.0), np.float32(-2.0) * np.arange(HD // 2, dtype=np.float32) / np.float32(HD))
    ang = np.arange(SL, dtype=np.float32)[:, None] * inv[None, :].astype(np.float32)
    cos = np.tile(np.cos(ang), (1, 2)).astype(np.float32)
    sin = np.tile(np.sin(ang), (1, 2)).astype(np.float32)
    sin[:, :HD // 2] *= -1.0
    lane = np.arange(P) % HD
    p = np.arange(CW) % SL
    return dict(ident=np.eye(P, dtype=np.float32), tri=tri, mask=mask, maskT=np.ascontiguousarray(mask.T),
                cos=np.ascontiguousarray(cos[p][:, lane].T), sin=np.ascontiguousarray(sin[p][:, lane].T))


def kernel(**inp):
    import concourse.bacc as bacc
    from concourse.bass_utils import run_bass_kernel_spmd

    f = {k: np.asarray(v) for k, v in inp.items()}

    def kmaj(w):
        return w.reshape(w.shape[0] // P, P, w.shape[1]).transpose(1, 0, 2)

    x = np.zeros((TP, DIN), np.float32)
    x[:T] = f["x"][:, :SL * 16].reshape(T, DIN)
    wt = kmaj(f["L0_tok_W"])
    wa = np.zeros((UNITS, P, KD, 512), np.float32)
    wb = np.zeros((UNITS, P, 1024), np.float32)
    q, k, v, c = (kmaj(f["L0_attn_W" + n]) for n in "qkvc")
    for n in range(HEADS):
        wa[n, :, :, 0:256] = q[:, :, 256 * n:256 * (n + 1)]
        wa[n, :, :, 256:384] = k[:, :, P * n:P * (n + 1)]
        wa[n, :, :, 384:512] = v[:, :, P * n:P * (n + 1)]
        wb[n] = c[:, 2 * n:2 * n + 2].reshape(P, 1024)
    for e in range(EXP + 1):
        g, u, d = ((f["L0_ffn_w_gate"][e], f["L0_ffn_w_up"][e], f["L0_ffn_w_down"][e]) if e < EXP else
                   (f["L0_ffn_sw_gate"], f["L0_ffn_sw_up"], f["L0_ffn_sw_down"]))
        wa[HEADS + e, :, :, 0:256] = kmaj(g.T)
        wa[HEADS + e, :, :, 256:512] = kmaj(u.T)
        wb[HEADS + e] = kmaj(d.T).reshape(P, 1024)
    wq1 = f["L1_attn_Wq"].reshape(D, G4, J4, HD).transpose(0, 2, 1, 3).reshape(D, D)
    wa[UNITS - 1] = kmaj(wq1)
    wb[UNITS - 1] = np.concatenate([kmaj(f["L1_attn_Wk"]), kmaj(f["L1_attn_Wv"])], axis=2).reshape(P, 1024)
    arrays = {
        "x": x.reshape(NT, P, DIN), "wt": wt.transpose(1, 0, 2).reshape(2, 4, P, D).transpose(0, 2, 1, 3).reshape(2, P, 2048),
        "g1": f["L0_tok_g1"].reshape(KI, P).T, "b1": f["L0_tok_b1"].reshape(KI, P).T, "tb": f["L0_tok_b"], "g2": f["L0_tok_g2"], "b2": f["L0_tok_b2"],
        "bcol": f["L0_attn_bc"].reshape(KD, P).T, "ebias": f["L0_ffn_expert_bias"],
        "gst": np.concatenate([kmaj(f["L0_attn_Wg"]), kmaj(f["L0_ffn_gate_w"].T)], axis=2),
        "wa": wa.reshape(UNITS, P, 2048), "wb": wb,
        "wo": kmaj(f["L1_attn_Wo"].reshape(G4, J4, HD, D).transpose(1, 0, 2, 3).reshape(D, D)).reshape(P, 2048),
        "ffq": np.stack([kmaj(f["L1_ffn_w_gate"].T).reshape(P, 8, 1024), kmaj(f["L1_ffn_w_up"].T).reshape(P, 8, 1024),
                         kmaj(f["L1_ffn_w_down"].T).reshape(P, 8, 1024)]).transpose(0, 2, 1, 3),
    }
    arrays.update(constants())
    nc = bacc.Bacc("TRN2", target_bir_lowering=False, num_devices=1)
    t = {}
    for name in list(arrays):
        a = arrays.pop(name)
        a = np.ascontiguousarray(a)
        arrays[f"in_{name}"] = a
        t[name] = nc.dram_tensor(f"in_{name}", a.shape, mybir.dt.from_np(a.dtype), kind="ExternalInput").ap()
    out = nc.dram_tensor("out", (T, D), F32, kind="ExternalOutput").ap()
    build(nc, t, out)
    r = run_bass_kernel_spmd(nc, [arrays], core_ids=[0])
    return np.asarray(r.results[0]["out"]).reshape(SEQS, SL, D)
```
